# Optimizing a Trainium2 kernel written in Bass

```python
import numpy as np
import jax
import jax.numpy as jnp

def _softmax(x, axis=-1):
    return jax.nn.softmax(x, axis=axis)

def _gelu(x):
    return jax.nn.gelu(x, approximate=True)

def _silu(x):
    return jax.nn.silu(x)

def _sigmoid(x):
    return jax.nn.sigmoid(x)

def _layernorm(x, axis=-1, eps=1e-05):
    m = jnp.mean(x, axis=axis, keepdims=True)
    v = jnp.var(x, axis=axis, keepdims=True)
    return (x - m) / jnp.sqrt(v + eps)

def _scatter_add(tgt, idx, src, axis=0):
    return tgt.at[idx].add(src)

def _segment_sum(src, seg, n):
    return jax.ops.segment_sum(src, seg, n)
kernel_name = 'mk_lm_tower_d2_tok_ids256_r4_bfcc91'

def setup_inputs(seed: int=0):
    np.random.seed(seed)
    _w = jnp.asarray

    def _rec_inputs():
        import jax
        import jax.numpy as jnp
        _rk = jax.random.key(seed)
        x = jax.random.randint(jax.random.fold_in(_rk, 1), (64, 256), 0, 64, jnp.int32)
        return x
    x = _rec_inputs()

    def _L0_tok_setup():
        import jax, jax.numpy as jnp
        import numpy as np
        V, C, D, N_ROUNDS, WIN = (64, 8, 128, 3, 4)
        B, T = (16, 2048)
        EPS = 1e-05

        def _ln(x, g, b):
            mu = jnp.mean(x, axis=-1, keepdims=True)
            var = jnp.mean((x - mu) ** 2, axis=-1, keepdims=True)
            return (x - mu) * jax.lax.rsqrt(var + EPS) * g + b

        def _mlp2(x, w1, b1, w2, b2):
            return jax.nn.gelu(x @ w1 + b1, approximate=False) @ w2 + b2
        key = jax.random.key(seed)
        ks = iter(jax.random.split(key, 32))
        nrm = lambda shp, s: jax.random.normal(next(ks), shp, jnp.float32) * s
        inp = {'x': jax.random.randint(next(ks), (B, T), 0, V, dtype=jnp.int32), 'emb': nrm((V, D), 0.02), 'pos': nrm((C, D), 0.02), 'lw1': nrm((D, 2 * D), 0.05), 'lb1': jnp.zeros((2 * D,)), 'lw2': nrm((2 * D, D), 0.05), 'lb2': jnp.zeros((D,)), 'lln_g': jnp.ones((D,)), 'lln_b': jnp.zeros((D,)), 'pool_w': nrm((D, D), 0.05), 'pool_b': jnp.zeros((D,)), 'msg_w1': nrm((2 * D, D), 0.05), 'msg_b1': jnp.zeros((D,)), 'msg_w2': nrm((D, D), 0.05), 'msg_b2': jnp.zeros((D,)), 'upd_w1': nrm((2 * D, D), 0.05), 'upd_b1': jnp.zeros((D,)), 'upd_w2': nrm((D, D), 0.05), 'upd_b2': jnp.zeros((D,)), 'mln_g': jnp.ones((D,)), 'mln_b': jnp.zeros((D,)), 'bc_w': nrm((D, D), 0.05), 'bc_b': jnp.zeros((D,)), 'fln_g': jnp.ones((D,)), 'fln_b': jnp.zeros((D,)), 'head_w': nrm((D, V), 0.05)}
        return inp
    _L0_tok_all = _L0_tok_setup()
    _L0_tok_in = {k: v for k, v in _L0_tok_all.items() if k in ('emb', 'pos', 'lw1', 'lb1', 'lw2', 'lb2', 'lln_g', 'lln_b', 'pool_w', 'pool_b', 'msg_w1', 'msg_b1', 'msg_w2', 'msg_b2', 'upd_w1', 'upd_b1', 'upd_w2', 'upd_b2', 'mln_g', 'mln_b', 'bc_w', 'bc_b', 'fln_g', 'fln_b', 'head_w')}
    del _L0_tok_all

    def _L0_attn_setup():
        import jax, jax.numpy as jnp
        import numpy as np
        DIM = 64
        WS = 64
        H = 8
        HD = DIM // H
        SCALE = HD ** (-0.5)
        key = jax.random.key(seed)
        k1, k2, k3, k4 = jax.random.split(key, 4)
        B, L = (8, 4096)
        x = jax.random.normal(k1, (B, L, DIM), dtype=jnp.float32)
        w_qkv = jax.random.normal(k2, (3 * DIM, DIM), dtype=jnp.float32) * DIM ** (-0.5)
        w_proj = jax.random.normal(k3, (DIM, DIM), dtype=jnp.float32) * DIM ** (-0.5)
        b_proj = jnp.zeros((DIM,), dtype=jnp.float32)
        rel_bias = jax.random.normal(k4, (2 * WS - 1,), dtype=jnp.float32) * 0.02
        return {'x': x, 'w_qkv': w_qkv, 'w_proj': w_proj, 'b_proj': b_proj, 'rel_bias': rel_bias}
    _L0_attn_all = _L0_attn_setup()
    _L0_attn_in = {k: v for k, v in _L0_attn_all.items() if k in ('w_qkv', 'w_proj', 'b_proj', 'rel_bias')}
    del _L0_attn_all

    def _L0_ffn_setup():
        import jax, jax.numpy as jnp
        import numpy as np
        BN_EPS = 0.001

        def _bn(h, g, b, m, v):
            return g * (h - m) * jax.lax.rsqrt(v + BN_EPS) + b
        key = jax.random.key(seed)
        ks = jax.random.split(key, 8)
        B, F, Df = (64, 64, 64)
        E, H, D = (8, 64, 64)
        s1 = 1.0 / np.sqrt(Df)
        s2 = 1.0 / np.sqrt(H)
        return {'x': jax.random.normal(ks[0], (B, F, Df), jnp.float32), 'Wr': jax.random.normal(ks[1], (Df, E), jnp.float32) * s1, 'br': jnp.zeros((E,), jnp.float32), 'W1': jax.random.normal(ks[2], (E, Df, H), jnp.float32) * s1, 'b1': jnp.zeros((E, H), jnp.float32), 'g1': jnp.ones((E, H), jnp.float32), 'be1': jnp.zeros((E, H), jnp.float32), 'm1': jnp.zeros((E, H), jnp.float32), 'v1': jnp.ones((E, H), jnp.float32), 'W2': jax.random.normal(ks[3], (E, H, H), jnp.float32) * s2, 'b2': jnp.zeros((E, H), jnp.float32), 'g2': jnp.ones((E, H), jnp.float32), 'be2': jnp.zeros((E, H), jnp.float32), 'm2': jnp.zeros((E, H), jnp.float32), 'v2': jnp.ones((E, H), jnp.float32), 'Wo': jax.random.normal(ks[4], (E, H, D), jnp.float32) * s2, 'bo': jnp.zeros((E, D), jnp.float32)}
    _L0_ffn_all = _L0_ffn_setup()
    _L0_ffn_in = {k: v for k, v in _L0_ffn_all.items() if k in ('Wr', 'br', 'W1', 'b1', 'g1', 'be1', 'm1', 'v1', 'W2', 'b2', 'g2', 'be2', 'm2', 'v2', 'Wo', 'bo')}
    del _L0_ffn_all

    def _L1_attn_setup():
        import jax, jax.numpy as jnp
        import numpy as np
        B, N, C, H = (1024, 64, 64, 8)
        key = jax.random.key(seed)
        ks = jax.random.split(key, 6)
        return {'x': jax.random.normal(ks[0], (B, N, C), dtype=jnp.float32), 'qkv_w': jax.random.normal(ks[1], (C, 3 * C), dtype=jnp.float32) * 0.02, 'qkv_b': jax.random.normal(ks[2], (3 * C,), dtype=jnp.float32) * 0.02, 'proj_w': jax.random.normal(ks[3], (C, C), dtype=jnp.float32) * 0.02, 'proj_b': jax.random.normal(ks[4], (C,), dtype=jnp.float32) * 0.02, 'rpb_table': jax.random.normal(ks[5], (2 * N - 1, H), dtype=jnp.float32) * 0.02}
    _L1_attn_all = _L1_attn_setup()
    _L1_attn_in = {k: v for k, v in _L1_attn_all.items() if k in ('qkv_w', 'qkv_b', 'proj_w', 'proj_b', 'rpb_table')}
    del _L1_attn_all

    def _L1_ffn_setup():
        import jax, jax.numpy as jnp
        import numpy as np
        E = 8
        K = 2
        D = 64
        H = 128
        DOUT = 64
        EPS = 1e-05
        key = jax.random.key(seed)
        ks = jax.random.split(key, 9)
        s = 0.02
        return {'x': jax.random.normal(ks[0], (4, 2048, D), jnp.float32), 'gamma': 1.0 + 0.05 * jax.random.normal(ks[1], (D,), jnp.float32), 'beta': 0.05 * jax.random.normal(ks[2], (D,), jnp.float32), 'Wr': 0.01 * jax.random.normal(ks[3], (D, E), jnp.float32), 'br': jnp.zeros((E,), jnp.float32), 'W1': s * jax.random.normal(ks[4], (E, D, H), jnp.float32), 'b1': s * jax.random.normal(ks[5], (E, H), jnp.float32), 'W2': s * jax.random.normal(ks[6], (E, H, DOUT), jnp.float32), 'b2': s * jax.random.normal(ks[7], (E, DOUT), jnp.float32)}
    _L1_ffn_all = _L1_ffn_setup()
    _L1_ffn_in = {k: v for k, v in _L1_ffn_all.items() if k in ('gamma', 'beta', 'Wr', 'br', 'W1', 'b1', 'W2', 'b2')}
    del _L1_ffn_all
    return {'x': x, 'L0_tok_emb': _L0_tok_in['emb'], 'L0_tok_pos': _L0_tok_in['pos'], 'L0_tok_lw1': _L0_tok_in['lw1'], 'L0_tok_lb1': _L0_tok_in['lb1'], 'L0_tok_lw2': _L0_tok_in['lw2'], 'L0_tok_lb2': _L0_tok_in['lb2'], 'L0_tok_lln_g': _L0_tok_in['lln_g'], 'L0_tok_lln_b': _L0_tok_in['lln_b'], 'L0_tok_pool_w': _L0_tok_in['pool_w'], 'L0_tok_pool_b': _L0_tok_in['pool_b'], 'L0_tok_msg_w1': _L0_tok_in['msg_w1'], 'L0_tok_msg_b1': _L0_tok_in['msg_b1'], 'L0_tok_msg_w2': _L0_tok_in['msg_w2'], 'L0_tok_msg_b2': _L0_tok_in['msg_b2'], 'L0_tok_upd_w1': _L0_tok_in['upd_w1'], 'L0_tok_upd_b1': _L0_tok_in['upd_b1'], 'L0_tok_upd_w2': _L0_tok_in['upd_w2'], 'L0_tok_upd_b2': _L0_tok_in['upd_b2'], 'L0_tok_mln_g': _L0_tok_in['mln_g'], 'L0_tok_mln_b': _L0_tok_in['mln_b'], 'L0_tok_bc_w': _L0_tok_in['bc_w'], 'L0_tok_bc_b': _L0_tok_in['bc_b'], 'L0_tok_fln_g': _L0_tok_in['fln_g'], 'L0_tok_fln_b': _L0_tok_in['fln_b'], 'L0_tok_head_w': _L0_tok_in['head_w'], 'L0_attn_w_qkv': _L0_attn_in['w_qkv'], 'L0_attn_w_proj': _L0_attn_in['w_proj'], 'L0_attn_b_proj': _L0_attn_in['b_proj'], 'L0_attn_rel_bias': _L0_attn_in['rel_bias'], 'L0_ffn_Wr': _L0_ffn_in['Wr'], 'L0_ffn_br': _L0_ffn_in['br'], 'L0_ffn_W1': _L0_ffn_in['W1'], 'L0_ffn_b1': _L0_ffn_in['b1'], 'L0_ffn_g1': _L0_ffn_in['g1'], 'L0_ffn_be1': _L0_ffn_in['be1'], 'L0_ffn_m1': _L0_ffn_in['m1'], 'L0_ffn_v1': _L0_ffn_in['v1'], 'L0_ffn_W2': _L0_ffn_in['W2'], 'L0_ffn_b2': _L0_ffn_in['b2'], 'L0_ffn_g2': _L0_ffn_in['g2'], 'L0_ffn_be2': _L0_ffn_in['be2'], 'L0_ffn_m2': _L0_ffn_in['m2'], 'L0_ffn_v2': _L0_ffn_in['v2'], 'L0_ffn_Wo': _L0_ffn_in['Wo'], 'L0_ffn_bo': _L0_ffn_in['bo'], 'L1_attn_qkv_w': _L1_attn_in['qkv_w'], 'L1_attn_qkv_b': _L1_attn_in['qkv_b'], 'L1_attn_proj_w': _L1_attn_in['proj_w'], 'L1_attn_proj_b': _L1_attn_in['proj_b'], 'L1_attn_rpb_table': _L1_attn_in['rpb_table'], 'L1_ffn_gamma': _L1_ffn_in['gamma'], 'L1_ffn_beta': _L1_ffn_in['beta'], 'L1_ffn_Wr': _L1_ffn_in['Wr'], 'L1_ffn_br': _L1_ffn_in['br'], 'L1_ffn_W1': _L1_ffn_in['W1'], 'L1_ffn_b1': _L1_ffn_in['b1'], 'L1_ffn_W2': _L1_ffn_in['W2'], 'L1_ffn_b2': _L1_ffn_in['b2']}

def reference(x, L0_tok_emb, L0_tok_pos, L0_tok_lw1, L0_tok_lb1, L0_tok_lw2, L0_tok_lb2, L0_tok_lln_g, L0_tok_lln_b, L0_tok_pool_w, L0_tok_pool_b, L0_tok_msg_w1, L0_tok_msg_b1, L0_tok_msg_w2, L0_tok_msg_b2, L0_tok_upd_w1, L0_tok_upd_b1, L0_tok_upd_w2, L0_tok_upd_b2, L0_tok_mln_g, L0_tok_mln_b, L0_tok_bc_w, L0_tok_bc_b, L0_tok_fln_g, L0_tok_fln_b, L0_tok_head_w, L0_attn_w_qkv, L0_attn_w_proj, L0_attn_b_proj, L0_attn_rel_bias, L0_ffn_Wr, L0_ffn_br, L0_ffn_W1, L0_ffn_b1, L0_ffn_g1, L0_ffn_be1, L0_ffn_m1, L0_ffn_v1, L0_ffn_W2, L0_ffn_b2, L0_ffn_g2, L0_ffn_be2, L0_ffn_m2, L0_ffn_v2, L0_ffn_Wo, L0_ffn_bo, L1_attn_qkv_w, L1_attn_qkv_b, L1_attn_proj_w, L1_attn_proj_b, L1_attn_rpb_table, L1_ffn_gamma, L1_ffn_beta, L1_ffn_Wr, L1_ffn_br, L1_ffn_W1, L1_ffn_b1, L1_ffn_W2, L1_ffn_b2):
    import jax
    import jax.numpy as jnp

    def _L0_tok_ref(x, emb, pos, lw1, lb1, lw2, lb2, lln_g, lln_b, pool_w, pool_b, msg_w1, msg_b1, msg_w2, msg_b2, upd_w1, upd_b1, upd_w2, upd_b2, mln_g, mln_b, bc_w, bc_b, fln_g, fln_b, head_w):
        import jax, jax.numpy as jnp
        import numpy as np
        V, C, D, N_ROUNDS, WIN = (64, 8, 128, 3, 4)
        B, T = (16, 2048)
        EPS = 1e-05

        def _ln(x, g, b):
            mu = jnp.mean(x, axis=-1, keepdims=True)
            var = jnp.mean((x - mu) ** 2, axis=-1, keepdims=True)
            return (x - mu) * jax.lax.rsqrt(var + EPS) * g + b

        def _mlp2(x, w1, b1, w2, b2):
            return jax.nn.gelu(x @ w1 + b1, approximate=False) @ w2 + b2
        Bv, Tv = x.shape
        pad = -Tv % C
        padded_T = Tv + pad
        n_chunks = padded_T // C
        x_pad = jnp.pad(x, ((0, 0), (0, pad)))
        chunks = x_pad.reshape(Bv, n_chunks, C)
        h = emb[chunks] + pos[None, None, :, :]
        local = h + _mlp2(_ln(h, lln_g, lln_b), lw1, lb1, lw2, lb2)
        summ = local.mean(axis=2) @ pool_w + pool_b
        i = jnp.arange(n_chunks)[:, None]
        d = jnp.arange(WIN + 1)[None, :]
        idx = jnp.clip(i - d, 0, None)
        valid = (i - d >= 0).astype(summ.dtype)
        count = valid.sum(axis=1)
        hmsg = summ
        for _ in range(N_ROUNDS):
            nbr = hmsg[:, idx]
            self_e = jnp.broadcast_to(hmsg[:, :, None, :], nbr.shape)
            msgs = _mlp2(jnp.concatenate([self_e, nbr], -1), msg_w1, msg_b1, msg_w2, msg_b2)
            agg = (msgs * valid[None, :, :, None]).sum(axis=2) / count[None, :, None]
            upd = _mlp2(jnp.concatenate([hmsg, agg], -1), upd_w1, upd_b1, upd_w2, upd_b2)
            hmsg = _ln(hmsg + upd, mln_g, mln_b)
        bc = hmsg @ bc_w + bc_b
        combined = (local + bc[:, :, None, :]).reshape(Bv, padded_T, D)[:, :Tv, :]
        logits = _ln(combined, fln_g, fln_b) @ head_w
        return logits

    def _L0_attn_ref(x, w_qkv, w_proj, b_proj, rel_bias):
        import jax, jax.numpy as jnp
        import numpy as np
        DIM = 64
        WS = 64
        H = 8
        HD = DIM // H
        SCALE = HD ** (-0.5)
        B, L, C = x.shape
        pad_len = (WS - L % WS) % WS
        if pad_len > 0:
            x = jnp.pad(x, ((0, 0), (0, pad_len), (0, 0)))
        padded_L = x.shape[1]
        nw = padded_L // WS
        xw = x.reshape(B, nw, WS, C)
        qkv = jnp.einsum('bnwc,oc->bnwo', xw, w_qkv)
        qkv = qkv.reshape(B, nw, WS, 3, H, HD)
        q = jnp.transpose(qkv[..., 0, :, :], (0, 1, 3, 2, 4))
        k = jnp.transpose(qkv[..., 1, :, :], (0, 1, 3, 2, 4))
        v = jnp.transpose(qkv[..., 2, :, :], (0, 1, 3, 2, 4))
        attn = jnp.einsum('bnhqd,bnhkd->bnhqk', q, k) * SCALE
        pos = jnp.arange(WS)
        rel_idx = pos[None, :] - pos[:, None] + WS - 1
        attn = attn + rel_bias[rel_idx]
        attn = jax.nn.softmax(attn, axis=-1)
        out = jnp.einsum('bnhqk,bnhkd->bnhqd', attn, v)
        out = jnp.transpose(out, (0, 1, 3, 2, 4)).reshape(B, nw, WS, C)
        out = jnp.einsum('bnwc,oc->bnwo', out, w_proj) + b_proj
        out = out.reshape(B, padded_L, C)
        if pad_len > 0:
            out = out[:, :L, :]
        return out

    def _L0_ffn_ref(x, Wr, br, W1, b1, g1, be1, m1, v1, W2, b2, g2, be2, m2, v2, Wo, bo):
        import jax, jax.numpy as jnp
        import numpy as np
        BN_EPS = 0.001

        def _bn(h, g, b, m, v):
            return g * (h - m) * jax.lax.rsqrt(v + BN_EPS) + b
        feat = jnp.mean(x, axis=0)
        w = jax.nn.softmax(feat @ Wr + br, axis=-1)
        h = jnp.einsum('bfd,edh->bfeh', x, W1) + b1
        h = jax.nn.relu(_bn(h, g1, be1, m1, v1))
        h = jnp.einsum('bfeh,ehk->bfek', h, W2) + b2
        h = jax.nn.relu(_bn(h, g2, be2, m2, v2))
        y = jnp.einsum('bfeh,ehd->bfed', h, Wo) + bo
        return jnp.einsum('bfed,fe->bfd', y, w)

    def _L1_attn_ref(x, qkv_w, qkv_b, proj_w, proj_b, rpb_table):
        import jax, jax.numpy as jnp
        import numpy as np
        B, N, C, H = (1024, 64, 64, 8)
        Bw, Nw, Cd = x.shape
        nh = rpb_table.shape[1]
        dh = Cd // nh
        scale = dh ** (-0.5)
        qkv = (x @ qkv_w + qkv_b).reshape(Bw, Nw, 3, nh, dh)
        q, k, v = (qkv[:, :, 0], qkv[:, :, 1], qkv[:, :, 2])
        attn = jnp.einsum('bnhd,bmhd->bhnm', q * scale, k)
        coords = jnp.arange(Nw)
        rel_idx = coords[:, None] - coords[None, :] + (Nw - 1)
        bias = jnp.transpose(rpb_table[rel_idx], (2, 0, 1))
        attn = jax.nn.softmax(attn + bias[None], axis=-1)
        out = jnp.einsum('bhnm,bmhd->bnhd', attn, v).reshape(Bw, Nw, Cd)
        return out @ proj_w + proj_b

    def _L1_ffn_ref(x, gamma, beta, Wr, br, W1, b1, W2, b2):
        import jax, jax.numpy as jnp
        import numpy as np
        E = 8
        K = 2
        D = 64
        H = 128
        DOUT = 64
        EPS = 1e-05
        mu = jnp.mean(x, axis=-1, keepdims=True)
        var = jnp.mean(jnp.square(x - mu), axis=-1, keepdims=True)
        xn = (x - mu) * jax.lax.rsqrt(var + EPS) * gamma + beta
        logits = jnp.einsum('bsd,de->bse', xn, Wr) + br
        top_vals, top_idx = jax.lax.top_k(logits, K)
        w = jax.nn.softmax(top_vals, axis=-1)
        w_full = jnp.einsum('bsk,bske->bse', w, jax.nn.one_hot(top_idx, E, dtype=w.dtype))
        y = jnp.zeros(x.shape[:-1] + (DOUT,), x.dtype)
        for e in range(E):
            h = jax.nn.gelu(jnp.einsum('bsd,dh->bsh', xn, W1[e]) + b1[e], approximate=False)
            y_e = jnp.einsum('bsh,hd->bsd', h, W2[e]) + b2[e]
            y = y + y_e * w_full[..., e, None]
        return y
    h = _L0_tok_ref(x, L0_tok_emb, L0_tok_pos, L0_tok_lw1, L0_tok_lb1, L0_tok_lw2, L0_tok_lb2, L0_tok_lln_g, L0_tok_lln_b, L0_tok_pool_w, L0_tok_pool_b, L0_tok_msg_w1, L0_tok_msg_b1, L0_tok_msg_w2, L0_tok_msg_b2, L0_tok_upd_w1, L0_tok_upd_b1, L0_tok_upd_w2, L0_tok_upd_b2, L0_tok_mln_g, L0_tok_mln_b, L0_tok_bc_w, L0_tok_bc_b, L0_tok_fln_g, L0_tok_fln_b, L0_tok_head_w)
    h = h + _L0_attn_ref(_layernorm(h, axis=-1), L0_attn_w_qkv, L0_attn_w_proj, L0_attn_b_proj, L0_attn_rel_bias)
    h = h + _L0_ffn_ref(_layernorm(h, axis=-1), L0_ffn_Wr, L0_ffn_br, L0_ffn_W1, L0_ffn_b1, L0_ffn_g1, L0_ffn_be1, L0_ffn_m1, L0_ffn_v1, L0_ffn_W2, L0_ffn_b2, L0_ffn_g2, L0_ffn_be2, L0_ffn_m2, L0_ffn_v2, L0_ffn_Wo, L0_ffn_bo)
    h = h + _L1_attn_ref(_layernorm(h, axis=-1), L1_attn_qkv_w, L1_attn_qkv_b, L1_attn_proj_w, L1_attn_proj_b, L1_attn_rpb_table)
    h = h + _L1_ffn_ref(_layernorm(h, axis=-1), L1_ffn_gamma, L1_ffn_beta, L1_ffn_Wr, L1_ffn_br, L1_ffn_W1, L1_ffn_b1, L1_ffn_W2, L1_ffn_b2)
    return h

_drawn_inputs = setup_inputs


def setup_inputs(seed=0):
    import zlib

    import numpy as np

    out = dict(_drawn_inputs(seed))
    spreads = {'L0_tok_lb1': (0.0, 0.1),
     'L0_tok_lb2': (0.0, 0.1),
     'L0_tok_lln_g': (1.0, 0.2),
     'L0_tok_lln_b': (0.0, 0.1),
     'L0_tok_pool_b': (0.0, 0.1),
     'L0_tok_msg_b1': (0.0, 0.424),
     'L0_tok_msg_b2': (0.0, 0.1),
     'L0_tok_upd_b1': (0.0, 0.1),
     'L0_tok_upd_b2': (0.0, 0.1),
     'L0_tok_mln_g': (1.0, 0.2),
     'L0_tok_mln_b': (0.0, 0.1),
     'L0_tok_bc_b': (0.0, 0.1),
     'L0_tok_fln_g': (1.0, 0.2),
     'L0_tok_fln_b': (0.0, 0.1),
     'L0_attn_b_proj': (0.0, 0.1),
     'L0_ffn_br': (0.0, 0.353),
     'L0_ffn_b1': (0.0, 0.312),
     'L0_ffn_g1': (1.0, 0.2),
     'L0_ffn_be1': (0.0, 0.331),
     'L0_ffn_m1': (0.0, 0.504),
     'L0_ffn_v1': (1.0, 0.6),
     'L0_ffn_b2': (0.0, 0.1),
     'L0_ffn_g2': (1.0, 0.2),
     'L0_ffn_be2': (0.0, 0.361),
     'L0_ffn_m2': (0.0, 0.1),
     'L0_ffn_v2': (1.0, 0.6),
     'L0_ffn_bo': (0.0, 0.1),
     'L1_ffn_br': (0.0, 0.503)}
    factors = {'L0_attn_rel_bias': 26.405,
     'L1_attn_qkv_w': 2.732,
     'L1_attn_qkv_b': 8.0,
     'L1_attn_proj_b': 3.67,
     'L1_attn_rpb_table': 64.0,
     'L1_ffn_gamma': 8.0,
     'L1_ffn_beta': 8.0,
     'L1_ffn_Wr': 7.076,
     'L1_ffn_W1': 4.734,
     'L1_ffn_b1': 8.0,
     'L1_ffn_W2': 5.806,
     'L1_ffn_b2': 14.616}
    for name, (base, spread) in spreads.items():
        noise = np.random.default_rng([zlib.crc32(name.encode()), seed]).standard_normal(out[name].shape)
        drawn = base * np.exp(spread * noise) if base else spread * noise
        out[name] = jnp.asarray(drawn.astype(out[name].dtype))
    for name, factor in factors.items():
        out[name] = (out[name] * factor).astype(out[name].dtype)
    return out
```

```python
import concourse.bass as bass
from concourse import mybir
from contextlib import ExitStack

F32 = mybir.dt.float32
I32 = mybir.dt.int32
ALU = mybir.AluOpType
ACT = mybir.ActivationFunctionType
AX = mybir.AxisListType

P = 128
V = 64
C = 8
D = 128
NTOK = 16384
SEQ, L = 64, 256
NCH = NTOK // C
CPS = L // C
WIN = 4
NG = NCH // P
KJ = C // 2
EPS = 1e-5


class Signals:

    def __init__(self, nc, prefix):
        self.nc, self.prefix, self.made = nc, prefix, {}

    def __call__(self, name):
        if name not in self.made:
            self.made[name] = self.nc.alloc_semaphore(self.prefix + name)
        return self.made[name]

    def close(self):
        self.nc.clear_and_free_semaphores(list(self.made.values()))
        self.nc.all_engine_barrier()


class Chain:

    def __init__(self, eng, sem, start=0):
        self.eng, self.sem, self.start, self.n = eng, sem, start, 0

    def __call__(self, ins):
        self.n += 1
        ins.then_inc(self.sem, 1)
        self.eng.wait_ge(self.sem, self.start + self.n)


def wait_alone(eng, sem, value, passed):
    eng.wait_ge(sem, value)
    eng.sem_inc(passed, 1)


def bcast(ap, shape):
    return ap.broadcast_to(shape)


def vector_rows(a):
    rows = []

    def whole(name, n=1):
        for r in range(n):
            rows.append((name, r, [(slice(0, P), a[name].rearrange("(r p) -> r p", p=P)[r])]))

    for name, n in (("L0_tok_lln_g", 1), ("L0_tok_lln_b", 1), ("L0_tok_lb1", 2), ("L0_tok_lb2", 1),
                    ("L0_tok_pool_b", 1), ("L0_tok_msg_b1", 1), ("L0_tok_msg_b2", 1), ("L0_tok_upd_b1", 1),
                    ("L0_tok_upd_b2", 1), ("L0_tok_mln_g", 1), ("L0_tok_mln_b", 1), ("L0_tok_bc_b", 1),
                    ("L0_tok_fln_g", 1), ("L0_tok_fln_b", 1)):
        whole(name, n)
    return rows


def chunk_tower(nc, a, h_out, K):
    rows = vector_rows(a)
    col = {(name, r): i for i, (name, r, _) in enumerate(rows)}
    NR = len(rows)
    with ExitStack() as ctx:
        def sb(name, shape, dt=F32):
            return ctx.enter_context(nc.sbuf_tensor(name, shape, dt))

        sem = Signals(nc, "tk_")
        ctx.callback(sem.close)

        ident, onesD = K.ident, K.onesD
        vrow = sb("vrow", [NR, P])
        vcol = sb("vcol", [P, NR])
        emb2 = sb("emb2", [P, D])
        posr = sb("posr", [P, KJ, D])
        lw1 = sb("lw1", [P, 2 * D])
        lw2 = sb("lw2", [P, 2, D])
        poolw = sb("poolw", [P, D])
        mw1 = sb("mw1", [P, 2, D])
        mw2 = sb("mw2", [P, D])
        uw1 = sb("uw1", [P, 2, D])
        uw2 = sb("uw2", [P, D])
        bcw = sb("bcw", [P, D])
        head = sb("head", [P, V])
        xi = sb("xi", [P, NG, C], I32)
        xf = sb("xf", [P, NG, C])
        xT = sb("xT", [P, P])
        vp = sb("vp", [P, 1])
        viota = sb("viota", [P, C, V])
        icnt = sb("icnt", [P, CPS])
        epost = sb("epost", [P, KJ, D])
        exc = sb("exc", [P, KJ, D])
        est = sb("est", [P, 3, KJ])
        exT = sb("exT", [P, KJ * P])
        g1 = sb("g1", [P, 2, KJ * P])
        TT = sb("TT", [P, KJ * P])
        TTc = sb("TTc", [P, KJ * P])
        Tp = sb("Tp", [P, KJ, D])
        Tl = sb("Tl", [P, KJ, 2, V])
        vTs = sb("vTs", [P, KJ, C])
        gh = sb("gh", [P, V])
        wl = sb("wl", [P, V])
        frow = sb("frow", [P, V])
        OH = sb("OH", [P, KJ, NCH])
        mw1t = sb("mw1t", [P, P])
        mw2T = sb("mw2T", [P, D])
        w21 = sb("w21", [P, D])
        bu1 = sb("bu1", [P, 1])
        hm = sb("hm", [P, NCH])
        pb = [ctx.enter_context(nc.psum_tensor(f"tkps{b}", [P, 512], F32)) for b in range(8)]

        def vc(name, r=0):
            c = col[(name, r)]
            return vcol[:, c:c + 1]

        NLOAD = 0
        with nc.Block() as block:
            @block.sync
            def _(sp):
                ld = sem("loaded")
                sp.wait_ge(sem("vrow0"), 1)
                n = 0

                def load(dst, src):
                    nonlocal n
                    sp.dma_start(dst, src).then_inc(ld, 16)
                    n += 1
                for j in range(2):
                    load(emb2[j * V:(j + 1) * V, :], a["L0_tok_emb"])
                    load(posr[j * V:(j + 1) * V, :, :],
                         a["L0_tok_pos"].rearrange("(k j) d -> j k d", j=2)[j].partition_broadcast(V))
                for i, (name, r, parts) in enumerate(rows):
                    for s, src in parts:
                        load(vrow[i:i + 1, s], src.unsqueeze(0))
                load(lw1[:, :], a["L0_tok_lw1"])
                load(lw2[:, :, :], a["L0_tok_lw2"].rearrange("(k p) n -> p k n", p=P))
                load(poolw[:, :], a["L0_tok_pool_w"])
                load(mw1[:, :, :], a["L0_tok_msg_w1"].rearrange("(k p) n -> p k n", p=P))
                load(mw2[:, :], a["L0_tok_msg_w2"])
                load(uw1[:, :, :], a["L0_tok_upd_w1"].rearrange("(k p) n -> p k n", p=P))
                load(uw2[:, :], a["L0_tok_upd_w2"])
                load(bcw[:, :], a["L0_tok_bc_w"])
                load(head[:, :], a["L0_tok_head_w"])
                load(xi[:, :, :], a["x"].rearrange("s l -> (s l)").rearrange("(g n c) -> n g c", n=P, c=C))
                assert n == 5 + NR + 9, n
            NLOAD = 16 * (5 + NR + 9)

            @block.gpsimd
            def _(pool):
                pool.iota(viota[:, :, :], pattern=[[0, C], [1, V]], base=0, channel_multiplier=0,
                          allow_small_or_imprecise_dtypes=True).then_inc(sem("iota"), 1)
                for j in range(2):
                    pool.wait_ge(sem("iota"), j + 1)
                    pool.iota(vp[j * V:(j + 1) * V, :], pattern=[[0, 1]], base=0, channel_multiplier=1,
                              allow_small_or_imprecise_dtypes=True).then_inc(sem("iota"), 1)
                pool.wait_ge(sem("iota"), 3)
                pool.wait_ge(sem("evar"), 1)
                nc.gpsimd.tensor_tensor(est[:, 2, :], est[:, 1, :], K.mhalf[:, 0:1].broadcast_to([P, KJ]), ALU.pow) \
                    .then_inc(sem("erstd"), 1)

            @block.vector
            def _(dve):
                step = Chain(dve, sem("dve"))
                step(nc.vector.memset(vrow[:, :], 0.0))
                dve.sem_inc(sem("vrow0"), 1)
                for i in range(CPS):
                    nc.vector.memset(icnt[:, i:i + 1] if i < WIN else icnt[:, i:], 1.0 / min(i + 1, WIN + 1)) \
                        .then_inc(sem("icnt"), 1)
                    if i == WIN:
                        break
                step(nc.vector.memset(Tl[:, :, :, :], 0.0))
                step(nc.vector.memset(vTs[:, :, :], 0.0))
                dve.wait_ge(sem("vcolp"), 1)
                step(nc.vector.tensor_copy(vcol[:, :], pb[0][:, 0:NR]))
                dve.sem_inc(sem("vcol"), 1)
                step(nc.vector.tensor_tensor(epost[:, :, :], posr[:, :, :],
                                             emb2[:, :].unsqueeze(1).broadcast_to([P, KJ, D]), ALU.add))
                dve.sem_inc(sem("epos"), 1)
                step(nc.vector.tensor_reduce(est[:, 0, :], epost[:, :, :], AX.X, ALU.add))
                step(nc.vector.tensor_scalar(est[:, 1, :], est[:, 0, :], 1.0 / D, None, ALU.mult))
                step(nc.vector.tensor_tensor(exc[:, :, :], epost[:, :, :],
                                             est[:, 1, :].unsqueeze(2).broadcast_to([P, KJ, D]), ALU.subtract))
                step(nc.vector.tensor_tensor(g1[:, 0, :].rearrange("p (k d) -> p k d", k=KJ), exc[:, :, :],
                                             exc[:, :, :], ALU.mult))
                step(nc.vector.tensor_reduce(est[:, 0, :], g1[:, 0, :].rearrange("p (k d) -> p k d", k=KJ),
                                             AX.X, ALU.add))
                step(nc.vector.tensor_scalar(est[:, 1, :], est[:, 0, :], 1.0 / D, EPS, ALU.mult, ALU.add))
                dve.sem_inc(sem("evar"), 1)
                dve.wait_ge(sem("erstd"), 1)
                step(nc.vector.tensor_tensor(exc[:, :, :], exc[:, :, :],
                                             est[:, 2, :].unsqueeze(2).broadcast_to([P, KJ, D]), ALU.mult))
                dve.sem_inc(sem("exn"), 1)
                dve.wait_ge(sem("exTp"), 1)
                step(nc.vector.tensor_scalar(exT[:, :], pb[1][:, :], vc("L0_tok_lln_g"), vc("L0_tok_lln_b"),
                                             ALU.mult, ALU.add))
                dve.sem_inc(sem("exT"), 1)
                dve.wait_ge(sem("eTp"), 1)
                step(nc.vector.tensor_scalar(TT[:, :], pb[2][:, :], vc("L0_tok_lb2"), None, ALU.add))
                step(nc.vector.tensor_scalar(gh[:, :], head[:, :], vc("L0_tok_fln_g"), None, ALU.mult))
                dve.sem_inc(sem("gh"), 1)
                dve.wait_ge(sem("ghm"), 1)
                step(nc.vector.tensor_tensor(wl[:, :], gh[:, :], pb[3][:, 0:V], ALU.subtract))
                step(nc.vector.tensor_copy(frow[:, :], pb[3][:, V:2 * V]))
                step(nc.vector.tensor_copy(mw2T[:, :], pb[4][:, 0:D]))
                dve.sem_inc(sem("mw2T"), 1)
                dve.wait_ge(sem("w21p"), 1)
                step(nc.vector.tensor_copy(w21[:, :], pb[7][:, 0:D]))
                step(nc.vector.tensor_tensor(bu1[:, :], pb[7][:, D:D + 1], vc("L0_tok_upd_b1"), ALU.add))
                dve.wait_ge(sem("tlp"), 1)
                step(nc.vector.tensor_tensor(TT[:, :], TT[:, :], pb[5][:, :], ALU.add))
                dve.sem_inc(sem("TT"), 1)
                dve.wait_ge(sem("TTm"), 1)
                step(nc.vector.tensor_tensor(TTc[:, :], TT[:, :], pb[6][:, :], ALU.subtract))
                step(nc.vector.tensor_tensor(g1[:, 0, :], TTc[:, :], TTc[:, :], ALU.mult))
                dve.sem_inc(sem("TTq"), 1)
                dve.wait_ge(sem("tabs"), 1)
                step(nc.vector.tensor_copy(Tp[:, :, :].rearrange("p k d -> p (k d)"), pb[1][:, :]))
                for j in range(2):
                    hf = slice(j * V, (j + 1) * V)
                    step(nc.vector.tensor_copy(Tl[hf, :, j, :],
                                               pb[2][hf, 0:KJ * V].rearrange("p (k e) -> p k e", k=KJ)))
                    for k in range(KJ):
                        step(nc.vector.tensor_copy(vTs[hf, k, 2 * k + j:2 * k + j + 1], pb[3][hf, k:k + 1]))
                dve.sem_inc(sem("tabsb"), 1)
                step(nc.vector.tensor_copy(xf[:, :, :], xi[:, :, :]))
                dve.sem_inc(sem("xf"), 1)
                dve.wait_ge(sem("xTp"), 1)
                step(nc.vector.tensor_copy(xT[:, :], pb[0][:, 0:P]))
                dve.sem_inc(sem("xT"), 1)
                dve.wait_ge(sem("iota"), 3)
                for g in range(NG):
                    dve.wait_ge(sem("xb"), g + 1)
                    nc.vector.tensor_scalar(OH[:, :, g * P:(g + 1) * P],
                                            pb[4 + g % 4][:, :].rearrange("p (k n) -> p k n", k=KJ),
                                            vp[:, 0:1], None, ALU.is_equal).then_inc(sem("oh"), 1)
                for b in range(4):
                    dve.wait_ge(sem("summ"), b + 1)
                    nc.vector.tensor_scalar(hm[:, b * 512:(b + 1) * 512], pb[b][:, :], 1.0 / C,
                                            vc("L0_tok_pool_b"), ALU.mult, ALU.add).then_inc(sem("hm"), 1)

            @block.scalar
            def _(act):
                for c in range(2):
                    act.wait_ge(sem("g1p"), c + 1)
                    nc.scalar.activation(g1[:, c, :], pb[6 + c][:, :], ACT.Gelu, bias=vc("L0_tok_lb1", c)) \
                        .then_inc(sem("g1"), 1)

            @block.tensor
            def _(pe):
                pe.wait_ge(sem("loaded"), NLOAD)
                nc.tensor.transpose(pb[0][:, 0:NR], vrow[:, :], ident[0:NR, 0:NR]).then_inc(sem("vcolp"), 1)
                pe.wait_ge(sem("exn"), 1)
                for k in range(KJ):
                    nc.tensor.transpose(pb[2][:, k * P:(k + 1) * P], epost[:, k, :], ident[:, :])
                    last = nc.tensor.transpose(pb[1][:, k * P:(k + 1) * P], exc[:, k, :], ident[:, :])
                last.then_inc(sem("exTp"), 1)
                pe.sem_inc(sem("eTp"), 1)
                pe.wait_ge(sem("exT"), 1)
                for c in range(2):
                    nc.tensor.matmul(pb[6 + c][:, :], lw1[:, c * D:(c + 1) * D], exT[:, :],
                                     start=True, stop=True).then_inc(sem("g1p"), 1)
                pe.wait_ge(sem("gh"), 1)
                nc.tensor.matmul(pb[3][:, 0:V], onesD[:, :], gh[:, :], start=True, stop=True)
                nc.tensor.matmul(pb[3][:, V:2 * V], bcast(vc("L0_tok_fln_b"), [P, P]), head[:, :],
                                 start=True, stop=True)
                nc.tensor.transpose(pb[4][:, 0:D], mw2[:, :], ident[:, :]).then_inc(sem("ghm"), 1)
                for c in range(2):
                    pe.wait_ge(sem("g1"), c + 1)
                    last = nc.tensor.matmul(pb[5][:, :], lw2[:, c, :], g1[:, c, :], start=c == 0, stop=c == 1)
                last.then_inc(sem("tlp"), 1)
                pe.wait_ge(sem("mw2T"), 1)
                nc.tensor.matmul(pb[7][:, 0:D], mw2T[:, :], uw1[:, 1, :], start=True, stop=True)
                nc.tensor.matmul(pb[7][:, D:D + 1], uw1[:, 1, :], vc("L0_tok_msg_b2"),
                                 start=True, stop=True).then_inc(sem("w21p"), 1)
                pe.wait_ge(sem("TT"), 1)
                nc.tensor.matmul(pb[6][:, :], onesD[:, :], TT[:, :], start=True, stop=True).then_inc(sem("TTm"), 1)
                pe.wait_ge(sem("TTq"), 1)
                for k in range(KJ):
                    sl = TT[:, k * P:(k + 1) * P]
                    nc.tensor.matmul(pb[1][:, k * D:(k + 1) * D], sl, poolw[:, :], start=True, stop=True)
                    nc.tensor.matmul(pb[2][:, k * V:(k + 1) * V], sl, wl[:, :], start=True, stop=True)
                    last = nc.tensor.matmul(pb[3][:, k:k + 1], g1[:, 0, k * P:(k + 1) * P], onesD[:, 0:1],
                                            start=True, stop=True)
                last.then_inc(sem("tabs"), 1)
                pe.wait_ge(sem("xf"), 1)
                nc.tensor.transpose(pb[0][:, 0:P], xf[:, :, :].rearrange("p g c -> p (g c)"), ident[:, :]) \
                    .then_inc(sem("xTp"), 1)
                pe.wait_ge(sem("xT"), 1)
                for g in range(NG):
                    if g >= 4:
                        pe.wait_ge(sem("oh"), g - 3)
                    for k in range(KJ):
                        for j in range(2):
                            r = g * C + 2 * k + j
                            last = nc.tensor.matmul(pb[4 + g % 4][j * V:(j + 1) * V, k * P:(k + 1) * P],
                                                    ident[:, r:r + 1].broadcast_to([P, V]), xT[:, :],
                                                    start=True, stop=True)
                    last.then_inc(sem("xb"), 1)
                pe.wait_ge(sem("oh"), NG)
                pe.wait_ge(sem("tabsb"), 1)
                for b in range(4):
                    for k in range(KJ):
                        last = nc.tensor.matmul(pb[b][:, :], Tp[:, k, :], OH[:, k, b * 512:(b + 1) * 512],
                                                start=k == 0, stop=k == KJ - 1)
                    last.then_inc(sem("summ"), 1)
        tower_rounds(nc, sem, pb, K, icnt, vc, mw1, w21, uw1, uw2, bu1, hm, sb)
        tower_logits(nc, sem, pb, K, vc, bcw, TTc, wl, OH, Tl, vTs, frow, hm, xf, viota, h_out, sb)


def tower_rounds(nc, sem, pb, K, icnt, vc, mw1, w21, uw1, uw2, bu1, hm, sb):
    NB, W = 4, NCH // 4
    SB = W // CPS
    selfp = [sb(f"selfp{i}", [P, W]) for i in range(4)]
    gel = [sb(f"gel{i}", [P, WIN + 1, W]) for i in range(2)]
    agg = [sb(f"agg{i}", [P, W]) for i in range(2)]
    ug = [sb(f"ug{i}", [P, W]) for i in range(4)]
    res = [sb(f"res{i}", [P, W]) for i in range(4)]
    sq = [sb(f"sqr{i}", [P, W]) for i in range(4)]
    blk = [slice(b * W, (b + 1) * W) for b in range(NB)]

    def seqs(ap):
        return ap.rearrange("p (s c) -> p s c", c=CPS)

    with nc.Block() as block:
        @block.tensor
        def _(pe):
            with pe.Fori(0, 3) as r:
                at = lambda b: r * NB + b + 1
                for b in range(NB):
                    pe.wait_ge(sem("hm"), at(b))
                    nc.tensor.matmul(pb[2 * b][:, :], mw1[:, 0, :], hm[:, blk[b]], start=True, stop=True)
                    nc.tensor.matmul(pb[2 * b + 1][:, :], mw1[:, 1, :], hm[:, blk[b]], start=True, stop=True) \
                        .then_inc(sem("msgp"), 1)
                for b in range(NB):
                    pe.wait_ge(sem("added"), at(b))
                    nc.tensor.matmul(pb[2 * b][:, :], uw1[:, 0, :], hm[:, blk[b]], start=True, stop=False)
                    pe.wait_ge(sem("agg"), at(b))
                    nc.tensor.matmul(pb[2 * b][:, :], w21[:, :], agg[b % 2][:, :], start=False, stop=True) \
                        .then_inc(sem("updp"), 1)
                for b in range(NB):
                    pe.wait_ge(sem("ug"), at(b))
                    nc.tensor.matmul(pb[2 * b + 1][:, :], uw2[:, :], ug[b][:, :], start=True, stop=True) \
                        .then_inc(sem("upd2p"), 1)
                for b in range(NB):
                    pe.wait_ge(sem("res"), at(b))
                    nc.tensor.matmul(pb[2 * b][:, :], K.onesD[:, :], res[b][:, :], start=True, stop=True) \
                        .then_inc(sem("meanp"), 1)
                for b in range(NB):
                    pe.wait_ge(sem("sq"), at(b))
                    nc.tensor.matmul(pb[2 * b + 1][:, :], K.onesD[:, :], sq[b][:, :], start=True, stop=True) \
                        .then_inc(sem("varp"), 1)

        @block.scalar
        def _(act):
            with act.Fori(0, 3) as r:
                at = lambda b: r * NB + b + 1
                for b in range(NB):
                    act.wait_ge(sem("msgp"), at(b))
                    nc.scalar.activation(selfp[b][:, :], pb[2 * b][:, :], ACT.Identity,
                                         bias=vc("L0_tok_msg_b1")).then_inc(sem("selfp"), 1)
                for b in range(NB):
                    act.wait_ge(sem("added"), at(b))
                    nc.scalar.activation(gel[b % 2][:, :, :], gel[b % 2][:, :, :], ACT.Gelu) \
                        .then_inc(sem("gel"), 1)
                for b in range(NB):
                    act.wait_ge(sem("updp"), at(b))
                    nc.scalar.activation(ug[b][:, :], pb[2 * b][:, :], ACT.Gelu, bias=bu1[:, 0:1]) \
                        .then_inc(sem("ug"), 1)
                for b in range(NB):
                    act.wait_ge(sem("resc"), at(b))
                    nc.scalar.activation(sq[b][:, :], res[b][:, :], ACT.Square).then_inc(sem("sq"), 1)
                for b in range(NB):
                    act.wait_ge(sem("varp"), at(b))
                    nc.scalar.activation(sq[b][:, :], pb[2 * b + 1][:, :], ACT.Sqrt, bias=K.eps[:, 0:1]) \
                        .then_inc(sem("std"), 1)

        @block.gpsimd
        def _(pool):
            step = None
            with pool.Fori(0, 3) as r:
                at = lambda b: r * NB + b + 1
                step = Chain(pool, sem("poolc"), r * (NB * WIN))
                for b in range(NB):
                    pool.wait_ge(sem("gel"), at(b))
                    g = gel[b % 2]
                    for d in range(1, WIN + 1):
                        step(nc.gpsimd.tensor_tensor(seqs(g[:, 0, :])[:, :, d:], seqs(g[:, 0, :])[:, :, d:],
                                                     seqs(g[:, d, :])[:, :, d:], ALU.add))
                    pool.wait_ge(sem("updp0"), at(b))
                    nc.gpsimd.tensor_tensor(seqs(agg[b % 2][:, :]), seqs(g[:, 0, :]),
                                            icnt[:, :].unsqueeze(1).broadcast_to([P, SB, CPS]), ALU.mult) \
                        .then_inc(sem("agg"), 1)

        @block.vector
        def _(dve):
            for g in gel:
                nc.vector.memset(g[:, :, :], 0.0).then_inc(sem("gel0"), 1)
            dve.wait_ge(sem("gel0"), 2)
            with dve.Fori(0, 3) as r:
                at = lambda b: r * NB + b + 1
                for b in range(NB):
                    dve.wait_ge(sem("selfp"), at(b))
                    if b >= 2:
                        dve.wait_ge(sem("agg"), at(b - 2))
                    g = gel[b % 2]
                    for d in range(WIN + 1):
                        last = nc.vector.tensor_tensor(seqs(g[:, d, :])[:, :, d:], seqs(selfp[b][:, :])[:, :, d:],
                                                       seqs(pb[2 * b + 1][:, :])[:, :, 0:CPS - d], ALU.add)
                    last.then_inc(sem("added"), 1)
                for b in range(NB):
                    dve.wait_ge(sem("upd2p"), at(b))
                    nc.vector.scalar_tensor_tensor(res[b][:, :], pb[2 * b + 1][:, :], vc("L0_tok_upd_b2"),
                                                   hm[:, blk[b]], ALU.add, ALU.add).then_inc(sem("res"), 1)
                for b in range(NB):
                    dve.wait_ge(sem("meanp"), at(b))
                    nc.vector.tensor_tensor(res[b][:, :], res[b][:, :], pb[2 * b][:, :], ALU.subtract) \
                        .then_inc(sem("resc"), 1)
                for b in range(NB):
                    dve.wait_ge(sem("std"), at(b))
                    nc.vector.reciprocal(sq[b][:, :], sq[b][:, :]).then_inc(sem("rs"), 1)
                for b in range(NB):
                    dve.wait_ge(sem("rs"), at(b))
                    nc.vector.tensor_tensor(res[b][:, :], res[b][:, :], sq[b][:, :], ALU.mult) \
                        .then_inc(sem("rn"), 1)
                    dve.wait_ge(sem("rn"), at(b))
                    nc.vector.tensor_scalar(hm[:, blk[b]], res[b][:, :], vc("L0_tok_mln_g"), vc("L0_tok_mln_b"),
                                            ALU.mult, ALU.add).then_inc(sem("hm"), 1)

        @block.sync
        def _(sp):
            sp.sem_inc(sem("updp0"), 2)
            for k in range(3 * NB - 2):
                sp.wait_ge(sem("updp"), k + 1)
                sp.sem_inc(sem("updp0"), 1)


def tower_logits(nc, sem, pb, K, vc, bcw, TTc, wl, OH, Tl, vTs, frow, hm, xf, viota, h_out, sb):
    NB, W = 4, NCH // 4
    bct = sb("bct", [P, NCH])
    bcq = sb("bcq", [P, NCH])
    oh = [sb(f"ohn{i}", [P, C, V]) for i in range(2)]
    cov = [sb(f"cov{i}", [P, C, V]) for i in range(2)]
    st = [sb(f"lst{i}", [P, 3, C]) for i in range(2)]
    lg = [sb(f"lg{i}", [P, C, V]) for i in range(2)]
    h_v = h_out.rearrange("(g n c) e -> g n (c e)", n=P, c=C)
    with nc.Block() as block:
        @block.tensor
        def _(pe):
            for b in range(NB):
                nc.tensor.matmul(pb[b][:, :], bcw[:, :], hm[:, b * W:(b + 1) * W],
                                 start=True, stop=True).then_inc(sem("bcp"), 1)
            for b in range(NB):
                pe.wait_ge(sem("bct"), b + 1)
                nc.tensor.matmul(pb[4 + b][:, :], K.onesD[:, :], bct[:, b * W:(b + 1) * W],
                                 start=True, stop=True).then_inc(sem("bcm"), 1)
            pe.wait_ge(sem("bcq"), 4)
            for g in range(NG):
                u, n = g % 2, slice(g * P, (g + 1) * P)
                pc, pl, pv = pb[u], pb[2 + u], pb[4 + u]
                if g >= 2:
                    pe.wait_ge(sem("lg"), g - 1)
                nc.tensor.matmul(pv[:, 0:C], bcq[:, n], bcast(K.onesD[:, 0:1], [P, C]), start=True, stop=False)
                nc.tensor.matmul(pl[:, :].rearrange("p (c e) -> p c e", c=C), bct[:, n],
                                 wl[:, :].unsqueeze(1).broadcast_to([P, C, V]), start=True, stop=False)
                nc.tensor.matmul(pc[:, :], bct[:, n], TTc[:, :], start=True, stop=True)
                for k in range(KJ):
                    nc.tensor.matmul(pv[:, 0:C], OH[:, k, n], vTs[:, k, :], start=False, stop=k == KJ - 1)
                    last = nc.tensor.matmul(pl[:, k * P:(k + 1) * P], OH[:, k, n],
                                            Tl[:, k, :, :].rearrange("p j e -> p (j e)"),
                                            start=False, stop=k == KJ - 1)
                last.then_inc(sem("lgp"), 1)

        @block.scalar
        def _(act):
            for b in range(NB):
                act.wait_ge(sem("bcp"), b + 1)
                nc.scalar.activation(bct[:, b * W:(b + 1) * W], pb[b][:, :], ACT.Identity,
                                     bias=vc("L0_tok_bc_b")).then_inc(sem("bct"), 1)
            for b in range(NB):
                act.wait_ge(sem("bcc"), b + 1)
                nc.scalar.activation(bcq[:, b * W:(b + 1) * W], bct[:, b * W:(b + 1) * W], ACT.Square) \
                    .then_inc(sem("bcq"), 1)

        @block.gpsimd
        def _(pool):
            for g in range(NG):
                st_ = st[g % 2]
                pool.wait_ge(sem("lvar"), g + 1)
                nc.gpsimd.tensor_tensor(st_[:, 2, :], st_[:, 1, :], K.mhalf[:, 0:1].broadcast_to([P, C]), ALU.pow) \
                    .then_inc(sem("lrstd"), 1)

        @block.vector
        def _(dve):
            for b in range(NB):
                dve.wait_ge(sem("bcm"), b + 1)
                nc.vector.tensor_tensor(bct[:, b * W:(b + 1) * W], bct[:, b * W:(b + 1) * W], pb[4 + b][:, :],
                                        ALU.subtract).then_inc(sem("bcc"), 1)
            step = Chain(dve, sem("ldve"))
            for g in range(NG):
                u = g % 2
                step(nc.vector.tensor_tensor(oh[u][:, :, :], viota[:, :, :],
                                             xf[:, g, :].unsqueeze(2).broadcast_to([P, C, V]), ALU.is_equal))
                dve.wait_ge(sem("lgp"), g + 1)
                nc.vector.tensor_tensor(cov[u][:, :, :], oh[u][:, :, :],
                                        pb[u][:, :].rearrange("p (c e) -> p c e", c=C), ALU.mult) \
                    .then_inc(sem("covm"), 1)
                dve.wait_ge(sem("covm"), g + 1)
                step(nc.vector.tensor_reduce(st[u][:, 0, :], cov[u][:, :, :], AX.X, ALU.add))
                step(nc.vector.scalar_tensor_tensor(st[u][:, 1, :], st[u][:, 0, :], 2.0 / D, pb[4 + u][:, 0:C],
                                                    ALU.mult, ALU.add))
                nc.vector.tensor_scalar(st[u][:, 1, :], st[u][:, 1, :], EPS, None, ALU.add).then_inc(sem("lvar"), 1)
                dve.wait_ge(sem("lrstd"), g + 1)
                if g >= 2:
                    dve.wait_ge(sem(f"lstored{u}"), 16 * (g // 2))
                step(nc.vector.tensor_tensor(lg[u][:, :, :], pb[2 + u][:, :].rearrange("p (c e) -> p c e", c=C),
                                             st[u][:, 2, :].unsqueeze(2).broadcast_to([P, C, V]), ALU.mult))
                nc.vector.tensor_tensor(lg[u][:, :, :], lg[u][:, :, :],
                                        frow[:, :].unsqueeze(1).broadcast_to([P, C, V]), ALU.add) \
                    .then_inc(sem("lg"), 1)

        @block.sync
        def _(sp):
            for g in range(NG):
                sp.wait_ge(sem("lg"), g + 1)
                sp.dma_start(h_v[g], lg[g % 2][:, :, :].rearrange("p c e -> p (c e)")) \
                    .then_inc(sem(f"lstored{g % 2}"), 16)
            for u in range(2):
                sp.wait_ge(sem(f"lstored{u}"), 16 * (NG // 2))


HEADS, HD = 8, 8
NJ = 4
NGRP = HEADS // NJ
Q_SCALE = HD ** -0.5


def attention(nc, name, K, A, h_in, h_out, wide):
    T = 2 if wide else 4
    NT = T * P
    NIT = NTOK // NT // 2
    W = 64
    with ExitStack() as ctx:
        def sb(n, shape, dt=F32):
            return [ctx.enter_context(nc.sbuf_tensor(f"{name}_{n}{u}", shape, dt)) for u in range(2)]

        sem = Signals(nc, name + "_")
        ctx.callback(sem.close)

        hin = sb("hin", [P, T, V])
        stat = sb("stat", [P, T, 6])
        mv = sb("mv", [P, T, 2])
        rstd = sb("rstd", [P, 2, T])
        xn = sb("xn", [P, T, V])
        xT = sb("xT", [V, NT])
        qs = sb("qs", [P, NGRP, NT])
        ks = sb("ks", [P, NGRP, NT])
        qa = sb("qa", [P, NGRP, NT])
        va = sb("va", [P, T, HEADS, 32])
        mx = sb("mx", [P, T, NGRP, P])
        if wide:
            pr = sb("pr", [P, 2, NJ, NGRP, NT])
        else:
            pr = sb("pr", [P, NJ, NGRP, T, W])
        oT = sb("oT", [P, NGRP, NT])
        rs = sb("rs", [P, T * NGRP, NJ])
        on = sb("on", [P, T, V])
        onT = sb("onT", [V, NT])
        hres = sb("hres", [P, T, V])
        hout = sb("hout", [P, T, V])
        quad = [ctx.enter_context(nc.psum_tensor(f"{name}_quad{u}", [P, 4, 512], F32)) for u in range(2)]
        flat = [q[:, :, :].rearrange("p b n -> p (b n)") for q in quad]
        hi_v = h_in.rearrange("(i u t p) e -> i u p t e", p=P, t=T, u=2)
        ho_v = h_out.rearrange("(i u t p) e -> i u p t e", p=P, t=T, u=2)
        NS = 2 if wide else 1
        vbase = 512 if wide else 0
        obase = 512 if wide else 1024
        rows = [slice(32 * j, 32 * j + HD + 1) for j in range(NJ)]

        def up(i, u):
            return 2 * i + u + 1

        def score_mms(u, p, stat_, mov):
            if wide:
                for g in range(NGRP):
                    for j in range(NJ):
                        last = nc.tensor.matmul(quad[u][:, j, g * NT:(g + 1) * NT],
                                                stat_[u][rows[j], g, p * P:(p + 1) * P], mov[u][rows[j], g, :],
                                                start=True, stop=True, tile_position=(32 * j, 0))
                return last
            for g in range(NGRP):
                for t in range(T):
                    for par in range(2):
                        w = slice(t * P + par * W, t * P + (par + 1) * W)
                        for j in range(NJ):
                            c = (g * T + t) * W
                            last = nc.tensor.matmul(quad[u][par * W:(par + 1) * W, j, c:c + W],
                                                    stat_[u][rows[j], g, w], mov[u][rows[j], g, w],
                                                    start=True, stop=True, tile_position=(32 * j, par * W))
            return last

        with nc.Block() as block:
            @block.sync
            def _(sp):
                with sp.Fori(0, NIT) as i:
                    for u in range(2):
                        sp.wait_ge(sem("hin_seen"), up(i, u))
                        sp.wait_ge(sem("hin_kept"), up(i, u))
                        sp.dma_start(hin[u][:, :, :], hi_v[i, u]).then_inc(sem(f"hin{u}"), 16)
                    for u in range(2):
                        sp.wait_ge(sem("hout"), up(i, u))
                        sp.dma_start(ho_v[i, u], hout[u][:, :, :]).then_inc(sem(f"stored{u}"), 16)
                for u in range(2):
                    sp.wait_ge(sem(f"stored{u}"), 16 * (NIT + 1))

            @block.gpsimd
            def _(pool):
                pool.sem_inc(sem("hin_kept"), 2)
                with pool.Fori(0, NIT) as i:
                    for u in range(2):
                        pool.wait_ge(sem("var"), up(i, u))
                        nc.gpsimd.tensor_tensor(rstd[u][:, 1, :], rstd[u][:, 0, :],
                                                K.mhalf[:, 0:1].broadcast_to([P, T]), ALU.pow) \
                            .then_inc(sem("rstd"), 1)
                    for u in range(2):
                        pool.wait_ge(sem("hres_free"), up(i, u))
                        nc.gpsimd.tensor_tensor(hres[u][:, :, :], hin[u][:, :, :],
                                                A.brow[:, :].unsqueeze(1).broadcast_to([P, T, V]), ALU.add) \
                            .then_inc(sem("hin_kept"), 1)

            @block.vector
            def _(dve):
                for u in range(2):
                    nc.vector.memset(va[u][:, :, :, :], 0.0).then_inc(sem("pad"), 1)
                    nc.vector.memset(mx[u][:, :, :, :], 0.0).then_inc(sem("pad"), 1)
                dve.wait_ge(sem("pad"), 4)
                for u in range(2):
                    nc.vector.memset(va[u][:, :, :, 0:1], 1.0).then_inc(sem("pad"), 1)
                dve.wait_ge(sem("pad"), 6)
                dve.sem_inc(sem("hin_seen"), 2)
                dve.sem_inc(sem("hres_free"), 2)
                dve.sem_inc(sem("quad_free"), 2)
                for u in range(2):
                    dve.sem_inc(sem(f"stored{u}"), 16)
                per = 2 * (2 * T + 2)
                with dve.Fori(0, NIT) as i:
                    step = Chain(dve, sem("ln"), i * per)
                    for u in range(2):
                        dve.wait_ge(sem(f"hin{u}"), 16 * i + 16)
                        for t in range(T):
                            nc.vector.bn_stats(stat[u][:, t, :], hin[u][:, t, :]).then_inc(sem("ln"), 1)
                            step.n += 1
                        wait_alone(dve, sem("ln"), step.start + step.n, sem("dve_passed"))
                        for t in range(T):
                            nc.vector.bn_aggr(mv[u][:, t, :], stat[u][:, t, :]).then_inc(sem("ln"), 1)
                            step.n += 1
                        dve.wait_ge(sem("ln"), step.start + step.n)
                        nc.vector.tensor_scalar(rstd[u][:, 0, :], mv[u][:, :, 1], EPS, None, ALU.add) \
                            .then_inc(sem("var"), 1)
                    for u in range(2):
                        step(nc.vector.tensor_tensor(xn[u][:, :, :], hin[u][:, :, :],
                                                     mv[u][:, :, 0:1].broadcast_to([P, T, V]), ALU.subtract))
                        dve.wait_ge(sem("rstd"), up(i, u))
                        step(nc.vector.tensor_tensor(xn[u][:, :, :], xn[u][:, :, :],
                                                     rstd[u][:, 1, :].unsqueeze(2).broadcast_to([P, T, V]),
                                                     ALU.mult))
                        dve.sem_inc(sem("hin_seen"), 1)
                        dve.sem_inc(sem("xn"), 1)
                    assert step.n == per
                    for u in range(2):
                        dve.wait_ge(sem("qk_ps"), up(i, u))
                        for g in range(NGRP):
                            nc.vector.tensor_scalar(ks[u][:, g, :], flat[u][:, 1024 + g * NT:1024 + (g + 1) * NT],
                                                    A.kb[:, g:g + 1], None, ALU.add).then_inc(sem("ks"), 1)
                        dve.wait_ge(sem("v_ps"), up(i, u))
                        nc.vector.tensor_copy(va[u][:, :, :, 1:HD + 1],
                                              flat[u][:, vbase:vbase + T * V].rearrange(
                                                  "p (t h d) -> p t h d", t=T, h=HEADS)).then_inc(sem("va"), 1)
                    for s in range(NS):
                        for u in range(2):
                            dve.wait_ge(sem(f"s{s}_ps"), up(i, u))
                            if wide and s == 0:
                                blk = flat[u].rearrange("p (h m) -> p h m", m=NT)[:, :, P:]
                                nc.vector.tensor_tensor(blk, blk, A.biasS[:, :, :], ALU.add) \
                                    .then_inc(sem("s_bias"), 1)
                                dve.wait_ge(sem("s_bias"), up(i, u))
                            elif not wide:
                                blk = flat[u].rearrange("p (h m) -> p h m", m=W)
                                nc.vector.tensor_tensor(blk, blk,
                                                        A.biasS[:, :].unsqueeze(1).broadcast_to([P, 2048 // W, W]),
                                                        ALU.add).then_inc(sem("s_bias"), 1)
                                dve.wait_ge(sem("s_bias"), up(i, u))
                            if wide:
                                nc.vector.tensor_reduce(
                                    mx[u][:, s, :, 0:P:32].rearrange("p g j -> p j g"),
                                    quad[u][:, :, :].rearrange("p j (g m) -> p j g m", g=NGRP), AX.X, ALU.max) \
                                    .then_inc(sem(f"m{s}"), 1)
                            else:
                                for g in range(NGRP):
                                    last = nc.vector.tensor_reduce(
                                        mx[u][:, :, g, 0:P:32].rearrange("p t j -> p j t"),
                                        quad[u][:, :, g * 256:(g + 1) * 256].rearrange("p j (t m) -> p j t m", t=T),
                                        AX.X, ALU.max)
                                last.then_inc(sem(f"m{s}"), 1)
                    for u in range(2):
                        dve.wait_ge(sem("mT_ps"), up(i, u))
                        nc.vector.tensor_tensor(qa[u][:, :, :].rearrange("p g n -> p (g n)"),
                                                qs[u][:, :, :].rearrange("p g n -> p (g n)"),
                                                flat[u][:, 0:NGRP * NT], ALU.subtract).then_inc(sem("qa"), 1)
                    for u in range(2):
                        dve.wait_ge(sem(f"t{NS - 1}_ps"), up(i, u))
                        if wide:
                            blk = flat[u].rearrange("p (h m) -> p h m", m=NT)[:, :, 0:P]
                            bias = A.biasT[:, :, :]
                        else:
                            blk = flat[u].rearrange("p (h m) -> p h m", m=W)
                            bias = A.biasT[:, :].unsqueeze(1).broadcast_to([P, 2048 // W, W])
                        nc.vector.tensor_tensor(blk, blk, bias, ALU.add).then_inc(sem("t_bias"), 1)
                    for u in range(2):
                        dve.wait_ge(sem("o_ps"), up(i, u))
                        o = flat[u][:, obase:obase + T * NGRP * P].rearrange("p (a j s) -> p a j s", j=NJ, s=32)
                        nc.vector.reciprocal(rs[u][:, :, :], o[:, :, :, 0]).then_inc(sem("rs"), 1)
                        dve.wait_ge(sem("rs"), up(i, u))
                        nc.vector.tensor_tensor(
                            on[u][:, :, :].rearrange("p t (g j d) -> p (t g) j d", g=NGRP, d=HD),
                            o[:, :, :, 1:HD + 1], rs[u][:, :, :].unsqueeze(3).broadcast_to([P, T * NGRP, NJ, HD]),
                            ALU.mult).then_inc(sem("on"), 1)
                    for u in range(2):
                        dve.wait_ge(sem("y_ps"), up(i, u))
                        dve.wait_ge(sem("hin_kept"), up(i, u) + 2)
                        dve.wait_ge(sem(f"stored{u}"), 16 * i + 16)
                        nc.vector.tensor_tensor(hout[u][:, :, :].rearrange("p t e -> p (t e)"),
                                                flat[u][:, 512:512 + T * V],
                                                hres[u][:, :, :].rearrange("p t e -> p (t e)"), ALU.add) \
                            .then_inc(sem("hout"), 1)
                        dve.wait_ge(sem("hout"), up(i, u))
                        dve.sem_inc(sem("hres_free"), 1)
                        dve.sem_inc(sem("quad_free"), 1)

            @block.scalar
            def _(act):
                with act.Fori(0, NIT) as i:
                    for u in range(2):
                        act.wait_ge(sem("xT_ps"), up(i, u))
                        nc.scalar.copy(xT[u][:, :], flat[u][0:V, 0:NT]).then_inc(sem("xT"), 1)
                    for u in range(2):
                        act.wait_ge(sem("qk_ps"), up(i, u))
                        for g in range(NGRP):
                            nc.scalar.activation(qs[u][:, g, :], flat[u][:, g * NT:(g + 1) * NT], ACT.Identity,
                                                 bias=A.qb[:, g:g + 1], scale=Q_SCALE).then_inc(sem("qs"), 1)
                    for s in range(NS):
                        for u in range(2):
                            if s == NS - 1:
                                act.wait_ge(sem("t_bias"), up(i, u))
                            else:
                                act.wait_ge(sem(f"t{s}_ps"), up(i, u))
                            dst = pr[u][:, s, :, :, :].rearrange("p j g n -> p (j g n)") if wide \
                                else pr[u][:, :, :, :, :].rearrange("p j g t n -> p (j g t n)")
                            nc.scalar.activation(dst, flat[u], ACT.Exp).then_inc(sem(f"p{s}"), 1)
                    for u in range(2):
                        act.wait_ge(sem("pv_ps"), up(i, u))
                        if wide:
                            last = nc.scalar.copy(oT[u][:, :, :].rearrange("p g n -> p (g n)"), flat[u][:, 0:512])
                        else:
                            for par in range(2):
                                last = nc.scalar.copy(
                                    oT[u][:, :, :].rearrange("p g (t q n) -> p (g t) q n", q=2, n=W)[:, :, par, :],
                                    quad[u][:, par, :].rearrange("p (a n) -> p a n", n=W))
                        last.then_inc(sem("oT"), 1)
                    for u in range(2):
                        act.wait_ge(sem("onT_ps"), up(i, u))
                        nc.scalar.copy(onT[u][:, :], flat[u][0:V, 0:NT]).then_inc(sem("onT"), 1)

            @block.tensor
            def _(pe):
                with pe.Fori(0, NIT) as i:
                    for u in range(2):
                        pe.wait_ge(sem("xn"), up(i, u))
                        wait_alone(pe, sem("quad_free"), up(i, u), sem("pe_passed"))
                        for t in range(T):
                            last = nc.tensor.transpose(flat[u][0:V, t * P:(t + 1) * P], xn[u][:, t, :], K.ident[:, :])
                        last.then_inc(sem("xT_ps"), 1)
                    for u in range(2):
                        pe.wait_ge(sem("xT"), up(i, u))
                        for g in range(NGRP):
                            nc.tensor.matmul(flat[u][:, g * NT:(g + 1) * NT], A.wq[:, g, :], xT[u][:, :],
                                             start=True, stop=True)
                        for g in range(NGRP):
                            last = nc.tensor.matmul(flat[u][:, 1024 + g * NT:1024 + (g + 1) * NT], A.wk[:, g, :],
                                                    xT[u][:, :], start=True, stop=True)
                        last.then_inc(sem("qk_ps"), 1)
                        if wide:
                            for t in range(T):
                                last = nc.tensor.matmul(flat[u][:, vbase + t * V:vbase + (t + 1) * V],
                                                        xT[u][:, t * P:(t + 1) * P], A.wv[:, :], start=True, stop=True)
                            last.then_inc(sem("v_ps"), 1)
                    if not wide:
                        for u in range(2):
                            pe.wait_ge(sem("qs"), NGRP * up(i, u))
                            for t in range(T):
                                last = nc.tensor.matmul(flat[u][:, vbase + t * V:vbase + (t + 1) * V],
                                                        xT[u][:, t * P:(t + 1) * P], A.wv[:, :], start=True, stop=True)
                            last.then_inc(sem("v_ps"), 1)
                    for s in range(NS):
                        for u in range(2):
                            if s == 0:
                                pe.wait_ge(sem("qs"), NGRP * up(i, u))
                                pe.wait_ge(sem("ks"), NGRP * up(i, u))
                                pe.wait_ge(sem("va"), up(i, u))
                            else:
                                pe.wait_ge(sem(f"m{s - 1}"), up(i, u))
                            score_mms(u, s, qs, ks).then_inc(sem(f"s{s}_ps"), 1)
                    for u in range(2):
                        pe.wait_ge(sem(f"m{NS - 1}"), up(i, u))
                        for g in range(NGRP):
                            for t in range(T):
                                c = g * NT + t * P
                                last = nc.tensor.transpose(flat[u][:, c:c + P], mx[u][:, t, g, :], K.ident[:, :])
                        last.then_inc(sem("mT_ps"), 1)
                    for s in range(NS):
                        for u in range(2):
                            if s == 0:
                                pe.wait_ge(sem("qa"), up(i, u))
                            else:
                                pe.wait_ge(sem(f"p{s - 1}"), up(i, u))
                            score_mms(u, s, ks, qa).then_inc(sem(f"t{s}_ps"), 1)
                    for u in range(2):
                        wait_alone(pe, sem(f"p{NS - 1}"), up(i, u), sem("pe_passed"))
                        if wide:
                            for g in range(NGRP):
                                for s in range(NS):
                                    for j in range(NJ):
                                        last = nc.tensor.matmul(flat[u][32 * j:32 * j + 32, g * NT:(g + 1) * NT],
                                                                va[u][:, s, g * NJ + j, :], pr[u][:, s, j, g, :],
                                                                start=s == 0, stop=s == NS - 1,
                                                                tile_position=(0, 32 * j))
                        else:
                            for g in range(NGRP):
                                for t in range(T):
                                    for par in range(2):
                                        for j in range(NJ):
                                            k = slice(par * W, (par + 1) * W)
                                            c = (g * T + t) * W
                                            last = nc.tensor.matmul(quad[u][32 * j:32 * j + 32, par, c:c + W],
                                                                    va[u][k, t, g * NJ + j, :], pr[u][k, j, g, t, :],
                                                                    start=True, stop=True,
                                                                    tile_position=(par * W, 32 * j))
                        last.then_inc(sem("pv_ps"), 1)
                    for u in range(2):
                        pe.wait_ge(sem("oT"), up(i, u))
                        for t in range(T):
                            for g in range(NGRP):
                                c = obase + (t * NGRP + g) * P
                                last = nc.tensor.transpose(flat[u][:, c:c + P], oT[u][:, g, t * P:(t + 1) * P],
                                                           K.ident[:, :])
                        last.then_inc(sem("o_ps"), 1)
                    for u in range(2):
                        wait_alone(pe, sem("on"), up(i, u), sem("pe_passed"))
                        for t in range(T):
                            last = nc.tensor.transpose(flat[u][0:V, t * P:(t + 1) * P], on[u][:, t, :], K.ident[:, :])
                        last.then_inc(sem("onT_ps"), 1)
                    for u in range(2):
                        pe.wait_ge(sem("onT"), up(i, u))
                        for t in range(T):
                            last = nc.tensor.matmul(flat[u][:, 512 + t * V:512 + (t + 1) * V],
                                                    onT[u][:, t * P:(t + 1) * P], A.wo[:, :], start=True, stop=True)
                        last.then_inc(sem("y_ps"), 1)


def attention_weights(nc, a, K, dram_ext, ctx):
    A0, A1 = Consts(), Consts()

    def sb(name, shape):
        return ctx.enter_context(nc.sbuf_tensor(name, shape, F32))

    for A, n in ((A0, "a0"), (A1, "a1")):
        A.wq, A.wk = sb(n + "_wq", [V, NGRP, P]), sb(n + "_wk", [V, NGRP, P])
        A.wv, A.wo = sb(n + "_wv", [V, V]), sb(n + "_wo", [V, V])
        A.qb, A.kb = sb(n + "_qb", [P, NGRP]), sb(n + "_kb", [P, NGRP])
        A.brow = sb(n + "_brow", [P, V])
    A0.biasS, A0.biasT = sb("a0_biasS", [P, 64]), sb("a0_biasT", [P, 64])
    A1.biasS, A1.biasT = sb("a1_biasS", [P, HEADS, P]), sb("a1_biasT", [P, HEADS, P])
    EXT = 2 * P - 1
    NTAB = a["L1_attn_rpb_table"].shape[0]
    with ExitStack() as tmp:
        def ts(name, shape):
            return tmp.enter_context(nc.sbuf_tensor(name, shape, F32))

        sem = Signals(nc, "aw_")
        tmp.callback(sem.close)

        w0 = ts("aw_w0", [V, 3, V])
        o0 = ts("aw_o0", [V, V])
        w1 = ts("aw_w1", [V, 3 * V])
        tab = ts("aw_tab", [NTAB, HEADS])
        ext = ts("aw_ext", [HEADS, EXT])
        hank0 = ts("aw_hank0", [P, 64])
        hank1 = ts("aw_hank1", [P, HEADS, P])
        brd = ts("aw_brd", [P, V])
        bv = ts("aw_bv", [V, 1])
        bcols = ts("aw_bcols", [4, P])
        rel2 = ts("aw_rel2", [64, 2, 64])
        ps = [tmp.enter_context(nc.psum_tensor(f"aw_ps{b}", [P, 512], F32)) for b in range(8)]

        def spread(ap):
            return ap.rearrange("p (j s) -> p j s", s=32)[:, :, 1:HD + 1]

        with nc.Block() as block:
            @block.sync
            def _(sp):
                sp.wait_ge(sem("zero"), 1)
                loads = [(w0[:, :, :], a["L0_attn_w_qkv"].rearrange("(q o) c -> o q c", q=3)),
                         (o0[:, :], a["L0_attn_w_proj"]),
                         (w1[:, :], a["L1_attn_qkv_w"]),
                         (A1.wo[:, :], a["L1_attn_proj_w"]),
                         (tab[:, :], a["L1_attn_rpb_table"]),
                         (A0.brow[:, :], a["L0_attn_b_proj"].partition_broadcast(P)),
                         (brd[:, :], a["L1_attn_proj_b"].partition_broadcast(P)),
                         (bv[:, :], a["L1_attn_qkv_b"][2 * V:3 * V].unsqueeze(1))]
                for r in range(4):
                    loads.append((spread(bcols[r:r + 1, :]),
                                  a["L1_attn_qkv_b"][r * 32:(r + 1) * 32].rearrange("(a j d) -> a j d", a=1, j=NJ)))
                rb = a["L0_attn_rel_bias"]
                for q in range(2):
                    loads.append((hank0[q * 64:(q + 1) * 64, :], bass.AP(rb.tensor, 0, [[1, 64], [1, 64]])))
                for dst, src in loads:
                    sp.dma_start(dst, src).then_inc(sem("loaded"), 16)
                K.n_aw = 16 * len(loads)
                sp.wait_ge(sem("ext"), 1)
                sp.dma_start(dram_ext, ext[:, :]).then_inc(sem("extd"), 16)
                sp.wait_ge(sem("extd"), 16)
                for j in range(NJ):
                    for g in range(NGRP):
                        h = g * NJ + j
                        sp.dma_start(hank1[:, j * NGRP + g, :],
                                     bass.AP(dram_ext.tensor, h * EXT, [[1, P], [1, P]])) \
                            .then_inc(sem("bT"), 16)

            @block.vector
            def _(dve):
                step = Chain(dve, sem("dve"))
                nc.vector.memset(bcols[:, :], 0.0).then_inc(sem("zero"), 1)
                for A in (A0, A1):
                    nc.vector.memset(A.wq[:, :, :], 0.0)
                    step(nc.vector.memset(A.wk[:, :, :], 0.0))
                nc.vector.memset(A0.qb[:, :], 0.0)
                dve.wait_ge(sem("loaded"), K.n_aw)
                for g in range(NGRP):
                    step(nc.vector.tensor_copy(spread(A1.wq[:, g, :]),
                                               w1[:, g * 32:(g + 1) * 32].rearrange("p (j d) -> p j d", j=NJ)))
                    step(nc.vector.tensor_copy(spread(A1.wk[:, g, :]),
                                               w1[:, V + g * 32:V + (g + 1) * 32].rearrange("p (j d) -> p j d", j=NJ)))
                step(nc.vector.tensor_copy(A1.wv[:, :], w1[:, 2 * V:3 * V]))
                step(nc.vector.tensor_reduce(A0.kb[:, 0:1], K.ident[:, 0:P:32], AX.X, ALU.add))
                step(nc.vector.tensor_copy(A0.kb[:, 1:2], A0.kb[:, 0:1]))
                step(nc.vector.tensor_copy(A0.biasT[:, :], hank0[:, ::-1]))
                for q in range(2):
                    step(nc.vector.tensor_copy(rel2[:, q, :], hank0[0:64, ::-1]))
                dve.sem_inc(sem("rel2"), 1)
                dve.wait_ge(sem("wT"), 1)
                for g in range(NGRP):
                    step(nc.vector.tensor_copy(spread(A0.wq[:, g, :]),
                                               ps[0][0:V, g * 32:(g + 1) * 32].rearrange("p (j d) -> p j d", j=NJ)))
                    step(nc.vector.tensor_copy(spread(A0.wk[:, g, :]),
                                               ps[1][0:V, g * 32:(g + 1) * 32].rearrange("p (j d) -> p j d", j=NJ)))
                step(nc.vector.tensor_copy(A0.wv[:, :], ps[2][0:V, 0:V]))
                step(nc.vector.tensor_copy(A0.wo[:, :], ps[3][0:V, 0:V]))
                step(nc.vector.tensor_copy(A0.biasS[:, :], ps[4][:, 0:64]))
                step(nc.vector.tensor_scalar(A1.qb[:, :], ps[5][:, 0:NGRP], Q_SCALE, None, ALU.mult))
                step(nc.vector.tensor_tensor(A1.kb[:, :], ps[5][:, NGRP:2 * NGRP], A0.kb[:, :], ALU.add))
                step(nc.vector.tensor_tensor(A1.brow[:, :], ps[7][:, 0:V], brd[:, :], ALU.add))
                step(nc.vector.memset(ext[:, :], 0.0))
                step(nc.vector.tensor_scalar(ext[:, 0:NTAB], ps[6][0:HEADS, 0:NTAB],
                                             ps[6][0:HEADS, NTAB - 1:NTAB], None, ALU.subtract))
                dve.sem_inc(sem("ext"), 1)
                dve.wait_ge(sem("bT"), 16 * HEADS)
                step(nc.vector.tensor_copy(A1.biasS[:, :, :], hank1[:, :, ::-1]))
                dve.sem_inc(sem("biasS"), 1)
                for c in range(2):
                    dve.wait_ge(sem("bS"), c + 1)
                    step(nc.vector.tensor_copy(A1.biasT[:, 4 * c:4 * c + 4, :].rearrange("p h m -> p (h m)"),
                                               ps[c][:, :]))

            @block.tensor
            def _(pe):
                pe.wait_ge(sem("loaded"), K.n_aw)
                idv = K.ident[0:V, 0:V]
                for q in range(3):
                    nc.tensor.transpose(ps[q][0:V, 0:V], w0[:, q, :], idv)
                nc.tensor.transpose(ps[3][0:V, 0:V], o0[:, :], idv)
                pe.wait_ge(sem("rel2"), 1)
                nc.tensor.transpose(ps[4][:, 0:64], rel2[:, :, :].rearrange("p q m -> p (q m)"), idv)
                nc.tensor.transpose(ps[5][:, 0:4], bcols[:, :], K.ident[0:4, 0:4])
                nc.tensor.transpose(ps[6][0:HEADS, 0:NTAB], tab[:, :], K.ident[0:NTAB, 0:NTAB])
                nc.tensor.matmul(ps[7][:, 0:V], bv[:, 0:1].broadcast_to([V, P]), A1.wo[:, :], start=True, stop=True) \
                    .then_inc(sem("wT"), 1)
                pe.wait_ge(sem("biasS"), 1)
                for h in range(HEADS):
                    last = nc.tensor.transpose(ps[h // 4][:, (h % 4) * P:(h % 4 + 1) * P], A1.biasS[:, h, :],
                                               K.ident[:, :])
                    if h % 4 == 3:
                        last.then_inc(sem("bS"), 1)
    return A0, A1


class Consts:
    pass


NE = 8
NPAIR = NE // 2
TB = 8
BN_EPS = 1e-3
NBLK = NTOK // (TB * P)


def norm_stats(nc, dve, sem, count, hin, stat, mv, tiles):
    n = count
    for t in range(tiles):
        nc.vector.bn_stats(stat[:, t, :], hin[:, t, :]).then_inc(sem, 1)
    wait = n + tiles
    dve.wait_ge(sem, wait)
    dve.sem_inc(sem, 1)
    for t in range(tiles):
        nc.vector.bn_aggr(mv[:, t, :], stat[:, t, :]).then_inc(sem, 1)
    dve.wait_ge(sem, wait + 1 + tiles)
    return 2 * tiles + 1


def ffn0_gate(nc, a, K, F, h_in):
    with ExitStack() as ctx:
        def sb(n, shape):
            return ctx.enter_context(nc.sbuf_tensor("fg_" + n, shape, F32))

        sem = Signals(nc, "fg_")
        ctx.callback(sem.close)

        names = ["b1", "g1", "be1", "m1", "v1", "b2", "g2", "be2", "m2", "v2"]
        NV = len(names)
        rows = sb("rows", [NV * NPAIR, P])
        col = sb("col", [P, NV, NPAIR])
        sc = sb("sc", [P, 2, NPAIR])
        dg = sb("dg", [P, P])
        b2m = sb("b2m", [P, NPAIR, NE])
        cb = sb("cb", [NE, V])
        bo = sb("bo", [NE, V])
        wr = sb("wr", [V, NE])
        br = sb("br", [P, NE])
        hin = [sb(f"hin{u}", [P, TB, V]) for u in range(2)]
        stat, mv = sb("stat", [P, TB, 6]), sb("mv", [P, TB, 2])
        rstd = sb("rstd", [P, 2, TB])
        xn = sb("xn", [P, TB, V])
        part = sb("part", [P, 2, V])
        feat = sb("feat", [P, 2, V])
        featT = sb("featT", [V, 2, P])
        lg = sb("lg", [P, 2, NE])
        st = sb("st", [P, 2, 2])
        gw = sb("gw", [P, 2, NE])
        gwT = sb("gwT", [NE, 2, P])
        ps = [ctx.enter_context(nc.psum_tensor(f"fg_ps{b}", [P, 512], F32)) for b in range(8)]
        hi_v = h_in.rearrange("(i u t p) e -> i u p t e", p=P, t=TB, u=2)
        NIT = NBLK // 2
        per = 2 * TB + 1 + 4
        with nc.Block() as block:
            @block.sync
            def _(sp):
                sp.wait_ge(sem("zero"), 1)
                n = 0

                def load(dst, src):
                    nonlocal n
                    sp.dma_start(dst, src).then_inc(sem("loaded"), 16)
                    n += 1
                for i, nm in enumerate(names):
                    load(rows[i * NPAIR:(i + 1) * NPAIR, :], a["L0_ffn_" + nm].rearrange("(q s) h -> q (s h)", s=2))
                for half in range(2):
                    load(F.w1[half * V:(half + 1) * V, :, :], a["L0_ffn_W1"].rearrange("e d h -> d e h"))
                    for p in range(NPAIR):
                        load(F.w2[half * V:(half + 1) * V, p, half * V:(half + 1) * V], a["L0_ffn_W2"][2 * p + half])
                load(F.wo[:, :, :], a["L0_ffn_Wo"].rearrange("(q s) h d -> (s h) q d", s=2))
                load(bo[:, :], a["L0_ffn_bo"])
                load(wr[:, :], a["L0_ffn_Wr"])
                load(br[:, :], a["L0_ffn_br"].partition_broadcast(P))
                F.n_loads = 16 * n
                with sp.Fori(0, NIT) as i:
                    for u in range(2):
                        sp.wait_ge(sem("hin_free"), 2 * i + u + 1)
                        sp.dma_start(hin[u][:, :, :], hi_v[i, u]).then_inc(sem(f"hin{u}"), 16)

            @block.gpsimd
            def _(pool):
                with pool.Fori(0, NIT) as i:
                    for u in range(2):
                        pool.wait_ge(sem("var"), 2 * i + u + 1)
                        nc.gpsimd.tensor_tensor(rstd[:, 1, :], rstd[:, 0, :], K.mhalf[:, 0:1].broadcast_to([P, TB]),
                                                ALU.pow).then_inc(sem("rstd"), 1)
                pool.wait_ge(sem("bnv"), 1)
                nc.gpsimd.tensor_tensor(sc[:, :, :], sc[:, :, :],
                                        K.mhalf[:, 0:1].unsqueeze(2).broadcast_to([P, 2, NPAIR]), ALU.pow) \
                    .then_inc(sem("bnr"), 1)

            @block.vector
            def _(dve):
                step = Chain(dve, sem("dve"))
                nc.vector.memset(b2m[:, :, :], 0.0).then_inc(sem("z"), 1)
                step(nc.vector.memset(F.w2[:, :, :], 0.0))
                dve.sem_inc(sem("zero"), 1)
                step(nc.vector.memset(feat[:, :, :], 0.0))
                dve.sem_inc(sem("hin_free"), 2)
                with dve.Fori(0, NIT) as i:
                    for u in range(2):
                        k = (2 * i + u) * per
                        dve.wait_ge(sem(f"hin{u}"), 16 * i + 16)
                        n = norm_stats(nc, dve, sem("ln"), k, hin[u], stat, mv, TB)
                        nc.vector.tensor_scalar(rstd[:, 0, :], mv[:, :, 1], EPS, None, ALU.add) \
                            .then_inc(sem("var"), 1)
                        link = Chain(dve, sem("ln"), k + n)
                        link(nc.vector.tensor_tensor(xn[:, :, :], hin[u][:, :, :],
                                                     mv[:, :, 0:1].broadcast_to([P, TB, V]), ALU.subtract))
                        dve.sem_inc(sem("hin_free"), 1)
                        dve.wait_ge(sem("rstd"), 2 * i + u + 1)
                        link(nc.vector.tensor_tensor(xn[:, :, :], xn[:, :, :],
                                                     rstd[:, 1, :].unsqueeze(2).broadcast_to([P, TB, V]), ALU.mult))
                        link(nc.vector.tensor_reduce(part[:, :, :],
                                                     xn[:, :, :].rearrange("p (s q) e -> p q e s", q=2), AX.X, ALU.add))
                        link(nc.vector.tensor_tensor(feat[:, :, :], feat[:, :, :], part[:, :, :], ALU.add))
                        assert n + 4 == per
                dve.sem_inc(sem("feat"), 1)
                dve.wait_ge(sem("colp"), 1)
                step(nc.vector.tensor_copy(col[:, :, :].rearrange("p v q -> p (v q)"), ps[0][:, 0:NV * NPAIR]))
                for k in range(2):
                    step(nc.vector.tensor_scalar(sc[:, k, :], col[:, 5 * k + 4, :], BN_EPS, None, ALU.add))
                dve.sem_inc(sem("bnv"), 1)
                dve.wait_ge(sem("bnr"), 1)
                for k, t in ((0, F.t1), (1, F.t2)):
                    b, g, be, m = (col[:, 5 * k + r, :] for r in range(4))
                    step(nc.vector.tensor_tensor(F.s[:, k, :], sc[:, k, :], g, ALU.mult))
                    step(nc.vector.tensor_tensor(t[:, :], b, m, ALU.subtract))
                    step(nc.vector.tensor_tensor(t[:, :], t[:, :], F.s[:, k, :], ALU.mult))
                    step(nc.vector.tensor_tensor(t[:, :], t[:, :], be, ALU.add))
                step(nc.vector.tensor_scalar(F.nt2[:, :], F.t2[:, :], -1.0, None, ALU.mult))
                for p in range(NPAIR):
                    step(nc.vector.tensor_scalar(dg[:, :], K.ident[:, :], F.s[:, 1, p:p + 1], float(D), ALU.mult, ALU.mult))
                    dve.sem_inc(sem("dg"), 1)
                    dve.wait_ge(sem("s2row"), p + 1)
                    step(nc.vector.tensor_tensor(F.w2[:, p, :], F.w2[:, p, :], ps[1][:, 0:P], ALU.mult))
                    for s in range(2):
                        hf = slice(s * V, (s + 1) * V)
                        step(nc.vector.tensor_copy(b2m[hf, p, 2 * p + s:2 * p + s + 1], F.t2[hf, p:p + 1]))
                dve.sem_inc(sem("b2m"), 1)
                dve.wait_ge(sem("cbp"), 1)
                step(nc.vector.tensor_tensor(cb[:, :], ps[2][0:NE, 0:V], bo[:, :], ALU.add))
                dve.wait_ge(sem("featp"), 1)
                step(nc.vector.tensor_scalar(featT[:, :, :].rearrange("p q n -> p (q n)"), ps[3][0:V, 0:2 * P],
                                             1.0 / SEQ, None, ALU.mult))
                dve.sem_inc(sem("featT"), 1)
                dve.wait_ge(sem("lgp"), 1)
                step(nc.vector.tensor_tensor(lg[:, :, :], ps[4][:, 0:2 * NE].rearrange("p (q e) -> p q e", q=2),
                                             br[:, :].unsqueeze(1).broadcast_to([P, 2, NE]), ALU.add))
                step(nc.vector.tensor_reduce(st[:, 0, :], lg[:, :, :], AX.X, ALU.max))
                step(nc.vector.tensor_tensor(lg[:, :, :], lg[:, :, :],
                                             st[:, 0, :].unsqueeze(2).broadcast_to([P, 2, NE]), ALU.subtract))
                dve.sem_inc(sem("lg"), 1)
                dve.wait_ge(sem("lge"), 1)
                step(nc.vector.tensor_reduce(st[:, 0, :], lg[:, :, :], AX.X, ALU.add))
                step(nc.vector.reciprocal(st[:, 1, :], st[:, 0, :]))
                step(nc.vector.tensor_tensor(gw[:, :, :], lg[:, :, :],
                                             st[:, 1, :].unsqueeze(2).broadcast_to([P, 2, NE]), ALU.mult))
                dve.sem_inc(sem("gw"), 1)
                dve.wait_ge(sem("gwp"), 1)
                for p in range(NPAIR):
                    step(nc.vector.tensor_copy(F.gate[:, p, :, :].rearrange("p q n -> p (q n)"),
                                               ps[5 + p // 2][:, (p % 2) * 256:(p % 2) * 256 + 256]))
                step(nc.vector.tensor_copy(gwT[:, :, :].rearrange("p q n -> p (q n)"), ps[7][0:NE, 0:2 * P]))
                dve.sem_inc(sem("gwT"), 1)
                dve.wait_ge(sem("corrp"), 1)
                step(nc.vector.tensor_copy(F.corr[:, :, :].rearrange("p q n -> p (q n)"), ps[0][:, 0:2 * V]))

            @block.scalar
            def _(act):
                act.wait_ge(sem("lg"), 1)
                nc.scalar.activation(lg[:, :, :], lg[:, :, :], ACT.Exp).then_inc(sem("lge"), 1)

            @block.tensor
            def _(pe):
                pe.wait_ge(sem("loaded"), F.n_loads)
                nc.tensor.transpose(ps[0][:, 0:NV * NPAIR], rows[:, :], K.ident[0:NV * NPAIR, 0:NV * NPAIR]) \
                    .then_inc(sem("colp"), 1)
                for p in range(NPAIR):
                    pe.wait_ge(sem("dg"), p + 1)
                    nc.tensor.matmul(ps[1][:, 0:P], K.onesD[:, :], dg[:, :], start=True, stop=True) \
                        .then_inc(sem("s2row"), 1)
                pe.wait_ge(sem("b2m"), 1)
                for p in range(NPAIR):
                    last = nc.tensor.matmul(ps[2][0:NE, 0:V], b2m[:, p, :], F.wo[:, p, :],
                                            start=p == 0, stop=p == NPAIR - 1)
                last.then_inc(sem("cbp"), 1)
                pe.wait_ge(sem("feat"), 1)
                for q in range(2):
                    last = nc.tensor.transpose(ps[3][0:V, q * P:(q + 1) * P], feat[:, q, :], K.ident[:, :])
                last.then_inc(sem("featp"), 1)
                pe.wait_ge(sem("featT"), 1)
                for q in range(2):
                    last = nc.tensor.matmul(ps[4][:, q * NE:(q + 1) * NE], featT[:, q, :], wr[:, :],
                                            start=True, stop=True)
                last.then_inc(sem("lgp"), 1)
                pe.wait_ge(sem("gw"), 1)
                for q in range(2):
                    for p in range(NPAIR):
                        for s in range(2):
                            c = (p % 2) * 256 + q * P
                            nc.tensor.matmul(ps[5 + p // 2][s * V:(s + 1) * V, c:c + P],
                                             gw[:, q, 2 * p + s:2 * p + s + 1].broadcast_to([P, V]), K.ident[:, :],
                                             start=True, stop=True)
                    last = nc.tensor.transpose(ps[7][0:NE, q * P:(q + 1) * P], gw[:, q, :], K.ident[:, :])
                last.then_inc(sem("gwp"), 1)
                pe.wait_ge(sem("gwT"), 1)
                for q in range(2):
                    last = nc.tensor.matmul(ps[0][:, q * V:(q + 1) * V], gwT[:, q, :], cb[:, :], start=True, stop=True)
                last.then_inc(sem("corrp"), 1)


def ffn0(nc, K, F, h_in, h_out):
    with ExitStack() as ctx:
        def sb(n, shape):
            return [ctx.enter_context(nc.sbuf_tensor(f"f0_{n}{u}", shape, F32)) for u in range(2)]

        sem = Signals(nc, "f0_")
        ctx.callback(sem.close)

        hin, hout, hres = sb("hin", [P, TB, V]), sb("hout", [P, TB, V]), sb("hres", [P, TB, V])
        stat, mv, rstd = sb("stat", [P, TB, 6]), sb("mv", [P, TB, 2]), sb("rstd", [P, 2, TB])
        xn, xT = sb("xn", [P, TB, V]), sb("xT", [P, 512])
        h1, g2 = sb("h1", [P, 2, 512]), sb("g2", [P, 2, 512])
        ps = [ctx.enter_context(nc.psum_tensor(f"f0_ps{b}", [P, 512], F32)) for b in range(8)]
        py, pt = ps[6], ps[7]
        hi_v = h_in.rearrange("(i u t p) e -> i u p t e", p=P, t=TB, u=2)
        ho_v = h_out.rearrange("(i u t p) e -> i u p t e", p=P, t=TB, u=2)
        NIT = NBLK // 2

        def up(i, u):
            return 2 * i + u + 1

        def pair(i, u, p):
            return NPAIR * (2 * i + u) + p + 1

        with nc.Block() as block:
            @block.sync
            def _(sp):
                with sp.Fori(0, NIT) as i:
                    for u in range(2):
                        sp.wait_ge(sem("hin_seen"), up(i, u))
                        sp.wait_ge(sem("hin_kept"), up(i, u))
                        sp.dma_start(hin[u][:, :, :], hi_v[i, u]).then_inc(sem(f"hin{u}"), 16)
                    for u in range(2):
                        sp.wait_ge(sem("hout"), up(i, u))
                        sp.dma_start(ho_v[i, u], hout[u][:, :, :]).then_inc(sem(f"stored{u}"), 16)
                for u in range(2):
                    sp.wait_ge(sem(f"stored{u}"), 16 * (NIT + 1))

            @block.gpsimd
            def _(pool):
                pool.sem_inc(sem("hin_kept"), 2)
                with pool.Fori(0, NIT) as i:
                    for u in range(2):
                        pool.wait_ge(sem("var"), up(i, u))
                        nc.gpsimd.tensor_tensor(rstd[u][:, 1, :], rstd[u][:, 0, :],
                                                K.mhalf[:, 0:1].broadcast_to([P, TB]), ALU.pow) \
                            .then_inc(sem("rstd"), 1)
                    for u in range(2):
                        pool.wait_ge(sem("hres_free"), up(i, u))
                        nc.gpsimd.tensor_tensor(hres[u][:, :, :].rearrange("p (s q) e -> p s (q e)", q=2),
                                                hin[u][:, :, :].rearrange("p (s q) e -> p s (q e)", q=2),
                                                F.corr[:, :, :].rearrange("p q e -> p (q e)").unsqueeze(1)
                                                .broadcast_to([P, TB // 2, 2 * V]), ALU.add) \
                            .then_inc(sem("hin_kept"), 1)

            @block.vector
            def _(dve):
                dve.sem_inc(sem("hin_seen"), 2)
                dve.sem_inc(sem("hres_free"), 2)
                for u in range(2):
                    dve.sem_inc(sem(f"stored{u}"), 16)
                per = 2 * TB + 1 + 2
                with dve.Fori(0, NIT) as i:
                    for u in range(2):
                        k = (2 * i + u) * per
                        dve.wait_ge(sem(f"hin{u}"), 16 * i + 16)
                        n = norm_stats(nc, dve, sem("ln"), k, hin[u], stat[u], mv[u], TB)
                        nc.vector.tensor_scalar(rstd[u][:, 0, :], mv[u][:, :, 1], EPS, None, ALU.add) \
                            .then_inc(sem("var"), 1)
                        link = Chain(dve, sem("ln"), k + n)
                        link(nc.vector.tensor_tensor(xn[u][:, :, :], hin[u][:, :, :],
                                                     mv[u][:, :, 0:1].broadcast_to([P, TB, V]), ALU.subtract))
                        dve.sem_inc(sem("hin_seen"), 1)
                        dve.wait_ge(sem("rstd"), up(i, u))
                        link(nc.vector.tensor_tensor(xn[u][:, :, :], xn[u][:, :, :],
                                                     rstd[u][:, 1, :].unsqueeze(2).broadcast_to([P, TB, V]),
                                                     ALU.mult))
                        dve.sem_inc(sem("xn"), 1)
                    for u in range(2):
                        for p in range(NPAIR):
                            for q in range(2):
                                dve.wait_ge(sem("h2_ps"), 2 * (pair(i, u, p) - 1) + q + 1)
                                nc.vector.scalar_tensor_tensor(
                                    g2[p % 2][:, q, :].rearrange("p (s n) -> p s n", n=P),
                                    ps[4 + q][:, :].rearrange("p (s n) -> p s n", n=P), F.nt2[:, p:p + 1],
                                    F.gate[:, p, q:q + 1, :].broadcast_to([P, TB // 2, P]), ALU.max, ALU.mult) \
                                    .then_inc(sem("g2"), 1)
                        dve.wait_ge(sem("y_ps"), up(i, u))
                        dve.wait_ge(sem("hin_kept"), up(i, u) + 2)
                        dve.wait_ge(sem(f"stored{u}"), 16 * i + 16)
                        nc.vector.tensor_tensor(hout[u][:, :, :].rearrange("p t e -> p (t e)"), py[:, :],
                                                hres[u][:, :, :].rearrange("p t e -> p (t e)"), ALU.add) \
                            .then_inc(sem("hout"), 1)
                        dve.wait_ge(sem("hout"), up(i, u))
                        dve.sem_inc(sem("hres_free"), 1)
                        dve.sem_inc(sem("py_free"), 1)

            @block.scalar
            def _(act):
                with act.Fori(0, NIT) as i:
                    for u in range(2):
                        act.wait_ge(sem("xT_ps"), up(i, u))
                        nc.scalar.copy(xT[u][:, :], pt[:, :]).then_inc(sem("xT"), 1)
                        for p in range(NPAIR):
                            act.wait_ge(sem("h1_ps"), pair(i, u, p))
                            for q in range(2):
                                nc.scalar.activation(h1[p % 2][:, q, :], ps[2 * (p % 2) + q][:, :], ACT.Relu,
                                                     bias=F.t1[:, p:p + 1], scale=F.s[:, 0, p:p + 1]) \
                                    .then_inc(sem("h1"), 1)

            @block.tensor
            def _(pe):
                pe.sem_inc(sem("py_free"), 1)

                def first(i, u, p):
                    for q in range(2):
                        hf = slice(q * V, (q + 1) * V)
                        last = nc.tensor.matmul(ps[2 * (p % 2) + q][:, :],
                                                F.w1[hf, 2 * p:2 * p + 2, :].rearrange("p e h -> p (e h)"),
                                                xT[u][hf, :], start=True, stop=True)
                    last.then_inc(sem("h1_ps"), 1)

                def out(i, u, p):
                    pe.wait_ge(sem("g2"), 2 * pair(i, u, p))
                    if p == 0:
                        pe.wait_ge(sem("py_free"), up(i, u))
                    for t in range(TB):
                        s, q = t // 2, t % 2
                        last = nc.tensor.matmul(py[:, t * V:(t + 1) * V], g2[p % 2][:, q, s * P:(s + 1) * P],
                                                F.wo[:, p, :], start=p == 0 and t == 0, stop=p == NPAIR - 1,
                                                skip_group_check=True)
                    if p == NPAIR - 1:
                        last.then_inc(sem("y_ps"), 1)

                with pe.Fori(0, NIT) as i:
                    for u in range(2):
                        pe.wait_ge(sem("xn"), up(i, u))
                        for s in range(TB // 2):
                            last = nc.tensor.transpose(pt[:, s * P:(s + 1) * P],
                                                       xn[u][:, 2 * s:2 * s + 2, :].rearrange("p q e -> p (q e)"),
                                                       K.ident[:, :])
                        last.then_inc(sem("xT_ps"), 1)
                        pe.wait_ge(sem("xT"), up(i, u))
                        first(i, u, 0)
                        for p in range(NPAIR):
                            if p + 1 < NPAIR:
                                first(i, u, p + 1)
                            if p >= 1:
                                out(i, u, p - 1)
                            for q in range(2):
                                pe.wait_ge(sem("h1"), 2 * (pair(i, u, p) - 1) + q + 1)
                                nc.tensor.matmul(ps[4 + q][:, :], F.w2[:, p, :], h1[p % 2][:, q, :],
                                                 start=True, stop=True).then_inc(sem("h2_ps"), 1)
                        out(i, u, NPAIR - 1)


def ffn1(nc, a, K, h_in, h_out):
    with ExitStack() as ctx:
        def one(n, shape):
            return ctx.enter_context(nc.sbuf_tensor("f1_" + n, shape, F32))

        def sb(n, shape):
            return [one(f"{n}{u}", shape) for u in range(2)]

        sem = Signals(nc, "f1_")
        ctx.callback(sem.close)

        H = P
        w1, w2 = one("w1", [P, NE, H]), one("w2", [H, NE, V])
        b1r, b1 = one("b1r", [NE, H]), one("b1", [H, NE])
        gam, bet = one("gam", [P, 1]), one("bet", [V, 1])
        wr, wrg = one("wr", [P, NE]), one("wrg", [P, 2, NE])
        br = one("br", [P, NE])
        b2bd = one("b2bd", [TB * NE, TB, V])
        lower = one("lower", [P, NE, NE])
        hin, hout = sb("hin", [P, TB, V]), sb("hout", [P, TB, V])
        stat, mv, rstd = sb("stat", [P, TB, 6]), sb("mv", [P, TB, 2]), sb("rstd", [P, 2, TB])
        xn, xT = sb("xn", [P, TB, V]), sb("xT", [P, 512])
        act1 = sb("act1", [H, 2, 512])
        lg = sb("lg", [P, TB, NE])
        gt, eq = one("gt", [P, TB, NE, NE]), one("eq", [P, TB, NE, NE])
        rank, sel = one("rank", [P, TB, NE]), one("sel", [P, 2, TB, NE])
        v12 = sb("v12", [P, 4, TB])
        gate = sb("gate", [P, TB, NE])
        gT = sb("gT", [TB * NE, P])
        term = sb("term", [P, TB, V])
        acc = sb("acc", [P, TB, V])
        ps = [ctx.enter_context(nc.psum_tensor(f"f1_ps{b}", [P, 512], F32)) for b in range(8)]
        pm, pt = ps[6], ps[7]
        hi_v = h_in.rearrange("(i u p t) e -> i u p t e", p=P, t=TB, u=2)
        ho_v = h_out.rearrange("(i u p t) e -> i u p t e", p=P, t=TB, u=2)
        NIT = NBLK // 2
        NL = [0]

        def up(i, u):
            return 2 * i + u + 1

        def ex(i, u, e):
            return NE * (2 * i + u) + e + 1

        with nc.Block() as block:
            @block.sync
            def _(sp):
                sp.wait_ge(sem("zero"), 1)

                def load(dst, src):
                    sp.dma_start(dst, src).then_inc(sem("loaded"), 16)
                    NL[0] += 16
                for q in range(2):
                    hf = slice(q * V, (q + 1) * V)
                    load(w1[hf, :, :], a["L1_ffn_W1"].rearrange("e d h -> d e h"))
                    load(wr[hf, :], a["L1_ffn_Wr"])
                    load(gam[hf, :], a["L1_ffn_gamma"].unsqueeze(1))
                load(bet[:, :], a["L1_ffn_beta"].unsqueeze(1))
                load(w2[:, :, :], a["L1_ffn_W2"].rearrange("e h d -> h e d"))
                load(b1r[:, :], a["L1_ffn_b1"])
                load(br[:, :], a["L1_ffn_br"].partition_broadcast(P))
                for t in range(TB):
                    load(b2bd[t * NE:(t + 1) * NE, t, :], a["L1_ffn_b2"])
                with sp.Fori(0, NIT) as i:
                    for u in range(2):
                        sp.wait_ge(sem("hin_seen"), up(i, u))
                        sp.wait_ge(sem("hin_kept"), up(i, u))
                        sp.dma_start(hin[u][:, :, :], hi_v[i, u]).then_inc(sem(f"hin{u}"), 16)
                    for u in range(2):
                        sp.wait_ge(sem("hout"), up(i, u))
                        sp.dma_start(ho_v[i, u], hout[u][:, :, :]).then_inc(sem(f"stored{u}"), 16)
                for u in range(2):
                    sp.wait_ge(sem(f"stored{u}"), 16 * (NIT + 1))

            @block.gpsimd
            def _(pool):
                pool.sem_inc(sem("hin_kept"), 2)
                pool.sem_inc(sem("acc"), 2)
                with pool.Fori(0, NIT) as i:
                    for u in range(2):
                        pool.wait_ge(sem("var"), up(i, u))
                        nc.gpsimd.tensor_tensor(rstd[u][:, 1, :], rstd[u][:, 0, :],
                                                K.mhalf[:, 0:1].broadcast_to([P, TB]), ALU.pow) \
                            .then_inc(sem("rstd"), 1)
                    for u in range(2):
                        for e in range(NE):
                            pool.wait_ge(sem("term"), ex(i, u, e) + 2)
                            pool.wait_ge(sem("acc"), ex(i, u, e) + 1)
                            if e == 0:
                                pool.wait_ge(sem("acc_free"), up(i, u))
                            nc.gpsimd.tensor_tensor(acc[u][:, :, :], (hin if e == 0 else acc)[u][:, :, :],
                                                    term[e % 2][:, :, :], ALU.add).then_inc(sem("acc"), 1)
                            if e == 0:
                                pool.wait_ge(sem("acc"), ex(i, u, e) + 2)
                                pool.sem_inc(sem("hin_kept"), 1)

            @block.vector
            def _(dve):
                step = Chain(dve, sem("dve"))
                step(nc.vector.memset(b2bd[:, :, :], 0.0))
                step(nc.vector.memset(wrg[:, :, :], 0.0))
                dve.sem_inc(sem("zero"), 1)
                step(nc.vector.memset(lower[:, :, :], 0.0))
                for e in range(1, NE):
                    step(nc.vector.memset(lower[:, e, 0:e], 1.0))
                dve.wait_ge(sem("setp"), 1)
                step(nc.vector.tensor_copy(b1[:, :], ps[0][:, 0:NE]))
                step(nc.vector.tensor_tensor(b1[:, :], b1[:, :], ps[1][:, 0:NE], ALU.add))
                step(nc.vector.tensor_tensor(br[:, :], br[:, :], ps[2][:, 0:NE], ALU.add))
                step(nc.vector.tensor_scalar(w1[:, :, :], w1[:, :, :], gam[:, 0:1], None, ALU.mult))
                for q in range(2):
                    hf = slice(q * V, (q + 1) * V)
                    step(nc.vector.tensor_scalar(wrg[hf, q, :], wr[hf, :], gam[hf, 0:1], None, ALU.mult))
                dve.sem_inc(sem("set"), 1)
                dve.sem_inc(sem("hin_seen"), 2)
                dve.sem_inc(sem("acc_free"), 2)
                dve.sem_inc(sem("term"), 2)
                for u in range(2):
                    dve.sem_inc(sem(f"stored{u}"), 16)
                per = 2 * TB + 1 + 2
                perg = 12
                with dve.Fori(0, NIT) as i:
                    for u in range(2):
                        k = (2 * i + u) * per
                        dve.wait_ge(sem(f"hin{u}"), 16 * i + 16)
                        n = norm_stats(nc, dve, sem("ln"), k, hin[u], stat[u], mv[u], TB)
                        nc.vector.tensor_scalar(rstd[u][:, 0, :], mv[u][:, :, 1], EPS, None, ALU.add) \
                            .then_inc(sem("var"), 1)
                        link = Chain(dve, sem("ln"), k + n)
                        link(nc.vector.tensor_tensor(xn[u][:, :, :], hin[u][:, :, :],
                                                     mv[u][:, :, 0:1].broadcast_to([P, TB, V]), ALU.subtract))
                        dve.sem_inc(sem("hin_seen"), 1)
                        dve.wait_ge(sem("rstd"), up(i, u))
                        link(nc.vector.tensor_tensor(xn[u][:, :, :], xn[u][:, :, :],
                                                     rstd[u][:, 1, :].unsqueeze(2).broadcast_to([P, TB, V]),
                                                     ALU.mult))
                        dve.sem_inc(sem("xn"), 1)
                    for u in range(2):
                        dve.wait_ge(sem("lg_ps"), up(i, u))
                        link = Chain(dve, sem("gate"), (2 * i + u) * perg)
                        l, r0, r1 = lg[u], sel[:, 0, :, :], sel[:, 1, :, :]
                        a4 = l[:, :, :].unsqueeze(2).broadcast_to([P, TB, NE, NE])
                        b4 = l[:, :, :].unsqueeze(3).broadcast_to([P, TB, NE, NE])
                        link(nc.vector.tensor_tensor(l[:, :, :], pt[:, 0:TB * NE].rearrange("p (t e) -> p t e", e=NE),
                                                     br[:, :].unsqueeze(1).broadcast_to([P, TB, NE]), ALU.add))
                        link(nc.vector.tensor_tensor(gt[:, :, :, :], a4, b4, ALU.is_gt))
                        link(nc.vector.tensor_tensor(eq[:, :, :, :], a4, b4, ALU.is_equal))
                        link(nc.vector.tensor_tensor(eq[:, :, :, :], eq[:, :, :, :],
                                                     lower[:, :, :].unsqueeze(1).broadcast_to([P, TB, NE, NE]),
                                                     ALU.mult))
                        link(nc.vector.tensor_tensor(gt[:, :, :, :], gt[:, :, :, :], eq[:, :, :, :], ALU.add))
                        link(nc.vector.tensor_reduce(rank[:, :, :], gt[:, :, :, :], AX.X, ALU.add))
                        for s in range(2):
                            nc.vector.tensor_scalar(sel[:, s, :, :], rank[:, :, :], float(s), None, ALU.is_equal) \
                                .then_inc(sem("gate"), 1)
                            link.n += 1
                        dve.wait_ge(sem("gate"), link.start + link.n)
                        link(nc.vector.tensor_tensor(gt[:, 0:2, :, :].rearrange("p s t e -> p s (t e)"),
                                                     sel[:, :, :, :].rearrange("p s t e -> p s (t e)"),
                                                     l[:, :, :].rearrange("p t e -> p (t e)").unsqueeze(1)
                                                     .broadcast_to([P, 2, TB * NE]), ALU.mult))
                        link(nc.vector.tensor_reduce(v12[u][:, 0:2, :], gt[:, 0:2, :, :], AX.X, ALU.add))
                        nc.vector.tensor_tensor(v12[u][:, 2, :], v12[u][:, 0, :], v12[u][:, 1, :], ALU.subtract) \
                            .then_inc(sem("dv"), 1)
                        dve.wait_ge(sem("th"), up(i, u))
                        for s in range(2):
                            nc.vector.tensor_scalar(v12[u][:, s, :], v12[u][:, 3, :], 0.5 - s, 0.5, ALU.mult, ALU.add) \
                                .then_inc(sem("v12"), 1)
                        dve.wait_ge(sem("v12"), 2 * up(i, u))
                        link(nc.vector.tensor_tensor(sel[:, :, :, :].rearrange("p s t e -> p (s t) e"),
                                                     sel[:, :, :, :].rearrange("p s t e -> p (s t) e"),
                                                     v12[u][:, 0:2, :].rearrange("p s t -> p (s t)").unsqueeze(2)
                                                     .broadcast_to([P, 2 * TB, NE]), ALU.mult))
                        link(nc.vector.tensor_tensor(gate[u][:, :, :], r0, r1, ALU.add))
                        assert link.n == perg, link.n
                        dve.sem_inc(sem("gated"), 1)
                        for e in range(NE):
                            dve.wait_ge(sem("y_ps"), ex(i, u, e))
                            dve.wait_ge(sem("acc"), ex(i, u, e))
                            nc.vector.tensor_tensor(term[e % 2][:, :, :],
                                                    ps[4 + e % 2][:, :].rearrange("p (t d) -> p t d", d=V),
                                                    gate[u][:, :, e:e + 1].broadcast_to([P, TB, V]), ALU.mult) \
                                .then_inc(sem("term"), 1)
                        dve.wait_ge(sem("b2_ps"), up(i, u))
                        dve.wait_ge(sem("acc"), NE * up(i, u) + 2)
                        dve.wait_ge(sem(f"stored{u}"), 16 * i + 16)
                        nc.vector.tensor_tensor(hout[u][:, :, :].rearrange("p t e -> p (t e)"), pm[:, :],
                                                acc[u][:, :, :].rearrange("p t e -> p (t e)"), ALU.add) \
                            .then_inc(sem("hout"), 1)
                        dve.wait_ge(sem("hout"), up(i, u))
                        dve.sem_inc(sem("acc_free"), 1)

            @block.scalar
            def _(act):
                with act.Fori(0, NIT) as i:
                    for u in range(2):
                        act.wait_ge(sem("xT_ps"), up(i, u))
                        nc.scalar.copy(xT[u][:, :], pt[:, :]).then_inc(sem("xT"), 1)
                        for e in range(NE):
                            act.wait_ge(sem("h_ps"), ex(i, u, e))
                            for q in range(2):
                                nc.scalar.activation(act1[e % 2][:, q, :], ps[2 * (e % 2) + q][:, :], ACT.Gelu,
                                                     bias=b1[:, e:e + 1]).then_inc(sem("act1"), 1)
                            if e == 1:
                                act.wait_ge(sem("dv"), up(i, u))
                                nc.scalar.activation(v12[u][:, 3, :], v12[u][:, 2, :], ACT.Tanh, scale=0.5) \
                                    .then_inc(sem("th"), 1)
                            if e == 5:
                                act.wait_ge(sem("gT_ps"), up(i, u))
                                nc.scalar.copy(gT[u][:, :], pm[0:TB * NE, 0:P]).then_inc(sem("gT"), 1)

            @block.tensor
            def _(pe):
                pe.wait_ge(sem("loaded"), NL[0])
                nc.tensor.transpose(ps[0][:, 0:NE], b1r[:, :], K.ident[0:NE, 0:NE])
                for e in range(NE):
                    nc.tensor.matmul(ps[1][:, e:e + 1], w1[0:V, e, :], bet[:, 0:1], start=True, stop=True)
                nc.tensor.matmul(ps[2][:, 0:NE], bet[:, 0:1].broadcast_to([V, P]), wr[0:V, :],
                                 start=True, stop=True).then_inc(sem("setp"), 1)
                pe.wait_ge(sem("set"), 1)

                def first(i, u, e):
                    for q in range(2):
                        hf = slice(q * V, (q + 1) * V)
                        last = nc.tensor.matmul(ps[2 * (e % 2) + q][:, :], w1[hf, e, :], xT[u][hf, :],
                                                start=True, stop=True)
                    last.then_inc(sem("h_ps"), 1)

                with pe.Fori(0, NIT) as i:
                    for u in range(2):
                        pe.wait_ge(sem("xn"), up(i, u))
                        for s in range(TB // 2):
                            last = nc.tensor.transpose(pt[:, s * P:(s + 1) * P],
                                                       xn[u][:, 2 * s:2 * s + 2, :].rearrange("p q e -> p (q e)"),
                                                       K.ident[:, :])
                        last.then_inc(sem("xT_ps"), 1)
                        pe.wait_ge(sem("xT"), up(i, u))
                        for s in range(TB // 2):
                            last = nc.tensor.matmul(pt[:, 2 * s * NE:2 * (s + 1) * NE], xT[u][:, s * P:(s + 1) * P],
                                                    wrg[:, :, :].rearrange("p q e -> p (q e)"), start=True, stop=True)
                        last.then_inc(sem("lg_ps"), 1)
                        first(i, u, 0)
                        for e in range(NE):
                            if e + 1 < NE:
                                first(i, u, e + 1)
                            if e == 4:
                                pe.wait_ge(sem("gated"), up(i, u))
                                wait_alone(pe, sem("acc_free"), up(i, u) + 1, sem("pe_passed"))
                                nc.tensor.transpose(pm[0:TB * NE, 0:P], gate[u][:, :, :].rearrange("p t e -> p (t e)"),
                                                    K.ident[:, :]).then_inc(sem("gT_ps"), 1)
                            if e == 7:
                                pe.wait_ge(sem("gT"), up(i, u))
                                nc.tensor.matmul(pm[:, :], gT[u][:, :], b2bd[:, :, :].rearrange("p t e -> p (t e)"),
                                                 start=True, stop=True).then_inc(sem("b2_ps"), 1)
                            pe.wait_ge(sem("act1"), 2 * ex(i, u, e))
                            pe.wait_ge(sem("term"), ex(i, u, e))
                            for t in range(TB):
                                s, q = t // 2, t % 2
                                last = nc.tensor.matmul(ps[4 + e % 2][:, t * V:(t + 1) * V],
                                                        act1[e % 2][:, q, s * P:(s + 1) * P], w2[:, e, :],
                                                        start=True, stop=True)
                            last.then_inc(sem("y_ps"), 1)


def build(nc, a, out):
    with ExitStack() as ctx:
        K = Consts()
        K.ident = ctx.enter_context(nc.sbuf_tensor("ident", [P, P], F32))
        K.onesD = ctx.enter_context(nc.sbuf_tensor("onesD", [P, P], F32))
        K.eps = ctx.enter_context(nc.sbuf_tensor("eps", [P, 1], F32))
        K.mhalf = ctx.enter_context(nc.sbuf_tensor("mhalf", [P, 1], F32))
        made = ctx.enter_context(nc.semaphore("consts"))
        with nc.Block() as block:
            @block.gpsimd
            def _(pool):
                nc.gpsimd.memset(K.ident[:, :], 0.0).then_inc(made, 1)
                pool.wait_ge(made, 1)
                nc.gpsimd.affine_select(out=K.ident[:, :], in_=K.ident[:, :], compare_op=ALU.not_equal, fill=1.0,
                                        base=0, pattern=[[-1, P]], channel_multiplier=1).then_inc(made, 1)

            @block.vector
            def _(dve):
                nc.vector.memset(K.onesD[:, :], 1.0 / D)
                nc.vector.memset(K.mhalf[:, :], -0.5)
                nc.vector.memset(K.eps[:, :], EPS)
        ext = nc.dram_tensor("ext_table", (HEADS, 2 * P - 1), F32, kind="Internal").ap()
        h0 = nc.dram_tensor("h_tower", (NTOK, V), F32, kind="Internal").ap()
        h1 = nc.dram_tensor("h_attn0", (NTOK, V), F32, kind="Internal").ap()
        h2 = nc.dram_tensor("h_ffn0", (NTOK, V), F32, kind="Internal").ap()
        h3 = nc.dram_tensor("h_attn1", (NTOK, V), F32, kind="Internal").ap()

        def sb(n, shape):
            return ctx.enter_context(nc.sbuf_tensor(n, shape, F32))
        F = Consts()
        F.w1, F.w2, F.wo = sb("f0_w1", [P, NE, V]), sb("f0_w2", [P, NPAIR, P]), sb("f0_wo", [P, NPAIR, V])
        F.s, F.t1, F.t2, F.nt2 = sb("f0_s", [P, 2, NPAIR]), sb("f0_t1", [P, NPAIR]), sb("f0_t2", [P, NPAIR]), \
            sb("f0_nt2", [P, NPAIR])
        F.gate, F.corr = sb("f0_gate", [P, NPAIR, 2, P]), sb("f0_corr", [P, 2, V])
        A0, A1 = attention_weights(nc, a, K, ext, ctx)
        chunk_tower(nc, a, h0, K)
        attention(nc, "a0", K, A0, h0, h1, False)
        ffn0_gate(nc, a, K, F, h1)
        ffn0(nc, K, F, h1, h2)
        attention(nc, "a1", K, A1, h2, h3, True)
        ffn1(nc, a, K, h3, out.rearrange("s l e -> (s l) e"))


def kernel(**inputs):
    import numpy as np
    import concourse.bacc as bacc
    from concourse.bass_utils import run_bass_kernel_spmd as run

    nc = bacc.Bacc("TRN2", target_bir_lowering=False, num_devices=1)
    arrays, args = {}, {}
    for name, x in inputs.items():
        x = np.ascontiguousarray(x)
        arrays["in_" + name] = x
        args[name] = nc.dram_tensor("in_" + name, x.shape, mybir.dt.from_np(x.dtype), kind="ExternalInput").ap()
    out = nc.dram_tensor("h_out", (SEQ, L, V), F32, kind="ExternalOutput").ap()
    build(nc, args, out)
    r = run(nc, [arrays], core_ids=[0])
    return r.results[0]["h_out"]
```

```python
import concourse.bass as bass
from concourse import mybir
from contextlib import ExitStack

F32 = mybir.dt.float32
BF16 = mybir.dt.bfloat16
I32 = mybir.dt.int32
ALU = mybir.AluOpType
ACT = mybir.ActivationFunctionType
AX = mybir.AxisListType

P = 128
V = 64
C = 8
D = 128
NTOK = 16384
SEQ, L = 64, 256
NCH = NTOK // C
CPS = L // C
WIN = 4
NG = NCH // P
KJ = C // 2
EPS = 1e-5


class Signals:

    def __init__(self, nc, prefix):
        self.nc, self.prefix, self.made = nc, prefix, {}

    def __call__(self, name):
        if name not in self.made:
            self.made[name] = self.nc.alloc_semaphore(self.prefix + name)
        return self.made[name]

    def close(self):
        self.nc.clear_and_free_semaphores(list(self.made.values()))
        self.nc.all_engine_barrier()


class Chain:

    def __init__(self, eng, sem, start=0):
        self.eng, self.sem, self.start, self.n = eng, sem, start, 0

    def __call__(self, ins):
        self.n += 1
        ins.then_inc(self.sem, 1)
        self.eng.wait_ge(self.sem, self.start + self.n)


def wait_alone(eng, sem, value, passed):
    eng.wait_ge(sem, value)
    eng.sem_inc(passed, 1)


def bcast(ap, shape):
    return ap.broadcast_to(shape)


def vector_rows(a):
    rows = []

    def whole(name, n=1):
        for r in range(n):
            rows.append((name, r, [(slice(0, P), a[name].rearrange("(r p) -> r p", p=P)[r])]))

    for name, n in (("L0_tok_lln_g", 1), ("L0_tok_lln_b", 1), ("L0_tok_lb1", 2), ("L0_tok_lb2", 1),
                    ("L0_tok_pool_b", 1), ("L0_tok_msg_b1", 1), ("L0_tok_msg_b2", 1), ("L0_tok_upd_b1", 1),
                    ("L0_tok_upd_b2", 1), ("L0_tok_mln_g", 1), ("L0_tok_mln_b", 1), ("L0_tok_bc_b", 1),
                    ("L0_tok_fln_g", 1), ("L0_tok_fln_b", 1)):
        whole(name, n)
    return rows


def chunk_tower(nc, a, h_out, K):
    rows = vector_rows(a)
    col = {(name, r): i for i, (name, r, _) in enumerate(rows)}
    NR = len(rows)
    with ExitStack() as ctx:
        def sb(name, shape, dt=F32):
            return ctx.enter_context(nc.sbuf_tensor(name, shape, dt))

        sem = Signals(nc, "tk_")
        ctx.callback(sem.close)

        ident, onesD = K.ident, K.onesD
        vrow = sb("vrow", [NR, P])
        vcol = sb("vcol", [P, NR])
        emb2 = sb("emb2", [P, D])
        posr = sb("posr", [P, KJ, D])
        lw1 = sb("lw1", [P, 2 * D])
        lw2 = sb("lw2", [P, 2, D])
        poolw = sb("poolw", [P, D])
        mw1 = sb("mw1", [P, 2, D])
        mw2 = sb("mw2", [P, D])
        uw1 = sb("uw1", [P, 2, D])
        uw2 = sb("uw2", [P, D])
        bcw = sb("bcw", [P, D])
        head = sb("head", [P, V])
        xi = sb("xi", [P, NG, C], I32)
        xf = sb("xf", [P, NG, C])
        xT = sb("xT", [P, P])
        vp = sb("vp", [P, 1])
        viota = sb("viota", [P, C, V])
        icnt = sb("icnt", [P, CPS])
        epost = sb("epost", [P, KJ, D])
        exc = sb("exc", [P, KJ, D])
        est = sb("est", [P, 3, KJ])
        exT = sb("exT", [P, KJ * P])
        g1 = sb("g1", [P, 2, KJ * P])
        TT = sb("TT", [P, KJ * P])
        TTc = sb("TTc", [P, KJ * P])
        Tp = sb("Tp", [P, KJ, D])
        Tl = sb("Tl", [P, KJ, 2, V])
        vTs = sb("vTs", [P, KJ, C])
        gh = sb("gh", [P, V])
        wl = sb("wl", [P, V])
        frow = sb("frow", [P, V])
        OH = sb("OH", [P, KJ, NCH])
        mw1t = sb("mw1t", [P, P])
        mw2T = sb("mw2T", [P, D])
        w21 = sb("w21", [P, D])
        bu1 = sb("bu1", [P, 1])
        hm = sb("hm", [P, NCH])
        pb = [ctx.enter_context(nc.psum_tensor(f"tkps{b}", [P, 512], F32)) for b in range(8)]

        def vc(name, r=0):
            c = col[(name, r)]
            return vcol[:, c:c + 1]

        NLOAD = 0
        with nc.Block() as block:
            @block.sync
            def _(sp):
                ld = sem("loaded")
                sp.wait_ge(sem("vrow0"), 1)
                n = 0

                def load(dst, src):
                    nonlocal n
                    sp.dma_start(dst, src).then_inc(ld, 16)
                    n += 1
                for j in range(2):
                    load(emb2[j * V:(j + 1) * V, :], a["L0_tok_emb"])
                    load(posr[j * V:(j + 1) * V, :, :],
                         a["L0_tok_pos"].rearrange("(k j) d -> j k d", j=2)[j].partition_broadcast(V))
                for i, (name, r, parts) in enumerate(rows):
                    for s, src in parts:
                        load(vrow[i:i + 1, s], src.unsqueeze(0))
                load(lw1[:, :], a["L0_tok_lw1"])
                load(lw2[:, :, :], a["L0_tok_lw2"].rearrange("(k p) n -> p k n", p=P))
                load(poolw[:, :], a["L0_tok_pool_w"])
                load(mw1[:, :, :], a["L0_tok_msg_w1"].rearrange("(k p) n -> p k n", p=P))
                load(mw2[:, :], a["L0_tok_msg_w2"])
                load(uw1[:, :, :], a["L0_tok_upd_w1"].rearrange("(k p) n -> p k n", p=P))
                load(uw2[:, :], a["L0_tok_upd_w2"])
                load(bcw[:, :], a["L0_tok_bc_w"])
                load(head[:, :], a["L0_tok_head_w"])
                load(xi[:, :, :], a["x"].rearrange("s l -> (s l)").rearrange("(g n c) -> n g c", n=P, c=C))
                assert n == 5 + NR + 9, n
            NLOAD = 16 * (5 + NR + 9)

            @block.gpsimd
            def _(pool):
                pool.iota(viota[:, :, :], pattern=[[0, C], [1, V]], base=0, channel_multiplier=0,
                          allow_small_or_imprecise_dtypes=True).then_inc(sem("iota"), 1)
                for j in range(2):
                    pool.wait_ge(sem("iota"), j + 1)
                    pool.iota(vp[j * V:(j + 1) * V, :], pattern=[[0, 1]], base=0, channel_multiplier=1,
                              allow_small_or_imprecise_dtypes=True).then_inc(sem("iota"), 1)
                pool.wait_ge(sem("iota"), 3)
                pool.wait_ge(sem("evar"), 1)
                nc.gpsimd.tensor_tensor(est[:, 2, :], est[:, 1, :], K.mhalf[:, 0:1].broadcast_to([P, KJ]), ALU.pow) \
                    .then_inc(sem("erstd"), 1)

            @block.vector
            def _(dve):
                step = Chain(dve, sem("dve"))
                step(nc.vector.memset(vrow[:, :], 0.0))
                dve.sem_inc(sem("vrow0"), 1)
                for i in range(CPS):
                    nc.vector.memset(icnt[:, i:i + 1] if i < WIN else icnt[:, i:], 1.0 / min(i + 1, WIN + 1)) \
                        .then_inc(sem("icnt"), 1)
                    if i == WIN:
                        break
                step(nc.vector.memset(Tl[:, :, :, :], 0.0))
                step(nc.vector.memset(vTs[:, :, :], 0.0))
                dve.wait_ge(sem("vcolp"), 1)
                step(nc.vector.tensor_copy(vcol[:, :], pb[0][:, 0:NR]))
                dve.sem_inc(sem("vcol"), 1)
                step(nc.vector.tensor_tensor(epost[:, :, :], posr[:, :, :],
                                             emb2[:, :].unsqueeze(1).broadcast_to([P, KJ, D]), ALU.add))
                dve.sem_inc(sem("epos"), 1)
                step(nc.vector.tensor_reduce(est[:, 0, :], epost[:, :, :], AX.X, ALU.add))
                step(nc.vector.tensor_scalar(est[:, 1, :], est[:, 0, :], 1.0 / D, None, ALU.mult))
                step(nc.vector.tensor_tensor(exc[:, :, :], epost[:, :, :],
                                             est[:, 1, :].unsqueeze(2).broadcast_to([P, KJ, D]), ALU.subtract))
                step(nc.vector.tensor_tensor(g1[:, 0, :].rearrange("p (k d) -> p k d", k=KJ), exc[:, :, :],
                                             exc[:, :, :], ALU.mult))
                step(nc.vector.tensor_reduce(est[:, 0, :], g1[:, 0, :].rearrange("p (k d) -> p k d", k=KJ),
                                             AX.X, ALU.add))
                step(nc.vector.tensor_scalar(est[:, 1, :], est[:, 0, :], 1.0 / D, EPS, ALU.mult, ALU.add))
                dve.sem_inc(sem("evar"), 1)
                dve.wait_ge(sem("erstd"), 1)
                step(nc.vector.tensor_tensor(exc[:, :, :], exc[:, :, :],
                                             est[:, 2, :].unsqueeze(2).broadcast_to([P, KJ, D]), ALU.mult))
                dve.sem_inc(sem("exn"), 1)
                dve.wait_ge(sem("exTp"), 1)
                step(nc.vector.tensor_scalar(exT[:, :], pb[1][:, :], vc("L0_tok_lln_g"), vc("L0_tok_lln_b"),
                                             ALU.mult, ALU.add))
                dve.sem_inc(sem("exT"), 1)
                dve.wait_ge(sem("eTp"), 1)
                step(nc.vector.tensor_scalar(TT[:, :], pb[2][:, :], vc("L0_tok_lb2"), None, ALU.add))
                step(nc.vector.tensor_scalar(gh[:, :], head[:, :], vc("L0_tok_fln_g"), None, ALU.mult))
                dve.sem_inc(sem("gh"), 1)
                dve.wait_ge(sem("ghm"), 1)
                step(nc.vector.tensor_tensor(wl[:, :], gh[:, :], pb[3][:, 0:V], ALU.subtract))
                step(nc.vector.tensor_copy(frow[:, :], pb[3][:, V:2 * V]))
                step(nc.vector.tensor_copy(mw2T[:, :], pb[4][:, 0:D]))
                dve.sem_inc(sem("mw2T"), 1)
                dve.wait_ge(sem("w21p"), 1)
                step(nc.vector.tensor_copy(w21[:, :], pb[7][:, 0:D]))
                step(nc.vector.tensor_tensor(bu1[:, :], pb[7][:, D:D + 1], vc("L0_tok_upd_b1"), ALU.add))
                dve.wait_ge(sem("tlp"), 1)
                step(nc.vector.tensor_tensor(TT[:, :], TT[:, :], pb[5][:, :], ALU.add))
                dve.sem_inc(sem("TT"), 1)
                dve.wait_ge(sem("TTm"), 1)
                step(nc.vector.tensor_tensor(TTc[:, :], TT[:, :], pb[6][:, :], ALU.subtract))
                step(nc.vector.tensor_tensor(g1[:, 0, :], TTc[:, :], TTc[:, :], ALU.mult))
                dve.sem_inc(sem("TTq"), 1)
                dve.wait_ge(sem("tabs"), 1)
                step(nc.vector.tensor_copy(Tp[:, :, :].rearrange("p k d -> p (k d)"), pb[1][:, :]))
                for j in range(2):
                    hf = slice(j * V, (j + 1) * V)
                    step(nc.vector.tensor_copy(Tl[hf, :, j, :],
                                               pb[2][hf, 0:KJ * V].rearrange("p (k e) -> p k e", k=KJ)))
                    for k in range(KJ):
                        step(nc.vector.tensor_copy(vTs[hf, k, 2 * k + j:2 * k + j + 1], pb[3][hf, k:k + 1]))
                dve.sem_inc(sem("tabsb"), 1)
                step(nc.vector.tensor_copy(xf[:, :, :], xi[:, :, :]))
                dve.sem_inc(sem("xf"), 1)
                dve.wait_ge(sem("xTp"), 1)
                step(nc.vector.tensor_copy(xT[:, :], pb[0][:, 0:P]))
                dve.sem_inc(sem("xT"), 1)
                dve.wait_ge(sem("iota"), 3)
                for g in range(NG):
                    dve.wait_ge(sem("xb"), g + 1)
                    nc.vector.tensor_scalar(OH[:, :, g * P:(g + 1) * P],
                                            pb[4 + g % 4][:, :].rearrange("p (k n) -> p k n", k=KJ),
                                            vp[:, 0:1], None, ALU.is_equal).then_inc(sem("oh"), 1)
                for b in range(4):
                    dve.wait_ge(sem("summ"), b + 1)
                    nc.vector.tensor_scalar(hm[:, b * 512:(b + 1) * 512], pb[b][:, :], 1.0 / C,
                                            vc("L0_tok_pool_b"), ALU.mult, ALU.add).then_inc(sem("hm"), 1)

            @block.scalar
            def _(act):
                for c in range(2):
                    act.wait_ge(sem("g1p"), c + 1)
                    nc.scalar.activation(g1[:, c, :], pb[6 + c][:, :], ACT.Gelu, bias=vc("L0_tok_lb1", c)) \
                        .then_inc(sem("g1"), 1)

            @block.tensor
            def _(pe):
                pe.wait_ge(sem("loaded"), NLOAD)
                nc.tensor.transpose(pb[0][:, 0:NR], vrow[:, :], ident[0:NR, 0:NR]).then_inc(sem("vcolp"), 1)
                pe.wait_ge(sem("exn"), 1)
                for k in range(KJ):
                    nc.tensor.transpose(pb[2][:, k * P:(k + 1) * P], epost[:, k, :], ident[:, :])
                    last = nc.tensor.transpose(pb[1][:, k * P:(k + 1) * P], exc[:, k, :], ident[:, :])
                last.then_inc(sem("exTp"), 1)
                pe.sem_inc(sem("eTp"), 1)
                pe.wait_ge(sem("exT"), 1)
                for c in range(2):
                    nc.tensor.matmul(pb[6 + c][:, :], lw1[:, c * D:(c + 1) * D], exT[:, :],
                                     start=True, stop=True).then_inc(sem("g1p"), 1)
                pe.wait_ge(sem("gh"), 1)
                nc.tensor.matmul(pb[3][:, 0:V], onesD[:, :], gh[:, :], start=True, stop=True)
                nc.tensor.matmul(pb[3][:, V:2 * V], bcast(vc("L0_tok_fln_b"), [P, P]), head[:, :],
                                 start=True, stop=True)
                nc.tensor.transpose(pb[4][:, 0:D], mw2[:, :], ident[:, :]).then_inc(sem("ghm"), 1)
                for c in range(2):
                    pe.wait_ge(sem("g1"), c + 1)
                    last = nc.tensor.matmul(pb[5][:, :], lw2[:, c, :], g1[:, c, :], start=c == 0, stop=c == 1)
                last.then_inc(sem("tlp"), 1)
                pe.wait_ge(sem("mw2T"), 1)
                nc.tensor.matmul(pb[7][:, 0:D], mw2T[:, :], uw1[:, 1, :], start=True, stop=True)
                nc.tensor.matmul(pb[7][:, D:D + 1], uw1[:, 1, :], vc("L0_tok_msg_b2"),
                                 start=True, stop=True).then_inc(sem("w21p"), 1)
                pe.wait_ge(sem("TT"), 1)
                nc.tensor.matmul(pb[6][:, :], onesD[:, :], TT[:, :], start=True, stop=True).then_inc(sem("TTm"), 1)
                pe.wait_ge(sem("TTq"), 1)
                for k in range(KJ):
                    sl = TT[:, k * P:(k + 1) * P]
                    nc.tensor.matmul(pb[1][:, k * D:(k + 1) * D], sl, poolw[:, :], start=True, stop=True)
                    nc.tensor.matmul(pb[2][:, k * V:(k + 1) * V], sl, wl[:, :], start=True, stop=True)
                    last = nc.tensor.matmul(pb[3][:, k:k + 1], g1[:, 0, k * P:(k + 1) * P], onesD[:, 0:1],
                                            start=True, stop=True)
                last.then_inc(sem("tabs"), 1)
                pe.wait_ge(sem("xf"), 1)
                nc.tensor.transpose(pb[0][:, 0:P], xf[:, :, :].rearrange("p g c -> p (g c)"), ident[:, :]) \
                    .then_inc(sem("xTp"), 1)
                pe.wait_ge(sem("xT"), 1)
                for g in range(NG):
                    if g >= 4:
                        pe.wait_ge(sem("oh"), g - 3)
                    for k in range(KJ):
                        for j in range(2):
                            r = g * C + 2 * k + j
                            last = nc.tensor.matmul(pb[4 + g % 4][j * V:(j + 1) * V, k * P:(k + 1) * P],
                                                    ident[:, r:r + 1].broadcast_to([P, V]), xT[:, :],
                                                    start=True, stop=True)
                    last.then_inc(sem("xb"), 1)
                pe.wait_ge(sem("oh"), NG)
                pe.wait_ge(sem("tabsb"), 1)
                for b in range(4):
                    for k in range(KJ):
                        last = nc.tensor.matmul(pb[b][:, :], Tp[:, k, :], OH[:, k, b * 512:(b + 1) * 512],
                                                start=k == 0, stop=k == KJ - 1)
                    last.then_inc(sem("summ"), 1)
        tower_rounds(nc, sem, pb, K, icnt, vc, mw1, w21, uw1, uw2, bu1, hm, sb)
        tower_logits(nc, sem, pb, K, vc, bcw, TTc, wl, OH, Tl, vTs, frow, hm, xf, viota, h_out, sb)


def tower_rounds(nc, sem, pb, K, icnt, vc, mw1, w21, uw1, uw2, bu1, hm, sb):
    NB, W = 4, NCH // 4
    SB = W // CPS
    selfp = [sb(f"selfp{i}", [P, W]) for i in range(4)]
    gel = [sb(f"gel{i}", [P, WIN + 1, W]) for i in range(2)]
    agg = [sb(f"agg{i}", [P, W]) for i in range(2)]
    ug = [sb(f"ug{i}", [P, W]) for i in range(4)]
    res = [sb(f"res{i}", [P, W]) for i in range(4)]
    sq = [sb(f"sqr{i}", [P, W]) for i in range(4)]
    blk = [slice(b * W, (b + 1) * W) for b in range(NB)]

    def seqs(ap):
        return ap.rearrange("p (s c) -> p s c", c=CPS)

    with nc.Block() as block:
        @block.tensor
        def _(pe):
            with pe.Fori(0, 3) as r:
                at = lambda b: r * NB + b + 1
                for b in range(NB):
                    pe.wait_ge(sem("hm"), at(b))
                    nc.tensor.matmul(pb[2 * b][:, :], mw1[:, 0, :], hm[:, blk[b]], start=True, stop=True)
                    nc.tensor.matmul(pb[2 * b + 1][:, :], mw1[:, 1, :], hm[:, blk[b]], start=True, stop=True) \
                        .then_inc(sem("msgp"), 1)
                for b in range(NB):
                    pe.wait_ge(sem("added"), at(b))
                    nc.tensor.matmul(pb[2 * b][:, :], uw1[:, 0, :], hm[:, blk[b]], start=True, stop=False)
                    pe.wait_ge(sem("agg"), at(b))
                    nc.tensor.matmul(pb[2 * b][:, :], w21[:, :], agg[b % 2][:, :], start=False, stop=True) \
                        .then_inc(sem("updp"), 1)
                for b in range(NB):
                    pe.wait_ge(sem("ug"), at(b))
                    nc.tensor.matmul(pb[2 * b + 1][:, :], uw2[:, :], ug[b][:, :], start=True, stop=True) \
                        .then_inc(sem("upd2p"), 1)
                for b in range(NB):
                    pe.wait_ge(sem("res"), at(b))
                    nc.tensor.matmul(pb[2 * b][:, :], K.onesD[:, :], res[b][:, :], start=True, stop=True) \
                        .then_inc(sem("meanp"), 1)
                for b in range(NB):
                    pe.wait_ge(sem("sq"), at(b))
                    nc.tensor.matmul(pb[2 * b + 1][:, :], K.onesD[:, :], sq[b][:, :], start=True, stop=True) \
                        .then_inc(sem("varp"), 1)

        @block.scalar
        def _(act):
            with act.Fori(0, 3) as r:
                at = lambda b: r * NB + b + 1
                for b in range(NB):
                    act.wait_ge(sem("msgp"), at(b))
                    nc.scalar.activation(selfp[b][:, :], pb[2 * b][:, :], ACT.Identity,
                                         bias=vc("L0_tok_msg_b1")).then_inc(sem("selfp"), 1)
                for b in range(NB):
                    act.wait_ge(sem("added"), at(b))
                    nc.scalar.activation(gel[b % 2][:, :, :], gel[b % 2][:, :, :], ACT.Gelu) \
                        .then_inc(sem("gel"), 1)
                for b in range(NB):
                    act.wait_ge(sem("updp"), at(b))
                    nc.scalar.activation(ug[b][:, :], pb[2 * b][:, :], ACT.Gelu, bias=bu1[:, 0:1]) \
                        .then_inc(sem("ug"), 1)
                for b in range(NB):
                    act.wait_ge(sem("resc"), at(b))
                    nc.scalar.activation(sq[b][:, :], res[b][:, :], ACT.Square).then_inc(sem("sq"), 1)
                for b in range(NB):
                    act.wait_ge(sem("varp"), at(b))
                    nc.scalar.activation(sq[b][:, :], pb[2 * b + 1][:, :], ACT.Sqrt, bias=K.eps[:, 0:1]) \
                        .then_inc(sem("std"), 1)

        @block.gpsimd
        def _(pool):
            step = None
            with pool.Fori(0, 3) as r:
                at = lambda b: r * NB + b + 1
                step = Chain(pool, sem("poolc"), r * (NB * WIN))
                for b in range(NB):
                    pool.wait_ge(sem("gel"), at(b))
                    g = gel[b % 2]
                    for d in range(1, WIN + 1):
                        step(nc.gpsimd.tensor_tensor(seqs(g[:, 0, :])[:, :, d:], seqs(g[:, 0, :])[:, :, d:],
                                                     seqs(g[:, d, :])[:, :, d:], ALU.add))
                    pool.wait_ge(sem("updp0"), at(b))
                    nc.gpsimd.tensor_tensor(seqs(agg[b % 2][:, :]), seqs(g[:, 0, :]),
                                            icnt[:, :].unsqueeze(1).broadcast_to([P, SB, CPS]), ALU.mult) \
                        .then_inc(sem("agg"), 1)

        @block.vector
        def _(dve):
            for g in gel:
                nc.vector.memset(g[:, :, :], 0.0).then_inc(sem("gel0"), 1)
            dve.wait_ge(sem("gel0"), 2)
            with dve.Fori(0, 3) as r:
                at = lambda b: r * NB + b + 1
                for b in range(NB):
                    dve.wait_ge(sem("selfp"), at(b))
                    if b >= 2:
                        dve.wait_ge(sem("agg"), at(b - 2))
                    g = gel[b % 2]
                    for d in range(WIN + 1):
                        last = nc.vector.tensor_tensor(seqs(g[:, d, :])[:, :, d:], seqs(selfp[b][:, :])[:, :, d:],
                                                       seqs(pb[2 * b + 1][:, :])[:, :, 0:CPS - d], ALU.add)
                    last.then_inc(sem("added"), 1)
                for b in range(NB):
                    dve.wait_ge(sem("upd2p"), at(b))
                    nc.vector.scalar_tensor_tensor(res[b][:, :], pb[2 * b + 1][:, :], vc("L0_tok_upd_b2"),
                                                   hm[:, blk[b]], ALU.add, ALU.add).then_inc(sem("res"), 1)
                for b in range(NB):
                    dve.wait_ge(sem("meanp"), at(b))
                    nc.vector.tensor_tensor(res[b][:, :], res[b][:, :], pb[2 * b][:, :], ALU.subtract) \
                        .then_inc(sem("resc"), 1)
                for b in range(NB):
                    dve.wait_ge(sem("std"), at(b))
                    nc.vector.reciprocal(sq[b][:, :], sq[b][:, :]).then_inc(sem("rs"), 1)
                for b in range(NB):
                    dve.wait_ge(sem("rs"), at(b))
                    nc.vector.tensor_tensor(res[b][:, :], res[b][:, :], sq[b][:, :], ALU.mult) \
                        .then_inc(sem("rn"), 1)
                    dve.wait_ge(sem("rn"), at(b))
                    nc.vector.tensor_scalar(hm[:, blk[b]], res[b][:, :], vc("L0_tok_mln_g"), vc("L0_tok_mln_b"),
                                            ALU.mult, ALU.add).then_inc(sem("hm"), 1)

        @block.sync
        def _(sp):
            sp.sem_inc(sem("updp0"), 2)
            for k in range(3 * NB - 2):
                sp.wait_ge(sem("updp"), k + 1)
                sp.sem_inc(sem("updp0"), 1)


def tower_logits(nc, sem, pb, K, vc, bcw, TTc, wl, OH, Tl, vTs, frow, hm, xf, viota, h_out, sb):
    NB, W = 4, NCH // 4
    bct = sb("bct", [P, NCH])
    bcq = sb("bcq", [P, NCH])
    oh = [sb(f"ohn{i}", [P, C, V]) for i in range(2)]
    cov = [sb(f"cov{i}", [P, C, V]) for i in range(2)]
    st = [sb(f"lst{i}", [P, 3, C]) for i in range(2)]
    lg = [sb(f"lg{i}", [P, C, V]) for i in range(2)]
    h_v = h_out.rearrange("(g n c) e -> g n (c e)", n=P, c=C)
    with nc.Block() as block:
        @block.tensor
        def _(pe):
            for b in range(NB):
                nc.tensor.matmul(pb[b][:, :], bcw[:, :], hm[:, b * W:(b + 1) * W],
                                 start=True, stop=True).then_inc(sem("bcp"), 1)
            for b in range(NB):
                pe.wait_ge(sem("bct"), b + 1)
                nc.tensor.matmul(pb[4 + b][:, :], K.onesD[:, :], bct[:, b * W:(b + 1) * W],
                                 start=True, stop=True).then_inc(sem("bcm"), 1)
            pe.wait_ge(sem("bcq"), 4)
            for g in range(NG):
                u, n = g % 2, slice(g * P, (g + 1) * P)
                pc, pl, pv = pb[u], pb[2 + u], pb[4 + u]
                if g >= 2:
                    pe.wait_ge(sem("lg"), g - 1)
                nc.tensor.matmul(pv[:, 0:C], bcq[:, n], bcast(K.onesD[:, 0:1], [P, C]), start=True, stop=False)
                nc.tensor.matmul(pl[:, :].rearrange("p (c e) -> p c e", c=C), bct[:, n],
                                 wl[:, :].unsqueeze(1).broadcast_to([P, C, V]), start=True, stop=False)
                nc.tensor.matmul(pc[:, :], bct[:, n], TTc[:, :], start=True, stop=True)
                for k in range(KJ):
                    nc.tensor.matmul(pv[:, 0:C], OH[:, k, n], vTs[:, k, :], start=False, stop=k == KJ - 1)
                    last = nc.tensor.matmul(pl[:, k * P:(k + 1) * P], OH[:, k, n],
                                            Tl[:, k, :, :].rearrange("p j e -> p (j e)"),
                                            start=False, stop=k == KJ - 1)
                last.then_inc(sem("lgp"), 1)

        @block.scalar
        def _(act):
            for b in range(NB):
                act.wait_ge(sem("bcp"), b + 1)
                nc.scalar.activation(bct[:, b * W:(b + 1) * W], pb[b][:, :], ACT.Identity,
                                     bias=vc("L0_tok_bc_b")).then_inc(sem("bct"), 1)
            for b in range(NB):
                act.wait_ge(sem("bcc"), b + 1)
                nc.scalar.activation(bcq[:, b * W:(b + 1) * W], bct[:, b * W:(b + 1) * W], ACT.Square) \
                    .then_inc(sem("bcq"), 1)

        @block.gpsimd
        def _(pool):
            for g in range(NG):
                st_ = st[g % 2]
                pool.wait_ge(sem("lvar"), g + 1)
                nc.gpsimd.tensor_tensor(st_[:, 2, :], st_[:, 1, :], K.mhalf[:, 0:1].broadcast_to([P, C]), ALU.pow) \
                    .then_inc(sem("lrstd"), 1)

        @block.vector
        def _(dve):
            for b in range(NB):
                dve.wait_ge(sem("bcm"), b + 1)
                nc.vector.tensor_tensor(bct[:, b * W:(b + 1) * W], bct[:, b * W:(b + 1) * W], pb[4 + b][:, :],
                                        ALU.subtract).then_inc(sem("bcc"), 1)
            step = Chain(dve, sem("ldve"))
            for g in range(NG):
                u = g % 2
                step(nc.vector.tensor_tensor(oh[u][:, :, :], viota[:, :, :],
                                             xf[:, g, :].unsqueeze(2).broadcast_to([P, C, V]), ALU.is_equal))
                dve.wait_ge(sem("lgp"), g + 1)
                nc.vector.tensor_tensor(cov[u][:, :, :], oh[u][:, :, :],
                                        pb[u][:, :].rearrange("p (c e) -> p c e", c=C), ALU.mult) \
                    .then_inc(sem("covm"), 1)
                dve.wait_ge(sem("covm"), g + 1)
                step(nc.vector.tensor_reduce(st[u][:, 0, :], cov[u][:, :, :], AX.X, ALU.add))
                step(nc.vector.scalar_tensor_tensor(st[u][:, 1, :], st[u][:, 0, :], 2.0 / D, pb[4 + u][:, 0:C],
                                                    ALU.mult, ALU.add))
                nc.vector.tensor_scalar(st[u][:, 1, :], st[u][:, 1, :], EPS, None, ALU.add).then_inc(sem("lvar"), 1)
                dve.wait_ge(sem("lrstd"), g + 1)
                if g >= 2:
                    dve.wait_ge(sem(f"lstored{u}"), 16 * (g // 2))
                step(nc.vector.tensor_tensor(lg[u][:, :, :], pb[2 + u][:, :].rearrange("p (c e) -> p c e", c=C),
                                             st[u][:, 2, :].unsqueeze(2).broadcast_to([P, C, V]), ALU.mult))
                nc.vector.tensor_tensor(lg[u][:, :, :], lg[u][:, :, :],
                                        frow[:, :].unsqueeze(1).broadcast_to([P, C, V]), ALU.add) \
                    .then_inc(sem("lg"), 1)

        @block.sync
        def _(sp):
            for g in range(NG):
                sp.wait_ge(sem("lg"), g + 1)
                sp.dma_start(h_v[g], lg[g % 2][:, :, :].rearrange("p c e -> p (c e)")) \
                    .then_inc(sem(f"lstored{g % 2}"), 16)
            for u in range(2):
                sp.wait_ge(sem(f"lstored{u}"), 16 * (NG // 2))


HEADS, HD = 8, 8
NJ = 4
NGRP = HEADS // NJ
Q_SCALE = HD ** -0.5
NPP = HEADS // 2
SLOTS = ((0, 0), (0, 1), (1, 0), (1, 1), (0, 2), (2, 0))
OFF = 8


def attention(nc, name, K, A, h_in, h_out, wide):
    T = 2 if wide else 4
    NT = T * P
    NIT = NTOK // NT // 2
    W = 64
    with ExitStack() as ctx:
        def sb(n, shape, dt=F32):
            return [ctx.enter_context(nc.sbuf_tensor(f"{name}_{n}{u}", shape, dt)) for u in range(2)]

        sem = Signals(nc, name + "_")
        ctx.callback(sem.close)

        hin = sb("hin", [P, T, V])
        stat = sb("stat", [P, T, 6])
        mv = sb("mv", [P, T, 2])
        rstd = sb("rstd", [P, 2, T])
        xn = sb("xn", [P, T, V])
        xT = sb("xT", [P, T // 2, P])
        parts = sb("parts", [P, 3, NT], BF16)
        rest = sb("rest", [P, NT])
        qst = sb("qst", [P, NPP, NT], BF16)
        kst = sb("kst", [P, HEADS if wide else NPP, NT], BF16)
        va = sb("va", [P, T, HEADS, 32])
        mx = sb("mx", [P, T, HEADS])
        mrest = sb("mrest", [P, T, HEADS])
        m3 = sb("m3", [P, T, 2, 3, NPP], BF16)
        mT = sb("mT", [3 * HEADS, NT], BF16)
        if wide:
            pr = sb("pr", [P, 2, HEADS, NT])
        else:
            pr = sb("pr", [P, HEADS, T, W])
        oT = sb("oT", [P, NGRP, NT])
        rs = sb("rs", [P, T * NGRP, NJ])
        on = sb("on", [P, T, V])
        onT = sb("onT", [P, T // 2, P])
        hres = sb("hres", [P, T, V])
        hout = sb("hout", [P, T, V])
        quad = [ctx.enter_context(nc.psum_tensor(f"{name}_quad{u}", [P, 4, 512], F32)) for u in range(2)]
        flat = [q[:, :, :].rearrange("p b n -> p (b n)") for q in quad]
        hi_v = h_in.rearrange("(i u t p) e -> i u p t e", p=P, t=T, u=2)
        ho_v = h_out.rearrange("(i u t p) e -> i u p t e", p=P, t=T, u=2)
        NS = 2 if wide else 1
        vbase = 512
        obase = 512 if wide else 1024
        halves = [slice(64 * q, 64 * q + 64) for q in range(2)]

        def up(i, u):
            return 2 * i + u + 1

        def score_mms(u, p, stat_, mov):
            if wide:
                for h in range(HEADS):
                    s_ = stat_[u][:, h if stat_ is kst else h % NPP, p * P:(p + 1) * P]
                    last = nc.tensor.matmul(flat[u][:, h * NT:(h + 1) * NT], s_,
                                            mov[u][:, h if mov is kst else h % NPP, :], start=True, stop=True)
                return last
            for pp in range(NPP):
                for t in range(T):
                    for par in range(2):
                        w = slice(t * P + par * W, t * P + (par + 1) * W)
                        for q in range(2):
                            c = ((q * NPP + pp) * T + t) * W
                            last = nc.tensor.matmul(flat[u][par * W:(par + 1) * W, c:c + W],
                                                    stat_[u][halves[q], pp, w], mov[u][halves[q], pp, w],
                                                    start=True, stop=True, tile_position=(64 * q, par * W))
            return last

        with nc.Block() as block:
            @block.sync
            def _(sp):
                with sp.Fori(0, NIT) as i:
                    for u in range(2):
                        sp.wait_ge(sem("mT"), up(i, u))
                        for q in range(2):
                            sp.dma_start(qst[u][64 * q:64 * q + 3, :, :], mT[u][q * 3 * NPP:(q + 1) * 3 * NPP, :]) \
                                .then_inc(sem(f"max{u}"), 16)
                    for u in range(2):
                        sp.wait_ge(sem("hout"), up(i, u))
                        sp.dma_start(ho_v[i, u], hout[u][:, :, :]).then_inc(sem(f"stored{u}"), 16)
                for u in range(2):
                    sp.wait_ge(sem(f"stored{u}"), 16 * (NIT + 1))

            @block.gpsimd
            def _(pool):
                if wide:
                    for u in range(2):
                        nc.gpsimd.memset(kst[u][:, :, :], 0.0).then_inc(sem("kst0"), 1)
                pool.sem_inc(sem("hin_kept"), 2)
                with pool.Fori(0, NIT) as i:
                    for u in range(2):
                        pool.wait_ge(sem("hin_seen"), up(i, u))
                        pool.wait_ge(sem("hin_kept"), up(i, u))
                        pool.dma_start(hin[u][:, :, :], hi_v[i, u]).then_inc(sem(f"hin{u}"), 16)
                    for u in range(2):
                        pool.wait_ge(sem("var"), up(i, u))
                        nc.gpsimd.tensor_tensor(rstd[u][:, 1, :], rstd[u][:, 0, :],
                                                K.mhalf[:, 0:1].broadcast_to([P, T]), ALU.pow) \
                            .then_inc(sem("rstd"), 1)
                    for u in range(2):
                        pool.wait_ge(sem("hres_free"), up(i, u))
                        nc.gpsimd.tensor_tensor(hres[u][:, :, :], hin[u][:, :, :],
                                                A.brow[:, :].unsqueeze(1).broadcast_to([P, T, V]), ALU.add) \
                            .then_inc(sem("hin_kept"), 1)

            @block.vector
            def _(dve):
                for u in range(2):
                    nc.vector.memset(va[u][:, :, :, :], 0.0).then_inc(sem("pad"), 1)
                dve.wait_ge(sem("pad"), 2)
                for u in range(2):
                    nc.vector.memset(va[u][:, :, :, 0:1], 1.0).then_inc(sem("pad"), 1)
                dve.wait_ge(sem("pad"), 4)
                dve.sem_inc(sem("hin_seen"), 2)
                dve.sem_inc(sem("hres_free"), 2)
                dve.sem_inc(sem("quad_free"), 2)
                for u in range(2):
                    dve.sem_inc(sem(f"stored{u}"), 16)
                per = 2 * (2 * T + 2)
                with dve.Fori(0, NIT) as i:
                    step = Chain(dve, sem("ln"), i * per)
                    for u in range(2):
                        dve.wait_ge(sem(f"hin{u}"), 16 * i + 16)
                        for t in range(T):
                            nc.vector.bn_stats(stat[u][:, t, :], hin[u][:, t, :]).then_inc(sem("ln"), 1)
                            step.n += 1
                        wait_alone(dve, sem("ln"), step.start + step.n, sem("dve_passed"))
                        for t in range(T):
                            nc.vector.bn_aggr(mv[u][:, t, :], stat[u][:, t, :]).then_inc(sem("ln"), 1)
                            step.n += 1
                        dve.wait_ge(sem("ln"), step.start + step.n)
                        nc.vector.tensor_scalar(rstd[u][:, 0, :], mv[u][:, :, 1], EPS, None, ALU.add) \
                            .then_inc(sem("var"), 1)
                    for u in range(2):
                        step(nc.vector.tensor_tensor(xn[u][:, :, :], hin[u][:, :, :],
                                                     mv[u][:, :, 0:1].broadcast_to([P, T, V]), ALU.subtract))
                        dve.wait_ge(sem("rstd"), up(i, u))
                        step(nc.vector.tensor_tensor(xn[u][:, :, :], xn[u][:, :, :],
                                                     rstd[u][:, 1, :].unsqueeze(2).broadcast_to([P, T, V]),
                                                     ALU.mult))
                        dve.sem_inc(sem("hin_seen"), 1)
                        dve.sem_inc(sem("xn"), 1)
                    assert step.n == per
                    link = Chain(dve, sem("split"), 4 * i)
                    for u in range(2):
                        dve.wait_ge(sem("part0"), up(i, u))
                        link(nc.vector.scalar_tensor_tensor(rest[u][:, :], flat[u][:, 0:NT], A.qkb[:, 0:1],
                                                            parts[u][:, 0, :], ALU.add, ALU.subtract))
                        link(nc.vector.tensor_copy(parts[u][:, 1, :], rest[u][:, :]))
                        nc.vector.tensor_tensor(parts[u][:, 2, :], rest[u][:, :], parts[u][:, 1, :],
                                                ALU.subtract).then_inc(sem("parts"), 1)
                        dve.wait_ge(sem("v_ps"), up(i, u))
                        nc.vector.tensor_copy(va[u][:, :, :, 1:HD + 1],
                                              flat[u][:, vbase:vbase + T * V].rearrange(
                                                  "p (t h d) -> p t h d", t=T, h=HEADS)).then_inc(sem("va"), 1)
                    for s in range(NS):
                        for u in range(2):
                            dve.wait_ge(sem(f"s{s}_ps"), up(i, u))
                            if wide and s == 0:
                                blk = flat[u].rearrange("p (h m) -> p h m", m=NT)[:, :, P:]
                                nc.vector.tensor_tensor(blk, blk, A.biasS[:, :, :], ALU.add) \
                                    .then_inc(sem("s_bias"), 1)
                                dve.wait_ge(sem("s_bias"), up(i, u))
                            elif not wide:
                                blk = flat[u].rearrange("p (h m) -> p h m", m=W)
                                nc.vector.tensor_tensor(blk, blk,
                                                        A.biasS[:, :].unsqueeze(1).broadcast_to([P, 2048 // W, W]),
                                                        ALU.add).then_inc(sem("s_bias"), 1)
                                dve.wait_ge(sem("s_bias"), up(i, u))
                            if wide:
                                nc.vector.tensor_reduce(mx[u][:, s, :],
                                                        flat[u].rearrange("p (h m) -> p h m", m=NT), AX.X, ALU.max) \
                                    .then_inc(sem(f"m{s}"), 1)
                            else:
                                nc.vector.tensor_reduce(mx[u][:, :, :].rearrange("p t h -> p h t"),
                                                        flat[u].rearrange("p (h t m) -> p h t m", h=HEADS, t=T),
                                                        AX.X, ALU.max).then_inc(sem(f"m{s}"), 1)
                    link = Chain(dve, sem("msplit"), 6 * i)
                    for u in range(2):
                        dve.wait_ge(sem(f"m{NS - 1}"), up(i, u))

                        def part(r):
                            return m3[u][:, :, :, r, :].rearrange("p t q h -> p (t q) h")

                        def heads(tile):
                            return tile[u][:, :, :].rearrange("p t (q h) -> p (t q) h", q=2)
                        link(nc.vector.tensor_scalar(part(0), heads(mx), -1.0, None, ALU.mult))
                        link(nc.vector.scalar_tensor_tensor(heads(mrest), heads(mx), -1.0, part(0),
                                                            ALU.mult, ALU.subtract))
                        link(nc.vector.tensor_copy(part(1), heads(mrest)))
                        nc.vector.tensor_tensor(part(2), heads(mrest), part(1), ALU.subtract) \
                            .then_inc(sem("m3"), 1)
                    for u in range(2):
                        dve.wait_ge(sem(f"t{NS - 1}_ps"), up(i, u))
                        if wide:
                            blk = flat[u].rearrange("p (h m) -> p h m", m=NT)[:, :, 0:P]
                            bias = A.biasT[:, :, :]
                        else:
                            blk = flat[u].rearrange("p (h m) -> p h m", m=W)
                            bias = A.biasT[:, :].unsqueeze(1).broadcast_to([P, 2048 // W, W])
                        nc.vector.tensor_tensor(blk, blk, bias, ALU.add).then_inc(sem("t_bias"), 1)
                    for u in range(2):
                        dve.wait_ge(sem("o_ps"), up(i, u))
                        o = flat[u][:, obase:obase + T * NGRP * P].rearrange("p (a j s) -> p a j s", j=NJ, s=32)
                        nc.vector.reciprocal(rs[u][:, :, :], o[:, :, :, 0]).then_inc(sem("rs"), 1)
                        dve.wait_ge(sem("rs"), up(i, u))
                        nc.vector.tensor_tensor(
                            on[u][:, :, :].rearrange("p t (g j d) -> p (t g) j d", g=NGRP, d=HD),
                            o[:, :, :, 1:HD + 1], rs[u][:, :, :].unsqueeze(3).broadcast_to([P, T * NGRP, NJ, HD]),
                            ALU.mult).then_inc(sem("on"), 1)
                    for u in range(2):
                        dve.wait_ge(sem("y_ps"), up(i, u))
                        dve.wait_ge(sem("hin_kept"), up(i, u) + 2)
                        dve.wait_ge(sem(f"stored{u}"), 16 * i + 16)
                        nc.vector.tensor_tensor(hout[u][:, :, :].rearrange("p t e -> p (t e)"),
                                                flat[u][:, 512:512 + T * V],
                                                hres[u][:, :, :].rearrange("p t e -> p (t e)"), ALU.add) \
                            .then_inc(sem("hout"), 1)
                        dve.wait_ge(sem("hout"), up(i, u))
                        dve.sem_inc(sem("hres_free"), 1)
                        dve.sem_inc(sem("quad_free"), 1)

            @block.scalar
            def _(act):
                if wide:
                    act.wait_ge(sem("kst0"), 2)
                with act.Fori(0, NIT) as i:
                    for u in range(2):
                        act.wait_ge(sem("xT_ps"), up(i, u))
                        nc.scalar.copy(xT[u][:, :, :].rearrange("p s n -> p (s n)"), flat[u][:, 0:NT // 2]) \
                            .then_inc(sem("xT"), 1)
                    for u in range(2):
                        act.wait_ge(sem("qk_ps"), up(i, u))
                        nc.scalar.activation(parts[u][:, 0, :], flat[u][:, 0:NT], ACT.Identity,
                                             bias=A.qkb[:, 0:1]).then_inc(sem("part0"), 1)
                    for u in range(2):
                        act.wait_ge(sem("q_ps"), up(i, u))
                        nc.scalar.copy(qst[u][:, :, :].rearrange("p a n -> p (a n)"), flat[u][:, 0:NPP * NT]) \
                            .then_inc(sem("qst"), 1)
                    for u in range(2):
                        act.wait_ge(sem("k_ps"), up(i, u))
                        if wide:
                            for q in range(2):
                                nc.scalar.activation(
                                    kst[u][halves[q], q * NPP:(q + 1) * NPP, :].rearrange("p a n -> p (a n)"),
                                    flat[u][halves[q], 1024:], ACT.Identity, bias=K.ones_rows[halves[q], 0:1]) \
                                    .then_inc(sem("kst"), 1)
                        else:
                            for q in range(2):
                                nc.scalar.activation(kst[u][:, 2 * q:2 * q + 2, :].rearrange("p a n -> p (a n)"),
                                                     flat[u][:, q * 1024:(q + 1) * 1024], ACT.Identity,
                                                     bias=K.ones_rows[:, 0:1]).then_inc(sem("kst"), 1)
                    for u in range(2):
                        act.wait_ge(sem("mT_ps"), up(i, u))
                        nc.scalar.copy(mT[u][:, :], flat[u][0:3 * HEADS, 0:NT]).then_inc(sem("mT"), 1)
                    for s in range(NS):
                        for u in range(2):
                            if s == NS - 1:
                                act.wait_ge(sem("t_bias"), up(i, u))
                            else:
                                act.wait_ge(sem(f"t{s}_ps"), up(i, u))
                            dst = pr[u][:, s, :, :].rearrange("p h n -> p (h n)") if wide \
                                else pr[u][:, :, :, :].rearrange("p h t n -> p (h t n)")
                            nc.scalar.activation(dst, flat[u], ACT.Exp).then_inc(sem(f"p{s}"), 1)
                    for u in range(2):
                        act.wait_ge(sem("pv_ps"), up(i, u))
                        if wide:
                            last = nc.scalar.copy(oT[u][:, :, :].rearrange("p g n -> p (g n)"), flat[u][:, 0:512])
                        else:
                            for par in range(2):
                                last = nc.scalar.copy(
                                    oT[u][:, :, :].rearrange("p g (t q n) -> p (g t) q n", q=2, n=W)[:, :, par, :],
                                    quad[u][:, par, :].rearrange("p (a n) -> p a n", n=W))
                        last.then_inc(sem("oT"), 1)
                    for u in range(2):
                        act.wait_ge(sem("onT_ps"), up(i, u))
                        nc.scalar.copy(onT[u][:, :, :].rearrange("p s n -> p (s n)"), flat[u][:, 0:NT // 2]) \
                            .then_inc(sem("onT"), 1)

            @block.tensor
            def _(pe):
                def turn(u, src):
                    for s in range(T // 2):
                        last = nc.tensor.transpose(flat[u][:, s * P:(s + 1) * P],
                                                   src[u][:, 2 * s:2 * s + 2, :].rearrange("p q e -> p (q e)"),
                                                   K.ident[:, :])
                    return last

                def product(u, srcT, w):
                    for s in range(T // 2):
                        last = nc.tensor.matmul(flat[u][:, 512 + s * P:512 + (s + 1) * P], srcT[u][:, s, :],
                                                w[:, :, :].rearrange("p q e -> p (q e)"), start=True, stop=True)
                    return last

                def select(u, qk, base):
                    for pp in range(NPP):
                        for r in range(3):
                            last = nc.tensor.matmul(flat[u][:, base + pp * NT:base + (pp + 1) * NT],
                                                    K.sel[:, qk, r, pp, :], parts[u][:, r, :],
                                                    start=r == 0, stop=r == 2)
                    return last

                with pe.Fori(0, NIT) as i:
                    for u in range(2):
                        pe.wait_ge(sem("xn"), up(i, u))
                        wait_alone(pe, sem("quad_free"), up(i, u), sem("pe_passed"))
                        turn(u, xn).then_inc(sem("xT_ps"), 1)
                    for u in range(2):
                        pe.wait_ge(sem("xT"), up(i, u))
                        for par in range(2):
                            last = nc.tensor.matmul(
                                flat[u][:, 0:NT].rearrange("p (s q n) -> p q s n", q=2, n=P)[:, par],
                                A.wqk[:, par, :], xT[u][:, :, :], start=True, stop=True)
                        last.then_inc(sem("qk_ps"), 1)
                        product(u, xT, A.wv).then_inc(sem("v_ps"), 1)
                    for u in range(2):
                        pe.wait_ge(sem("parts"), up(i, u))
                        pe.wait_ge(sem("va"), up(i, u))
                        select(u, 0, 0).then_inc(sem("q_ps"), 1)
                    for u in range(2):
                        if not wide:
                            pe.wait_ge(sem("qst"), up(i, u))
                        select(u, 1, 1024 if wide else 0).then_inc(sem("k_ps"), 1)
                    for s in range(NS):
                        for u in range(2):
                            if s == 0:
                                pe.wait_ge(sem("qst"), up(i, u))
                                wait_alone(pe, sem("kst"), 2 * up(i, u), sem("pe_passed"))
                            else:
                                pe.wait_ge(sem(f"m{s - 1}"), up(i, u))
                            score_mms(u, s, qst, kst).then_inc(sem(f"s{s}_ps"), 1)
                    for u in range(2):
                        pe.wait_ge(sem("m3"), up(i, u))
                        for t in range(T):
                            last = nc.tensor.matmul(flat[u][0:3 * HEADS, t * P:(t + 1) * P],
                                                    m3[u][:, t, :, :, :].rearrange("p q r h -> p (q r h)"),
                                                    K.identb[:, :], start=True, stop=True)
                        last.then_inc(sem("mT_ps"), 1)
                    for s in range(NS):
                        for u in range(2):
                            if s == 0:
                                wait_alone(pe, sem(f"max{u}"), 32 * i + 32, sem("pe_passed"))
                            else:
                                pe.wait_ge(sem(f"p{s - 1}"), up(i, u))
                            score_mms(u, s, kst, qst).then_inc(sem(f"t{s}_ps"), 1)
                    for u in range(2):
                        wait_alone(pe, sem(f"p{NS - 1}"), up(i, u), sem("pe_passed"))
                        if wide:
                            for g in range(NGRP):
                                for s in range(NS):
                                    for j in range(NJ):
                                        last = nc.tensor.matmul(flat[u][32 * j:32 * j + 32, g * NT:(g + 1) * NT],
                                                                va[u][:, s, g * NJ + j, :], pr[u][:, s, g * NJ + j, :],
                                                                start=s == 0, stop=s == NS - 1,
                                                                tile_position=(0, 32 * j))
                        else:
                            for g in range(NGRP):
                                for t in range(T):
                                    for par in range(2):
                                        for j in range(NJ):
                                            k = slice(par * W, (par + 1) * W)
                                            c = (g * T + t) * W
                                            last = nc.tensor.matmul(quad[u][32 * j:32 * j + 32, par, c:c + W],
                                                                    va[u][k, t, g * NJ + j, :],
                                                                    pr[u][k, g * NJ + j, t, :],
                                                                    start=True, stop=True,
                                                                    tile_position=(par * W, 32 * j))
                        last.then_inc(sem("pv_ps"), 1)
                    for u in range(2):
                        pe.wait_ge(sem("oT"), up(i, u))
                        for t in range(T):
                            for g in range(NGRP):
                                c = obase + (t * NGRP + g) * P
                                last = nc.tensor.transpose(flat[u][:, c:c + P], oT[u][:, g, t * P:(t + 1) * P],
                                                           K.ident[:, :])
                        last.then_inc(sem("o_ps"), 1)
                    for u in range(2):
                        wait_alone(pe, sem("on"), up(i, u), sem("pe_passed"))
                        turn(u, on).then_inc(sem("onT_ps"), 1)
                    for u in range(2):
                        pe.wait_ge(sem("onT"), up(i, u))
                        product(u, onT, A.wo).then_inc(sem("y_ps"), 1)


def attention_weights(nc, a, K, dram_ext, ctx):
    A0, A1 = Consts(), Consts()

    def sb(name, shape, dt=F32):
        return ctx.enter_context(nc.sbuf_tensor(name, shape, dt))

    for A, n in ((A0, "a0"), (A1, "a1")):
        A.wqk = sb(n + "_wqk", [P, 2, P])
        A.wv, A.wo = sb(n + "_wv", [P, 2, V]), sb(n + "_wo", [P, 2, V])
        A.qkb = sb(n + "_qkb", [P, 1])
        A.brow = sb(n + "_brow", [P, V])
    A0.biasS, A0.biasT = sb("a0_biasS", [P, 64]), sb("a0_biasT", [P, 64])
    A1.biasS, A1.biasT = sb("a1_biasS", [P, HEADS, P]), sb("a1_biasT", [P, HEADS, P])
    K.sel = sb("sel", [P, 2, 3, NPP, P], BF16)
    K.identb = sb("identb", [P, P], BF16)
    K.ones_rows = sb("ones_rows", [P, 1])
    EXT = 2 * P - 1
    NTAB = a["L1_attn_rpb_table"].shape[0]
    with ExitStack() as tmp:
        def ts(name, shape):
            return tmp.enter_context(nc.sbuf_tensor(name, shape, F32))

        sem = Signals(nc, "aw_")
        tmp.callback(sem.close)

        w0 = ts("aw_w0", [V, 3, 2, V])
        o0 = ts("aw_o0", [V, 2, V])
        w1 = ts("aw_w1", [P, 3 * V])
        o1 = ts("aw_o1", [P, V])
        tab = ts("aw_tab", [NTAB, HEADS])
        ext = ts("aw_ext", [HEADS, EXT])
        hank0 = ts("aw_hank0", [P, 64])
        hank1 = ts("aw_hank1", [P, HEADS, P])
        brd = ts("aw_brd", [P, V])
        bv = ts("aw_bv", [V, 1])
        bqk = ts("aw_bqk", [P, 1])
        onesh = ts("aw_onesh", [P, 2])
        rel2 = ts("aw_rel2", [64, 2, 64])
        ps = [tmp.enter_context(nc.psum_tensor(f"aw_ps{b}", [P, 512], F32)) for b in range(8)]
        hf = [slice(64 * q, 64 * q + 64) for q in range(2)]

        with nc.Block() as block:
            @block.sync
            def _(sp):
                wq0 = a["L0_attn_w_qkv"].rearrange("(q o) c -> o q c", q=3)
                loads = [(w0[:, :, r, :], wq0) for r in range(2)]
                loads += [(o0[:, r, :], a["L0_attn_w_proj"]) for r in range(2)]
                loads += [(w1[hf[r], :], a["L1_attn_qkv_w"]) for r in range(2)]
                loads += [(o1[hf[r], :], a["L1_attn_proj_w"]) for r in range(2)]
                loads += [(tab[:, :], a["L1_attn_rpb_table"]),
                          (A0.brow[:, :], a["L0_attn_b_proj"].partition_broadcast(P)),
                          (brd[:, :], a["L1_attn_proj_b"].partition_broadcast(P)),
                          (bv[:, :], a["L1_attn_qkv_b"][2 * V:3 * V].unsqueeze(1)),
                          (bqk[:, :], a["L1_attn_qkv_b"][0:2 * V].unsqueeze(1))]
                rb = a["L0_attn_rel_bias"]
                for q in range(2):
                    loads.append((hank0[hf[q], :], bass.AP(rb.tensor, 0, [[1, 64], [1, 64]])))
                for dst, src in loads:
                    sp.dma_start(dst, src).then_inc(sem("loaded"), 16)
                K.n_aw = 16 * len(loads)
                sp.wait_ge(sem("ext"), 1)
                sp.dma_start(dram_ext, ext[:, :]).then_inc(sem("extd"), 16)
                sp.wait_ge(sem("extd"), 16)
                for h in range(HEADS):
                    sp.dma_start(hank1[:, h, :], bass.AP(dram_ext.tensor, h * EXT, [[1, P], [1, P]])) \
                        .then_inc(sem("bT"), 16)

            @block.gpsimd
            def _(pool):
                nc.gpsimd.memset(K.sel[:, :, :, :, :], 0.0).then_inc(sem("sel0"), 1)

            @block.vector
            def _(dve):
                step = Chain(dve, sem("dve"))
                for A in (A0, A1):
                    nc.vector.memset(A.wqk[:, :, :], 0.0)
                    nc.vector.memset(A.wv[:, :, :], 0.0)
                    step(nc.vector.memset(A.wo[:, :, :], 0.0))
                nc.vector.memset(A0.qkb[:, :], 0.0)
                step(nc.vector.tensor_reduce(onesh[:, :], K.ident[:, :].rearrange("p (q n) -> p q n", q=2)[:, :, 0:3],
                                             AX.X, ALU.add))
                step(nc.vector.tensor_reduce(K.ones_rows[:, :], onesh[:, :], AX.X, ALU.add))
                step(nc.vector.tensor_copy(K.identb[:, :], K.ident[:, :]))
                dve.wait_ge(sem("sel0"), 1)
                for n, pair in enumerate(SLOTS):
                    for qk in range(2):
                        c = OFF + n * HD
                        dst = K.sel[:, qk, pair[qk], :, :].rearrange("p a (q n) -> p a q n", q=2)[:, :, :, c:c + HD]
                        src = K.ident[:, qk * V:(qk + 1) * V].rearrange("p (q a d) -> p a q d", q=2, a=NPP)
                        step(nc.vector.tensor_copy(dst, src))
                dve.wait_ge(sem("loaded"), K.n_aw)
                for r in range(2):
                    nc.vector.tensor_scalar(A1.wqk[hf[r], r, 0:V], w1[hf[r], 0:V], Q_SCALE, None, ALU.mult)
                    nc.vector.tensor_copy(A1.wqk[hf[r], r, V:], w1[hf[r], V:2 * V])
                    nc.vector.tensor_copy(A1.wv[hf[r], r, :], w1[hf[r], 2 * V:])
                    step(nc.vector.tensor_copy(A1.wo[hf[r], r, :], o1[hf[r], :]))
                nc.vector.tensor_scalar(A1.qkb[hf[0], :], bqk[hf[0], :], Q_SCALE, None, ALU.mult)
                step(nc.vector.tensor_copy(A1.qkb[hf[1], :], bqk[hf[1], :]))
                step(nc.vector.tensor_copy(A0.biasT[:, :], hank0[:, ::-1]))
                for q in range(2):
                    step(nc.vector.tensor_copy(rel2[:, q, :], hank0[0:64, ::-1]))
                dve.sem_inc(sem("rel2"), 1)
                dve.wait_ge(sem("wT"), 1)
                for r in range(2):
                    nc.vector.tensor_scalar(A0.wqk[hf[r], r, 0:V], ps[0][hf[r], 0:V], Q_SCALE, None, ALU.mult)
                    nc.vector.tensor_copy(A0.wqk[hf[r], r, V:], ps[1][hf[r], 0:V])
                    nc.vector.tensor_copy(A0.wv[hf[r], r, :], ps[2][hf[r], 0:V])
                    step(nc.vector.tensor_copy(A0.wo[hf[r], r, :], ps[3][hf[r], 0:V]))
                step(nc.vector.tensor_copy(A0.biasS[:, :], ps[4][:, 0:64]))
                step(nc.vector.tensor_tensor(A1.brow[:, :], ps[7][:, 0:V], brd[:, :], ALU.add))
                step(nc.vector.memset(ext[:, :], 0.0))
                step(nc.vector.tensor_scalar(ext[:, 0:NTAB], ps[6][0:HEADS, 0:NTAB],
                                             ps[6][0:HEADS, NTAB - 1:NTAB], None, ALU.subtract))
                dve.sem_inc(sem("ext"), 1)
                dve.wait_ge(sem("bT"), 16 * HEADS)
                step(nc.vector.tensor_copy(A1.biasS[:, :, :], hank1[:, :, ::-1]))
                dve.sem_inc(sem("biasS"), 1)
                for c in range(2):
                    dve.wait_ge(sem("bS"), c + 1)
                    step(nc.vector.tensor_copy(A1.biasT[:, 4 * c:4 * c + 4, :].rearrange("p h m -> p (h m)"),
                                               ps[c][:, :]))

            @block.tensor
            def _(pe):
                pe.wait_ge(sem("loaded"), K.n_aw)
                idv = K.ident[0:V, 0:V]
                for q in range(3):
                    nc.tensor.transpose(ps[q][:, 0:V], w0[:, q, :, :].rearrange("p r c -> p (r c)"), idv)
                nc.tensor.transpose(ps[3][:, 0:V], o0[:, :, :].rearrange("p r c -> p (r c)"), idv)
                pe.wait_ge(sem("rel2"), 1)
                nc.tensor.transpose(ps[4][:, 0:64], rel2[:, :, :].rearrange("p q m -> p (q m)"), idv)
                nc.tensor.transpose(ps[6][0:HEADS, 0:NTAB], tab[:, :], K.ident[0:NTAB, 0:NTAB])
                nc.tensor.matmul(ps[7][:, 0:V], bv[:, 0:1].broadcast_to([V, P]), o1[0:V, :], start=True, stop=True) \
                    .then_inc(sem("wT"), 1)
                pe.wait_ge(sem("biasS"), 1)
                for h in range(HEADS):
                    last = nc.tensor.transpose(ps[h // 4][:, (h % 4) * P:(h % 4 + 1) * P], A1.biasS[:, h, :],
                                               K.ident[:, :])
                    if h % 4 == 3:
                        last.then_inc(sem("bS"), 1)
    return A0, A1


class Consts:
    pass


NE = 8
NPAIR = NE // 2
TB = 8
BN_EPS = 1e-3
NBLK = NTOK // (TB * P)


def norm_stats(nc, dve, sem, count, hin, stat, mv, tiles):
    n = count
    for t in range(tiles):
        nc.vector.bn_stats(stat[:, t, :], hin[:, t, :]).then_inc(sem, 1)
    wait = n + tiles
    dve.wait_ge(sem, wait)
    dve.sem_inc(sem, 1)
    for t in range(tiles):
        nc.vector.bn_aggr(mv[:, t, :], stat[:, t, :]).then_inc(sem, 1)
    dve.wait_ge(sem, wait + 1 + tiles)
    return 2 * tiles + 1


def ffn0_gate(nc, a, K, F, h_in):
    with ExitStack() as ctx:
        def sb(n, shape):
            return ctx.enter_context(nc.sbuf_tensor("fg_" + n, shape, F32))

        sem = Signals(nc, "fg_")
        ctx.callback(sem.close)

        names = ["b1", "g1", "be1", "m1", "v1", "b2", "g2", "be2", "m2", "v2"]
        NV = len(names)
        rows = sb("rows", [NV * NPAIR, P])
        col = sb("col", [P, NV, NPAIR])
        sc = sb("sc", [P, 2, NPAIR])
        dg = sb("dg", [P, P])
        b2m = sb("b2m", [P, NPAIR, NE])
        cb = sb("cb", [NE, V])
        bo = sb("bo", [NE, V])
        wr = sb("wr", [V, NE])
        br = sb("br", [P, NE])
        hin = [sb(f"hin{u}", [P, TB, V]) for u in range(2)]
        stat, mv = sb("stat", [P, TB, 6]), sb("mv", [P, TB, 2])
        rstd = sb("rstd", [P, 2, TB])
        xn = sb("xn", [P, TB, V])
        part = sb("part", [P, 2, V])
        feat = sb("feat", [P, 2, V])
        featT = sb("featT", [V, 2, P])
        lg = sb("lg", [P, 2, NE])
        st = sb("st", [P, 2, 2])
        gw = sb("gw", [P, 2, NE])
        gwT = sb("gwT", [NE, 2, P])
        ps = [ctx.enter_context(nc.psum_tensor(f"fg_ps{b}", [P, 512], F32)) for b in range(8)]
        hi_v = h_in.rearrange("(i u t p) e -> i u p t e", p=P, t=TB, u=2)
        NIT = NBLK // 2
        per = 2 * TB + 1 + 4
        with nc.Block() as block:
            @block.sync
            def _(sp):
                sp.wait_ge(sem("zero"), 1)
                n = 0

                def load(dst, src):
                    nonlocal n
                    sp.dma_start(dst, src).then_inc(sem("loaded"), 16)
                    n += 1
                for i, nm in enumerate(names):
                    load(rows[i * NPAIR:(i + 1) * NPAIR, :], a["L0_ffn_" + nm].rearrange("(q s) h -> q (s h)", s=2))
                for half in range(2):
                    load(F.w1[half * V:(half + 1) * V, :, :], a["L0_ffn_W1"].rearrange("e d h -> d e h"))
                    for p in range(NPAIR):
                        load(F.w2[half * V:(half + 1) * V, p, half * V:(half + 1) * V], a["L0_ffn_W2"][2 * p + half])
                load(F.wo[:, :, :], a["L0_ffn_Wo"].rearrange("(q s) h d -> (s h) q d", s=2))
                load(bo[:, :], a["L0_ffn_bo"])
                load(wr[:, :], a["L0_ffn_Wr"])
                load(br[:, :], a["L0_ffn_br"].partition_broadcast(P))
                F.n_loads = 16 * n
                with sp.Fori(0, NIT) as i:
                    for u in range(2):
                        sp.wait_ge(sem("hin_free"), 2 * i + u + 1)
                        sp.dma_start(hin[u][:, :, :], hi_v[i, u]).then_inc(sem(f"hin{u}"), 16)

            @block.gpsimd
            def _(pool):
                with pool.Fori(0, NIT) as i:
                    for u in range(2):
                        pool.wait_ge(sem("var"), 2 * i + u + 1)
                        nc.gpsimd.tensor_tensor(rstd[:, 1, :], rstd[:, 0, :], K.mhalf[:, 0:1].broadcast_to([P, TB]),
                                                ALU.pow).then_inc(sem("rstd"), 1)
                pool.wait_ge(sem("bnv"), 1)
                nc.gpsimd.tensor_tensor(sc[:, :, :], sc[:, :, :],
                                        K.mhalf[:, 0:1].unsqueeze(2).broadcast_to([P, 2, NPAIR]), ALU.pow) \
                    .then_inc(sem("bnr"), 1)

            @block.vector
            def _(dve):
                step = Chain(dve, sem("dve"))
                nc.vector.memset(b2m[:, :, :], 0.0).then_inc(sem("z"), 1)
                step(nc.vector.memset(F.w2[:, :, :], 0.0))
                dve.sem_inc(sem("zero"), 1)
                step(nc.vector.memset(feat[:, :, :], 0.0))
                dve.sem_inc(sem("hin_free"), 2)
                with dve.Fori(0, NIT) as i:
                    for u in range(2):
                        k = (2 * i + u) * per
                        dve.wait_ge(sem(f"hin{u}"), 16 * i + 16)
                        n = norm_stats(nc, dve, sem("ln"), k, hin[u], stat, mv, TB)
                        nc.vector.tensor_scalar(rstd[:, 0, :], mv[:, :, 1], EPS, None, ALU.add) \
                            .then_inc(sem("var"), 1)
                        link = Chain(dve, sem("ln"), k + n)
                        link(nc.vector.tensor_tensor(xn[:, :, :], hin[u][:, :, :],
                                                     mv[:, :, 0:1].broadcast_to([P, TB, V]), ALU.subtract))
                        dve.sem_inc(sem("hin_free"), 1)
                        dve.wait_ge(sem("rstd"), 2 * i + u + 1)
                        link(nc.vector.tensor_tensor(xn[:, :, :], xn[:, :, :],
                                                     rstd[:, 1, :].unsqueeze(2).broadcast_to([P, TB, V]), ALU.mult))
                        link(nc.vector.tensor_reduce(part[:, :, :],
                                                     xn[:, :, :].rearrange("p (s q) e -> p q e s", q=2), AX.X, ALU.add))
                        link(nc.vector.tensor_tensor(feat[:, :, :], feat[:, :, :], part[:, :, :], ALU.add))
                        assert n + 4 == per
                dve.sem_inc(sem("feat"), 1)
                dve.wait_ge(sem("colp"), 1)
                step(nc.vector.tensor_copy(col[:, :, :].rearrange("p v q -> p (v q)"), ps[0][:, 0:NV * NPAIR]))
                for k in range(2):
                    step(nc.vector.tensor_scalar(sc[:, k, :], col[:, 5 * k + 4, :], BN_EPS, None, ALU.add))
                dve.sem_inc(sem("bnv"), 1)
                dve.wait_ge(sem("bnr"), 1)
                for k, t in ((0, F.t1), (1, F.t2)):
                    b, g, be, m = (col[:, 5 * k + r, :] for r in range(4))
                    step(nc.vector.tensor_tensor(F.s[:, k, :], sc[:, k, :], g, ALU.mult))
                    step(nc.vector.tensor_tensor(t[:, :], b, m, ALU.subtract))
                    step(nc.vector.tensor_tensor(t[:, :], t[:, :], F.s[:, k, :], ALU.mult))
                    step(nc.vector.tensor_tensor(t[:, :], t[:, :], be, ALU.add))
                step(nc.vector.tensor_scalar(F.nt2[:, :], F.t2[:, :], -1.0, None, ALU.mult))
                for p in range(NPAIR):
                    step(nc.vector.tensor_scalar(dg[:, :], K.ident[:, :], F.s[:, 1, p:p + 1], float(D), ALU.mult, ALU.mult))
                    dve.sem_inc(sem("dg"), 1)
                    dve.wait_ge(sem("s2row"), p + 1)
                    step(nc.vector.tensor_tensor(F.w2[:, p, :], F.w2[:, p, :], ps[1][:, 0:P], ALU.mult))
                    for s in range(2):
                        hf = slice(s * V, (s + 1) * V)
                        step(nc.vector.tensor_copy(b2m[hf, p, 2 * p + s:2 * p + s + 1], F.t2[hf, p:p + 1]))
                dve.sem_inc(sem("b2m"), 1)
                dve.wait_ge(sem("cbp"), 1)
                step(nc.vector.tensor_tensor(cb[:, :], ps[2][0:NE, 0:V], bo[:, :], ALU.add))
                dve.wait_ge(sem("featp"), 1)
                step(nc.vector.tensor_scalar(featT[:, :, :].rearrange("p q n -> p (q n)"), ps[3][0:V, 0:2 * P],
                                             1.0 / SEQ, None, ALU.mult))
                dve.sem_inc(sem("featT"), 1)
                dve.wait_ge(sem("lgp"), 1)
                step(nc.vector.tensor_tensor(lg[:, :, :], ps[4][:, 0:2 * NE].rearrange("p (q e) -> p q e", q=2),
                                             br[:, :].unsqueeze(1).broadcast_to([P, 2, NE]), ALU.add))
                step(nc.vector.tensor_reduce(st[:, 0, :], lg[:, :, :], AX.X, ALU.max))
                step(nc.vector.tensor_tensor(lg[:, :, :], lg[:, :, :],
                                             st[:, 0, :].unsqueeze(2).broadcast_to([P, 2, NE]), ALU.subtract))
                dve.sem_inc(sem("lg"), 1)
                dve.wait_ge(sem("lge"), 1)
                step(nc.vector.tensor_reduce(st[:, 0, :], lg[:, :, :], AX.X, ALU.add))
                step(nc.vector.reciprocal(st[:, 1, :], st[:, 0, :]))
                step(nc.vector.tensor_tensor(gw[:, :, :], lg[:, :, :],
                                             st[:, 1, :].unsqueeze(2).broadcast_to([P, 2, NE]), ALU.mult))
                dve.sem_inc(sem("gw"), 1)
                dve.wait_ge(sem("gwp"), 1)
                for p in range(NPAIR):
                    step(nc.vector.tensor_copy(F.gate[:, p, :, :].rearrange("p q n -> p (q n)"),
                                               ps[5 + p // 2][:, (p % 2) * 256:(p % 2) * 256 + 256]))
                step(nc.vector.tensor_copy(gwT[:, :, :].rearrange("p q n -> p (q n)"), ps[7][0:NE, 0:2 * P]))
                dve.sem_inc(sem("gwT"), 1)
                dve.wait_ge(sem("corrp"), 1)
                step(nc.vector.tensor_copy(F.corr[:, :, :].rearrange("p q n -> p (q n)"), ps[0][:, 0:2 * V]))

            @block.scalar
            def _(act):
                act.wait_ge(sem("lg"), 1)
                nc.scalar.activation(lg[:, :, :], lg[:, :, :], ACT.Exp).then_inc(sem("lge"), 1)

            @block.tensor
            def _(pe):
                pe.wait_ge(sem("loaded"), F.n_loads)
                nc.tensor.transpose(ps[0][:, 0:NV * NPAIR], rows[:, :], K.ident[0:NV * NPAIR, 0:NV * NPAIR]) \
                    .then_inc(sem("colp"), 1)
                for p in range(NPAIR):
                    pe.wait_ge(sem("dg"), p + 1)
                    nc.tensor.matmul(ps[1][:, 0:P], K.onesD[:, :], dg[:, :], start=True, stop=True) \
                        .then_inc(sem("s2row"), 1)
                pe.wait_ge(sem("b2m"), 1)
                for p in range(NPAIR):
                    last = nc.tensor.matmul(ps[2][0:NE, 0:V], b2m[:, p, :], F.wo[:, p, :],
                                            start=p == 0, stop=p == NPAIR - 1)
                last.then_inc(sem("cbp"), 1)
                pe.wait_ge(sem("feat"), 1)
                for q in range(2):
                    last = nc.tensor.transpose(ps[3][0:V, q * P:(q + 1) * P], feat[:, q, :], K.ident[:, :])
                last.then_inc(sem("featp"), 1)
                pe.wait_ge(sem("featT"), 1)
                for q in range(2):
                    last = nc.tensor.matmul(ps[4][:, q * NE:(q + 1) * NE], featT[:, q, :], wr[:, :],
                                            start=True, stop=True)
                last.then_inc(sem("lgp"), 1)
                pe.wait_ge(sem("gw"), 1)
                for q in range(2):
                    for p in range(NPAIR):
                        for s in range(2):
                            c = (p % 2) * 256 + q * P
                            nc.tensor.matmul(ps[5 + p // 2][s * V:(s + 1) * V, c:c + P],
                                             gw[:, q, 2 * p + s:2 * p + s + 1].broadcast_to([P, V]), K.ident[:, :],
                                             start=True, stop=True)
                    last = nc.tensor.transpose(ps[7][0:NE, q * P:(q + 1) * P], gw[:, q, :], K.ident[:, :])
                last.then_inc(sem("gwp"), 1)
                pe.wait_ge(sem("gwT"), 1)
                for q in range(2):
                    last = nc.tensor.matmul(ps[0][:, q * V:(q + 1) * V], gwT[:, q, :], cb[:, :], start=True, stop=True)
                last.then_inc(sem("corrp"), 1)


def ffn0(nc, K, F, h_in, h_out):
    with ExitStack() as ctx:
        def sb(n, shape):
            return [ctx.enter_context(nc.sbuf_tensor(f"f0_{n}{u}", shape, F32)) for u in range(2)]

        sem = Signals(nc, "f0_")
        ctx.callback(sem.close)

        hin, hout, hres = sb("hin", [P, TB, V]), sb("hout", [P, TB, V]), sb("hres", [P, TB, V])
        stat, mv, rstd = sb("stat", [P, TB, 6]), sb("mv", [P, TB, 2]), sb("rstd", [P, 2, TB])
        xn, xT = sb("xn", [P, TB, V]), sb("xT", [P, 512])
        h1, g2 = sb("h1", [P, 2, 512]), sb("g2", [P, 2, 512])
        ps = [ctx.enter_context(nc.psum_tensor(f"f0_ps{b}", [P, 512], F32)) for b in range(8)]
        py, pt = ps[6], ps[7]
        hi_v = h_in.rearrange("(i u t p) e -> i u p t e", p=P, t=TB, u=2)
        ho_v = h_out.rearrange("(i u t p) e -> i u p t e", p=P, t=TB, u=2)
        NIT = NBLK // 2

        def up(i, u):
            return 2 * i + u + 1

        def pair(i, u, p):
            return NPAIR * (2 * i + u) + p + 1

        with nc.Block() as block:
            @block.sync
            def _(sp):
                with sp.Fori(0, NIT) as i:
                    for u in range(2):
                        sp.wait_ge(sem("hin_seen"), up(i, u))
                        sp.wait_ge(sem("hin_kept"), up(i, u))
                        sp.dma_start(hin[u][:, :, :], hi_v[i, u]).then_inc(sem(f"hin{u}"), 16)
                    for u in range(2):
                        sp.wait_ge(sem("hout"), up(i, u))
                        sp.dma_start(ho_v[i, u], hout[u][:, :, :]).then_inc(sem(f"stored{u}"), 16)
                for u in range(2):
                    sp.wait_ge(sem(f"stored{u}"), 16 * (NIT + 1))

            @block.gpsimd
            def _(pool):
                pool.sem_inc(sem("hin_kept"), 2)
                with pool.Fori(0, NIT) as i:
                    for u in range(2):
                        pool.wait_ge(sem("var"), up(i, u))
                        nc.gpsimd.tensor_tensor(rstd[u][:, 1, :], rstd[u][:, 0, :],
                                                K.mhalf[:, 0:1].broadcast_to([P, TB]), ALU.pow) \
                            .then_inc(sem("rstd"), 1)
                    for u in range(2):
                        pool.wait_ge(sem("hres_free"), up(i, u))
                        nc.gpsimd.tensor_tensor(hres[u][:, :, :].rearrange("p (s q) e -> p s (q e)", q=2),
                                                hin[u][:, :, :].rearrange("p (s q) e -> p s (q e)", q=2),
                                                F.corr[:, :, :].rearrange("p q e -> p (q e)").unsqueeze(1)
                                                .broadcast_to([P, TB // 2, 2 * V]), ALU.add) \
                            .then_inc(sem("hin_kept"), 1)

            @block.vector
            def _(dve):
                dve.sem_inc(sem("hin_seen"), 2)
                dve.sem_inc(sem("hres_free"), 2)
                for u in range(2):
                    dve.sem_inc(sem(f"stored{u}"), 16)
                per = 2 * TB + 1 + 2
                with dve.Fori(0, NIT) as i:
                    for u in range(2):
                        k = (2 * i + u) * per
                        dve.wait_ge(sem(f"hin{u}"), 16 * i + 16)
                        n = norm_stats(nc, dve, sem("ln"), k, hin[u], stat[u], mv[u], TB)
                        nc.vector.tensor_scalar(rstd[u][:, 0, :], mv[u][:, :, 1], EPS, None, ALU.add) \
                            .then_inc(sem("var"), 1)
                        link = Chain(dve, sem("ln"), k + n)
                        link(nc.vector.tensor_tensor(xn[u][:, :, :], hin[u][:, :, :],
                                                     mv[u][:, :, 0:1].broadcast_to([P, TB, V]), ALU.subtract))
                        dve.sem_inc(sem("hin_seen"), 1)
                        dve.wait_ge(sem("rstd"), up(i, u))
                        link(nc.vector.tensor_tensor(xn[u][:, :, :], xn[u][:, :, :],
                                                     rstd[u][:, 1, :].unsqueeze(2).broadcast_to([P, TB, V]),
                                                     ALU.mult))
                        dve.sem_inc(sem("xn"), 1)
                    for u in range(2):
                        for p in range(NPAIR):
                            for q in range(2):
                                dve.wait_ge(sem("h2_ps"), 2 * (pair(i, u, p) - 1) + q + 1)
                                nc.vector.scalar_tensor_tensor(
                                    g2[p % 2][:, q, :].rearrange("p (s n) -> p s n", n=P),
                                    ps[4 + q][:, :].rearrange("p (s n) -> p s n", n=P), F.nt2[:, p:p + 1],
                                    F.gate[:, p, q:q + 1, :].broadcast_to([P, TB // 2, P]), ALU.max, ALU.mult) \
                                    .then_inc(sem("g2"), 1)
                        dve.wait_ge(sem("y_ps"), up(i, u))
                        dve.wait_ge(sem("hin_kept"), up(i, u) + 2)
                        dve.wait_ge(sem(f"stored{u}"), 16 * i + 16)
                        nc.vector.tensor_tensor(hout[u][:, :, :].rearrange("p t e -> p (t e)"), py[:, :],
                                                hres[u][:, :, :].rearrange("p t e -> p (t e)"), ALU.add) \
                            .then_inc(sem("hout"), 1)
                        dve.wait_ge(sem("hout"), up(i, u))
                        dve.sem_inc(sem("hres_free"), 1)
                        dve.sem_inc(sem("py_free"), 1)

            @block.scalar
            def _(act):
                with act.Fori(0, NIT) as i:
                    for u in range(2):
                        act.wait_ge(sem("xT_ps"), up(i, u))
                        nc.scalar.copy(xT[u][:, :], pt[:, :]).then_inc(sem("xT"), 1)
                        for p in range(NPAIR):
                            act.wait_ge(sem("h1_ps"), pair(i, u, p))
                            for q in range(2):
                                nc.scalar.activation(h1[p % 2][:, q, :], ps[2 * (p % 2) + q][:, :], ACT.Relu,
                                                     bias=F.t1[:, p:p + 1], scale=F.s[:, 0, p:p + 1]) \
                                    .then_inc(sem("h1"), 1)

            @block.tensor
            def _(pe):
                pe.sem_inc(sem("py_free"), 1)

                def first(i, u, p):
                    for q in range(2):
                        hf = slice(q * V, (q + 1) * V)
                        last = nc.tensor.matmul(ps[2 * (p % 2) + q][:, :],
                                                F.w1[hf, 2 * p:2 * p + 2, :].rearrange("p e h -> p (e h)"),
                                                xT[u][hf, :], start=True, stop=True)
                    last.then_inc(sem("h1_ps"), 1)

                def out(i, u, p):
                    pe.wait_ge(sem("g2"), 2 * pair(i, u, p))
                    if p == 0:
                        pe.wait_ge(sem("py_free"), up(i, u))
                    for t in range(TB):
                        s, q = t // 2, t % 2
                        last = nc.tensor.matmul(py[:, t * V:(t + 1) * V], g2[p % 2][:, q, s * P:(s + 1) * P],
                                                F.wo[:, p, :], start=p == 0 and t == 0, stop=p == NPAIR - 1,
                                                skip_group_check=True)
                    if p == NPAIR - 1:
                        last.then_inc(sem("y_ps"), 1)

                with pe.Fori(0, NIT) as i:
                    for u in range(2):
                        pe.wait_ge(sem("xn"), up(i, u))
                        for s in range(TB // 2):
                            last = nc.tensor.transpose(pt[:, s * P:(s + 1) * P],
                                                       xn[u][:, 2 * s:2 * s + 2, :].rearrange("p q e -> p (q e)"),
                                                       K.ident[:, :])
                        last.then_inc(sem("xT_ps"), 1)
                        pe.wait_ge(sem("xT"), up(i, u))
                        first(i, u, 0)
                        for p in range(NPAIR):
                            if p + 1 < NPAIR:
                                first(i, u, p + 1)
                            if p >= 1:
                                out(i, u, p - 1)
                            for q in range(2):
                                pe.wait_ge(sem("h1"), 2 * (pair(i, u, p) - 1) + q + 1)
                                nc.tensor.matmul(ps[4 + q][:, :], F.w2[:, p, :], h1[p % 2][:, q, :],
                                                 start=True, stop=True).then_inc(sem("h2_ps"), 1)
                        out(i, u, NPAIR - 1)


def ffn1(nc, a, K, h_in, h_out):
    with ExitStack() as ctx:
        def one(n, shape):
            return ctx.enter_context(nc.sbuf_tensor("f1_" + n, shape, F32))

        def sb(n, shape):
            return [one(f"{n}{u}", shape) for u in range(2)]

        sem = Signals(nc, "f1_")
        ctx.callback(sem.close)

        H = P
        w1, w2 = one("w1", [P, NE, H]), one("w2", [H, NE, V])
        b1r, b1 = one("b1r", [NE, H]), one("b1", [H, NE])
        gam, bet = one("gam", [P, 1]), one("bet", [V, 1])
        wr, wrg = one("wr", [P, NE]), one("wrg", [P, 2, NE])
        br = one("br", [P, NE])
        b2bd = one("b2bd", [TB * NE, TB, V])
        lower = one("lower", [P, NE, NE])
        hin, hout = sb("hin", [P, TB, V]), sb("hout", [P, TB, V])
        stat, mv, rstd = sb("stat", [P, TB, 6]), sb("mv", [P, TB, 2]), sb("rstd", [P, 2, TB])
        xn, xT = sb("xn", [P, TB, V]), sb("xT", [P, 512])
        act1 = sb("act1", [H, 2, 512])
        lg = sb("lg", [P, TB, NE])
        gt, eq = one("gt", [P, TB, NE, NE]), one("eq", [P, TB, NE, NE])
        rank, sel = one("rank", [P, TB, NE]), one("sel", [P, 2, TB, NE])
        v12 = sb("v12", [P, 4, TB])
        gate = sb("gate", [P, TB, NE])
        gT = sb("gT", [TB * NE, P])
        term = sb("term", [P, TB, V])
        acc = sb("acc", [P, TB, V])
        ps = [ctx.enter_context(nc.psum_tensor(f"f1_ps{b}", [P, 512], F32)) for b in range(8)]
        pm, pt = ps[6], ps[7]
        hi_v = h_in.rearrange("(i u p t) e -> i u p t e", p=P, t=TB, u=2)
        ho_v = h_out.rearrange("(i u p t) e -> i u p t e", p=P, t=TB, u=2)
        NIT = NBLK // 2
        NL = [0]

        def up(i, u):
            return 2 * i + u + 1

        def ex(i, u, e):
            return NE * (2 * i + u) + e + 1

        with nc.Block() as block:
            @block.sync
            def _(sp):
                sp.wait_ge(sem("zero"), 1)

                def load(dst, src):
                    sp.dma_start(dst, src).then_inc(sem("loaded"), 16)
                    NL[0] += 16
                for q in range(2):
                    hf = slice(q * V, (q + 1) * V)
                    load(w1[hf, :, :], a["L1_ffn_W1"].rearrange("e d h -> d e h"))
                    load(wr[hf, :], a["L1_ffn_Wr"])
                    load(gam[hf, :], a["L1_ffn_gamma"].unsqueeze(1))
                load(bet[:, :], a["L1_ffn_beta"].unsqueeze(1))
                load(w2[:, :, :], a["L1_ffn_W2"].rearrange("e h d -> h e d"))
                load(b1r[:, :], a["L1_ffn_b1"])
                load(br[:, :], a["L1_ffn_br"].partition_broadcast(P))
                for t in range(TB):
                    load(b2bd[t * NE:(t + 1) * NE, t, :], a["L1_ffn_b2"])
                with sp.Fori(0, NIT) as i:
                    for u in range(2):
                        sp.wait_ge(sem("hin_seen"), up(i, u))
                        sp.wait_ge(sem("hin_kept"), up(i, u))
                        sp.dma_start(hin[u][:, :, :], hi_v[i, u]).then_inc(sem(f"hin{u}"), 16)
                    for u in range(2):
                        sp.wait_ge(sem("hout"), up(i, u))
                        sp.dma_start(ho_v[i, u], hout[u][:, :, :]).then_inc(sem(f"stored{u}"), 16)
                for u in range(2):
                    sp.wait_ge(sem(f"stored{u}"), 16 * (NIT + 1))

            @block.gpsimd
            def _(pool):
                pool.sem_inc(sem("hin_kept"), 2)
                pool.sem_inc(sem("acc"), 2)
                with pool.Fori(0, NIT) as i:
                    for u in range(2):
                        pool.wait_ge(sem("var"), up(i, u))
                        nc.gpsimd.tensor_tensor(rstd[u][:, 1, :], rstd[u][:, 0, :],
                                                K.mhalf[:, 0:1].broadcast_to([P, TB]), ALU.pow) \
                            .then_inc(sem("rstd"), 1)
                    for u in range(2):
                        for e in range(NE):
                            pool.wait_ge(sem("term"), ex(i, u, e) + 2)
                            pool.wait_ge(sem("acc"), ex(i, u, e) + 1)
                            if e == 0:
                                pool.wait_ge(sem("acc_free"), up(i, u))
                            nc.gpsimd.tensor_tensor(acc[u][:, :, :], (hin if e == 0 else acc)[u][:, :, :],
                                                    term[e % 2][:, :, :], ALU.add).then_inc(sem("acc"), 1)
                            if e == 0:
                                pool.wait_ge(sem("acc"), ex(i, u, e) + 2)
                                pool.sem_inc(sem("hin_kept"), 1)

            @block.vector
            def _(dve):
                step = Chain(dve, sem("dve"))
                step(nc.vector.memset(b2bd[:, :, :], 0.0))
                step(nc.vector.memset(wrg[:, :, :], 0.0))
                dve.sem_inc(sem("zero"), 1)
                step(nc.vector.memset(lower[:, :, :], 0.0))
                for e in range(1, NE):
                    step(nc.vector.memset(lower[:, e, 0:e], 1.0))
                dve.wait_ge(sem("setp"), 1)
                step(nc.vector.tensor_copy(b1[:, :], ps[0][:, 0:NE]))
                step(nc.vector.tensor_tensor(b1[:, :], b1[:, :], ps[1][:, 0:NE], ALU.add))
                step(nc.vector.tensor_tensor(br[:, :], br[:, :], ps[2][:, 0:NE], ALU.add))
                step(nc.vector.tensor_scalar(w1[:, :, :], w1[:, :, :], gam[:, 0:1], None, ALU.mult))
                for q in range(2):
                    hf = slice(q * V, (q + 1) * V)
                    step(nc.vector.tensor_scalar(wrg[hf, q, :], wr[hf, :], gam[hf, 0:1], None, ALU.mult))
                dve.sem_inc(sem("set"), 1)
                dve.sem_inc(sem("hin_seen"), 2)
                dve.sem_inc(sem("acc_free"), 2)
                dve.sem_inc(sem("term"), 2)
                for u in range(2):
                    dve.sem_inc(sem(f"stored{u}"), 16)
                per = 2 * TB + 1 + 2
                perg = 12
                with dve.Fori(0, NIT) as i:
                    for u in range(2):
                        k = (2 * i + u) * per
                        dve.wait_ge(sem(f"hin{u}"), 16 * i + 16)
                        n = norm_stats(nc, dve, sem("ln"), k, hin[u], stat[u], mv[u], TB)
                        nc.vector.tensor_scalar(rstd[u][:, 0, :], mv[u][:, :, 1], EPS, None, ALU.add) \
                            .then_inc(sem("var"), 1)
                        link = Chain(dve, sem("ln"), k + n)
                        link(nc.vector.tensor_tensor(xn[u][:, :, :], hin[u][:, :, :],
                                                     mv[u][:, :, 0:1].broadcast_to([P, TB, V]), ALU.subtract))
                        dve.sem_inc(sem("hin_seen"), 1)
                        dve.wait_ge(sem("rstd"), up(i, u))
                        link(nc.vector.tensor_tensor(xn[u][:, :, :], xn[u][:, :, :],
                                                     rstd[u][:, 1, :].unsqueeze(2).broadcast_to([P, TB, V]),
                                                     ALU.mult))
                        dve.sem_inc(sem("xn"), 1)
                    for u in range(2):
                        dve.wait_ge(sem("lg_ps"), up(i, u))
                        link = Chain(dve, sem("gate"), (2 * i + u) * perg)
                        l, r0, r1 = lg[u], sel[:, 0, :, :], sel[:, 1, :, :]
                        a4 = l[:, :, :].unsqueeze(2).broadcast_to([P, TB, NE, NE])
                        b4 = l[:, :, :].unsqueeze(3).broadcast_to([P, TB, NE, NE])
                        link(nc.vector.tensor_tensor(l[:, :, :], pt[:, 0:TB * NE].rearrange("p (t e) -> p t e", e=NE),
                                                     br[:, :].unsqueeze(1).broadcast_to([P, TB, NE]), ALU.add))
                        link(nc.vector.tensor_tensor(gt[:, :, :, :], a4, b4, ALU.is_gt))
                        link(nc.vector.tensor_tensor(eq[:, :, :, :], a4, b4, ALU.is_equal))
                        link(nc.vector.tensor_tensor(eq[:, :, :, :], eq[:, :, :, :],
                                                     lower[:, :, :].unsqueeze(1).broadcast_to([P, TB, NE, NE]),
                                                     ALU.mult))
                        link(nc.vector.tensor_tensor(gt[:, :, :, :], gt[:, :, :, :], eq[:, :, :, :], ALU.add))
                        link(nc.vector.tensor_reduce(rank[:, :, :], gt[:, :, :, :], AX.X, ALU.add))
                        for s in range(2):
                            nc.vector.tensor_scalar(sel[:, s, :, :], rank[:, :, :], float(s), None, ALU.is_equal) \
                                .then_inc(sem("gate"), 1)
                            link.n += 1
                        dve.wait_ge(sem("gate"), link.start + link.n)
                        link(nc.vector.tensor_tensor(gt[:, 0:2, :, :].rearrange("p s t e -> p s (t e)"),
                                                     sel[:, :, :, :].rearrange("p s t e -> p s (t e)"),
                                                     l[:, :, :].rearrange("p t e -> p (t e)").unsqueeze(1)
                                                     .broadcast_to([P, 2, TB * NE]), ALU.mult))
                        link(nc.vector.tensor_reduce(v12[u][:, 0:2, :], gt[:, 0:2, :, :], AX.X, ALU.add))
                        nc.vector.tensor_tensor(v12[u][:, 2, :], v12[u][:, 0, :], v12[u][:, 1, :], ALU.subtract) \
                            .then_inc(sem("dv"), 1)
                        dve.wait_ge(sem("th"), up(i, u))
                        for s in range(2):
                            nc.vector.tensor_scalar(v12[u][:, s, :], v12[u][:, 3, :], 0.5 - s, 0.5, ALU.mult, ALU.add) \
                                .then_inc(sem("v12"), 1)
                        dve.wait_ge(sem("v12"), 2 * up(i, u))
                        link(nc.vector.tensor_tensor(sel[:, :, :, :].rearrange("p s t e -> p (s t) e"),
                                                     sel[:, :, :, :].rearrange("p s t e -> p (s t) e"),
                                                     v12[u][:, 0:2, :].rearrange("p s t -> p (s t)").unsqueeze(2)
                                                     .broadcast_to([P, 2 * TB, NE]), ALU.mult))
                        link(nc.vector.tensor_tensor(gate[u][:, :, :], r0, r1, ALU.add))
                        assert link.n == perg, link.n
                        dve.sem_inc(sem("gated"), 1)
                        for e in range(NE):
                            dve.wait_ge(sem("y_ps"), ex(i, u, e))
                            dve.wait_ge(sem("acc"), ex(i, u, e))
                            nc.vector.tensor_tensor(term[e % 2][:, :, :],
                                                    ps[4 + e % 2][:, :].rearrange("p (t d) -> p t d", d=V),
                                                    gate[u][:, :, e:e + 1].broadcast_to([P, TB, V]), ALU.mult) \
                                .then_inc(sem("term"), 1)
                        dve.wait_ge(sem("b2_ps"), up(i, u))
                        dve.wait_ge(sem("acc"), NE * up(i, u) + 2)
                        dve.wait_ge(sem(f"stored{u}"), 16 * i + 16)
                        nc.vector.tensor_tensor(hout[u][:, :, :].rearrange("p t e -> p (t e)"), pm[:, :],
                                                acc[u][:, :, :].rearrange("p t e -> p (t e)"), ALU.add) \
                            .then_inc(sem("hout"), 1)
                        dve.wait_ge(sem("hout"), up(i, u))
                        dve.sem_inc(sem("acc_free"), 1)

            @block.scalar
            def _(act):
                with act.Fori(0, NIT) as i:
                    for u in range(2):
                        act.wait_ge(sem("xT_ps"), up(i, u))
                        nc.scalar.copy(xT[u][:, :], pt[:, :]).then_inc(sem("xT"), 1)
                        for e in range(NE):
                            act.wait_ge(sem("h_ps"), ex(i, u, e))
                            for q in range(2):
                                nc.scalar.activation(act1[e % 2][:, q, :], ps[2 * (e % 2) + q][:, :], ACT.Gelu,
                                                     bias=b1[:, e:e + 1]).then_inc(sem("act1"), 1)
                            if e == 1:
                                act.wait_ge(sem("dv"), up(i, u))
                                nc.scalar.activation(v12[u][:, 3, :], v12[u][:, 2, :], ACT.Tanh, scale=0.5) \
                                    .then_inc(sem("th"), 1)
                            if e == 5:
                                act.wait_ge(sem("gT_ps"), up(i, u))
                                nc.scalar.copy(gT[u][:, :], pm[0:TB * NE, 0:P]).then_inc(sem("gT"), 1)

            @block.tensor
            def _(pe):
                pe.wait_ge(sem("loaded"), NL[0])
                nc.tensor.transpose(ps[0][:, 0:NE], b1r[:, :], K.ident[0:NE, 0:NE])
                for e in range(NE):
                    nc.tensor.matmul(ps[1][:, e:e + 1], w1[0:V, e, :], bet[:, 0:1], start=True, stop=True)
                nc.tensor.matmul(ps[2][:, 0:NE], bet[:, 0:1].broadcast_to([V, P]), wr[0:V, :],
                                 start=True, stop=True).then_inc(sem("setp"), 1)
                pe.wait_ge(sem("set"), 1)

                def first(i, u, e):
                    for q in range(2):
                        hf = slice(q * V, (q + 1) * V)
                        last = nc.tensor.matmul(ps[2 * (e % 2) + q][:, :], w1[hf, e, :], xT[u][hf, :],
                                                start=True, stop=True)
                    last.then_inc(sem("h_ps"), 1)

                with pe.Fori(0, NIT) as i:
                    for u in range(2):
                        pe.wait_ge(sem("xn"), up(i, u))
                        for s in range(TB // 2):
                            last = nc.tensor.transpose(pt[:, s * P:(s + 1) * P],
                                                       xn[u][:, 2 * s:2 * s + 2, :].rearrange("p q e -> p (q e)"),
                                                       K.ident[:, :])
                        last.then_inc(sem("xT_ps"), 1)
                        pe.wait_ge(sem("xT"), up(i, u))
                        for s in range(TB // 2):
                            last = nc.tensor.matmul(pt[:, 2 * s * NE:2 * (s + 1) * NE], xT[u][:, s * P:(s + 1) * P],
                                                    wrg[:, :, :].rearrange("p q e -> p (q e)"), start=True, stop=True)
                        last.then_inc(sem("lg_ps"), 1)
                        first(i, u, 0)
                        for e in range(NE):
                            if e + 1 < NE:
                                first(i, u, e + 1)
                            if e == 4:
                                pe.wait_ge(sem("gated"), up(i, u))
                                wait_alone(pe, sem("acc_free"), up(i, u) + 1, sem("pe_passed"))
                                nc.tensor.transpose(pm[0:TB * NE, 0:P], gate[u][:, :, :].rearrange("p t e -> p (t e)"),
                                                    K.ident[:, :]).then_inc(sem("gT_ps"), 1)
                            if e == 7:
                                pe.wait_ge(sem("gT"), up(i, u))
                                nc.tensor.matmul(pm[:, :], gT[u][:, :], b2bd[:, :, :].rearrange("p t e -> p (t e)"),
                                                 start=True, stop=True).then_inc(sem("b2_ps"), 1)
                            pe.wait_ge(sem("act1"), 2 * ex(i, u, e))
                            pe.wait_ge(sem("term"), ex(i, u, e))
                            for t in range(TB):
                                s, q = t // 2, t % 2
                                last = nc.tensor.matmul(ps[4 + e % 2][:, t * V:(t + 1) * V],
                                                        act1[e % 2][:, q, s * P:(s + 1) * P], w2[:, e, :],
                                                        start=True, stop=True)
                            last.then_inc(sem("y_ps"), 1)


def build(nc, a, out):
    with ExitStack() as ctx:
        K = Consts()
        K.ident = ctx.enter_context(nc.sbuf_tensor("ident", [P, P], F32))
        K.onesD = ctx.enter_context(nc.sbuf_tensor("onesD", [P, P], F32))
        K.eps = ctx.enter_context(nc.sbuf_tensor("eps", [P, 1], F32))
        K.mhalf = ctx.enter_context(nc.sbuf_tensor("mhalf", [P, 1], F32))
        made = ctx.enter_context(nc.semaphore("consts"))
        with nc.Block() as block:
            @block.gpsimd
            def _(pool):
                nc.gpsimd.memset(K.ident[:, :], 0.0).then_inc(made, 1)
                pool.wait_ge(made, 1)
                nc.gpsimd.affine_select(out=K.ident[:, :], in_=K.ident[:, :], compare_op=ALU.not_equal, fill=1.0,
                                        base=0, pattern=[[-1, P]], channel_multiplier=1).then_inc(made, 1)

            @block.vector
            def _(dve):
                nc.vector.memset(K.onesD[:, :], 1.0 / D)
                nc.vector.memset(K.mhalf[:, :], -0.5)
                nc.vector.memset(K.eps[:, :], EPS)
        ext = nc.dram_tensor("ext_table", (HEADS, 2 * P - 1), F32, kind="Internal").ap()
        h0 = nc.dram_tensor("h_tower", (NTOK, V), F32, kind="Internal").ap()
        h1 = nc.dram_tensor("h_attn0", (NTOK, V), F32, kind="Internal").ap()
        h2 = nc.dram_tensor("h_ffn0", (NTOK, V), F32, kind="Internal").ap()
        h3 = nc.dram_tensor("h_attn1", (NTOK, V), F32, kind="Internal").ap()

        def sb(n, shape):
            return ctx.enter_context(nc.sbuf_tensor(n, shape, F32))
        F = Consts()
        F.w1, F.w2, F.wo = sb("f0_w1", [P, NE, V]), sb("f0_w2", [P, NPAIR, P]), sb("f0_wo", [P, NPAIR, V])
        F.s, F.t1, F.t2, F.nt2 = sb("f0_s", [P, 2, NPAIR]), sb("f0_t1", [P, NPAIR]), sb("f0_t2", [P, NPAIR]), \
            sb("f0_nt2", [P, NPAIR])
        F.gate, F.corr = sb("f0_gate", [P, NPAIR, 2, P]), sb("f0_corr", [P, 2, V])
        A0, A1 = attention_weights(nc, a, K, ext, ctx)
        chunk_tower(nc, a, h0, K)
        attention(nc, "a0", K, A0, h0, h1, False)
        ffn0_gate(nc, a, K, F, h1)
        ffn0(nc, K, F, h1, h2)
        attention(nc, "a1", K, A1, h2, h3, True)
        ffn1(nc, a, K, h3, out.rearrange("s l e -> (s l) e"))


def kernel(**inputs):
    import numpy as np
    import concourse.bacc as bacc
    from concourse.bass_utils import run_bass_kernel_spmd as run

    nc = bacc.Bacc("TRN2", target_bir_lowering=False, num_devices=1)
    arrays, args = {}, {}
    for name, x in inputs.items():
        x = np.ascontiguousarray(x)
        arrays["in_" + name] = x
        args[name] = nc.dram_tensor("in_" + name, x.shape, mybir.dt.from_np(x.dtype), kind="ExternalInput").ap()
    out = nc.dram_tensor("h_out", (SEQ, L, V), F32, kind="ExternalOutput").ap()
    build(nc, args, out)
    r = run(nc, [arrays], core_ids=[0])
    return r.results[0]["h_out"]
```

```python
import concourse.bass as bass
from concourse import mybir
from contextlib import ExitStack

F32 = mybir.dt.float32
BF16 = mybir.dt.bfloat16
I32 = mybir.dt.int32
ALU = mybir.AluOpType
ACT = mybir.ActivationFunctionType
AX = mybir.AxisListType

P = 128
V = 64
C = 8
D = 128
NTOK = 16384
SEQ, L = 64, 256
NCH = NTOK // C
CPS = L // C
WIN = 4
NG = NCH // P
KJ = C // 2
EPS = 1e-5


class Signals:

    def __init__(self, nc, prefix):
        self.nc, self.prefix, self.made = nc, prefix, {}

    def __call__(self, name):
        if name not in self.made:
            self.made[name] = self.nc.alloc_semaphore(self.prefix + name)
        return self.made[name]

    def close(self):
        self.nc.clear_and_free_semaphores(list(self.made.values()))
        self.nc.all_engine_barrier()


class Chain:

    def __init__(self, eng, sem, start=0):
        self.eng, self.sem, self.start, self.n = eng, sem, start, 0

    def __call__(self, ins):
        self.n += 1
        ins.then_inc(self.sem, 1)
        self.eng.wait_ge(self.sem, self.start + self.n)


def wait_alone(eng, sem, value, passed):
    eng.wait_ge(sem, value)
    eng.sem_inc(passed, 1)


def in_turns(eng, nit, block):
    with eng.Fori(0, nit - 1) as i:
        block(i, 0, (i, 1))
        block(i, 1, (i + 1, 0))
    block(nit - 1, 0, (nit - 1, 1))
    block(nit - 1, 1, None)


def bcast(ap, shape):
    return ap.broadcast_to(shape)


def vector_rows(a):
    rows = []

    def whole(name, n=1):
        for r in range(n):
            rows.append((name, r, [(slice(0, P), a[name].rearrange("(r p) -> r p", p=P)[r])]))

    for name, n in (("L0_tok_lln_g", 1), ("L0_tok_lln_b", 1), ("L0_tok_lb1", 2), ("L0_tok_lb2", 1),
                    ("L0_tok_pool_b", 1), ("L0_tok_msg_b1", 1), ("L0_tok_msg_b2", 1), ("L0_tok_upd_b1", 1),
                    ("L0_tok_upd_b2", 1), ("L0_tok_mln_g", 1), ("L0_tok_mln_b", 1), ("L0_tok_bc_b", 1),
                    ("L0_tok_fln_g", 1), ("L0_tok_fln_b", 1)):
        whole(name, n)
    return rows


def chunk_tower(nc, a, h_out, K):
    rows = vector_rows(a)
    col = {(name, r): i for i, (name, r, _) in enumerate(rows)}
    NR = len(rows)
    with ExitStack() as ctx:
        def sb(name, shape, dt=F32):
            return ctx.enter_context(nc.sbuf_tensor(name, shape, dt))

        sem = Signals(nc, "tk_")
        ctx.callback(sem.close)

        ident, onesD = K.ident, K.onesD
        vrow = sb("vrow", [NR, P])
        vcol = sb("vcol", [P, NR])
        emb2 = sb("emb2", [P, D])
        posr = sb("posr", [P, KJ, D])
        lw1 = sb("lw1", [P, 2 * D])
        lw2 = sb("lw2", [P, 2, D])
        poolw = sb("poolw", [P, D])
        mw1 = sb("mw1", [P, 2, D])
        mw2 = sb("mw2", [P, D])
        uw1 = sb("uw1", [P, 2, D])
        uw2 = sb("uw2", [P, D])
        bcw = sb("bcw", [P, D])
        head = sb("head", [P, V])
        xi = sb("xi", [P, NG, C], I32)
        xf = sb("xf", [P, NG, C])
        xT = sb("xT", [P, P])
        vp = sb("vp", [P, 1])
        viota = sb("viota", [P, C, V])
        icnt = sb("icnt", [P, CPS])
        epost = sb("epost", [P, KJ, D])
        exc = sb("exc", [P, KJ, D])
        est = sb("est", [P, 3, KJ])
        exT = sb("exT", [P, KJ * P])
        g1 = sb("g1", [P, 2, KJ * P])
        TT = sb("TT", [P, KJ * P])
        TTc = sb("TTc", [P, KJ * P])
        Tp = sb("Tp", [P, KJ, D])
        Tl = sb("Tl", [P, KJ, 2, V])
        vTs = sb("vTs", [P, KJ, C])
        gh = sb("gh", [P, V])
        wl = sb("wl", [P, V])
        frow = sb("frow", [P, V])
        OH = sb("OH", [P, KJ, NCH])
        mw1t = sb("mw1t", [P, P])
        mw2T = sb("mw2T", [P, D])
        w21 = sb("w21", [P, D])
        bu1 = sb("bu1", [P, 1])
        hm = sb("hm", [P, NCH])
        pb = [ctx.enter_context(nc.psum_tensor(f"tkps{b}", [P, 512], F32)) for b in range(8)]

        def vc(name, r=0):
            c = col[(name, r)]
            return vcol[:, c:c + 1]

        NLOAD = 0
        with nc.Block() as block:
            @block.sync
            def _(sp):
                ld = sem("loaded")
                sp.wait_ge(sem("vrow0"), 1)
                n = 0

                def load(dst, src):
                    nonlocal n
                    sp.dma_start(dst, src).then_inc(ld, 16)
                    n += 1
                for j in range(2):
                    load(emb2[j * V:(j + 1) * V, :], a["L0_tok_emb"])
                    load(posr[j * V:(j + 1) * V, :, :],
                         a["L0_tok_pos"].rearrange("(k j) d -> j k d", j=2)[j].partition_broadcast(V))
                for i, (name, r, parts) in enumerate(rows):
                    for s, src in parts:
                        load(vrow[i:i + 1, s], src.unsqueeze(0))
                load(lw1[:, :], a["L0_tok_lw1"])
                load(lw2[:, :, :], a["L0_tok_lw2"].rearrange("(k p) n -> p k n", p=P))
                load(poolw[:, :], a["L0_tok_pool_w"])
                load(mw1[:, :, :], a["L0_tok_msg_w1"].rearrange("(k p) n -> p k n", p=P))
                load(mw2[:, :], a["L0_tok_msg_w2"])
                load(uw1[:, :, :], a["L0_tok_upd_w1"].rearrange("(k p) n -> p k n", p=P))
                load(uw2[:, :], a["L0_tok_upd_w2"])
                load(bcw[:, :], a["L0_tok_bc_w"])
                load(head[:, :], a["L0_tok_head_w"])
                load(xi[:, :, :], a["x"].rearrange("s l -> (s l)").rearrange("(g n c) -> n g c", n=P, c=C))
                assert n == 5 + NR + 9, n
            NLOAD = 16 * (5 + NR + 9)

            @block.gpsimd
            def _(pool):
                pool.iota(viota[:, :, :], pattern=[[0, C], [1, V]], base=0, channel_multiplier=0,
                          allow_small_or_imprecise_dtypes=True).then_inc(sem("iota"), 1)
                for j in range(2):
                    pool.wait_ge(sem("iota"), j + 1)
                    pool.iota(vp[j * V:(j + 1) * V, :], pattern=[[0, 1]], base=0, channel_multiplier=1,
                              allow_small_or_imprecise_dtypes=True).then_inc(sem("iota"), 1)
                pool.wait_ge(sem("iota"), 3)
                pool.wait_ge(sem("evar"), 1)
                nc.gpsimd.tensor_tensor(est[:, 2, :], est[:, 1, :], K.mhalf[:, 0:1].broadcast_to([P, KJ]), ALU.pow) \
                    .then_inc(sem("erstd"), 1)

            @block.vector
            def _(dve):
                step = Chain(dve, sem("dve"))
                step(nc.vector.memset(vrow[:, :], 0.0))
                dve.sem_inc(sem("vrow0"), 1)
                for i in range(CPS):
                    nc.vector.memset(icnt[:, i:i + 1] if i < WIN else icnt[:, i:], 1.0 / min(i + 1, WIN + 1)) \
                        .then_inc(sem("icnt"), 1)
                    if i == WIN:
                        break
                step(nc.vector.memset(Tl[:, :, :, :], 0.0))
                step(nc.vector.memset(vTs[:, :, :], 0.0))
                dve.wait_ge(sem("vcolp"), 1)
                step(nc.vector.tensor_copy(vcol[:, :], pb[0][:, 0:NR]))
                dve.sem_inc(sem("vcol"), 1)
                step(nc.vector.tensor_tensor(epost[:, :, :], posr[:, :, :],
                                             emb2[:, :].unsqueeze(1).broadcast_to([P, KJ, D]), ALU.add))
                dve.sem_inc(sem("epos"), 1)
                step(nc.vector.tensor_reduce(est[:, 0, :], epost[:, :, :], AX.X, ALU.add))
                step(nc.vector.tensor_scalar(est[:, 1, :], est[:, 0, :], 1.0 / D, None, ALU.mult))
                step(nc.vector.tensor_tensor(exc[:, :, :], epost[:, :, :],
                                             est[:, 1, :].unsqueeze(2).broadcast_to([P, KJ, D]), ALU.subtract))
                step(nc.vector.tensor_tensor(g1[:, 0, :].rearrange("p (k d) -> p k d", k=KJ), exc[:, :, :],
                                             exc[:, :, :], ALU.mult))
                step(nc.vector.tensor_reduce(est[:, 0, :], g1[:, 0, :].rearrange("p (k d) -> p k d", k=KJ),
                                             AX.X, ALU.add))
                step(nc.vector.tensor_scalar(est[:, 1, :], est[:, 0, :], 1.0 / D, EPS, ALU.mult, ALU.add))
                dve.sem_inc(sem("evar"), 1)
                dve.wait_ge(sem("erstd"), 1)
                step(nc.vector.tensor_tensor(exc[:, :, :], exc[:, :, :],
                                             est[:, 2, :].unsqueeze(2).broadcast_to([P, KJ, D]), ALU.mult))
                dve.sem_inc(sem("exn"), 1)
                dve.wait_ge(sem("exTp"), 1)
                step(nc.vector.tensor_scalar(exT[:, :], pb[1][:, :], vc("L0_tok_lln_g"), vc("L0_tok_lln_b"),
                                             ALU.mult, ALU.add))
                dve.sem_inc(sem("exT"), 1)
                dve.wait_ge(sem("eTp"), 1)
                step(nc.vector.tensor_scalar(TT[:, :], pb[2][:, :], vc("L0_tok_lb2"), None, ALU.add))
                step(nc.vector.tensor_scalar(gh[:, :], head[:, :], vc("L0_tok_fln_g"), None, ALU.mult))
                dve.sem_inc(sem("gh"), 1)
                dve.wait_ge(sem("ghm"), 1)
                step(nc.vector.tensor_tensor(wl[:, :], gh[:, :], pb[3][:, 0:V], ALU.subtract))
                step(nc.vector.tensor_copy(frow[:, :], pb[3][:, V:2 * V]))
                step(nc.vector.tensor_copy(mw2T[:, :], pb[4][:, 0:D]))
                dve.sem_inc(sem("mw2T"), 1)
                dve.wait_ge(sem("w21p"), 1)
                step(nc.vector.tensor_copy(w21[:, :], pb[7][:, 0:D]))
                step(nc.vector.tensor_tensor(bu1[:, :], pb[7][:, D:D + 1], vc("L0_tok_upd_b1"), ALU.add))
                dve.wait_ge(sem("tlp"), 1)
                step(nc.vector.tensor_tensor(TT[:, :], TT[:, :], pb[5][:, :], ALU.add))
                dve.sem_inc(sem("TT"), 1)
                dve.wait_ge(sem("TTm"), 1)
                step(nc.vector.tensor_tensor(TTc[:, :], TT[:, :], pb[6][:, :], ALU.subtract))
                step(nc.vector.tensor_tensor(g1[:, 0, :], TTc[:, :], TTc[:, :], ALU.mult))
                dve.sem_inc(sem("TTq"), 1)
                dve.wait_ge(sem("tabs"), 1)
                step(nc.vector.tensor_copy(Tp[:, :, :].rearrange("p k d -> p (k d)"), pb[1][:, :]))
                for j in range(2):
                    hf = slice(j * V, (j + 1) * V)
                    step(nc.vector.tensor_copy(Tl[hf, :, j, :],
                                               pb[2][hf, 0:KJ * V].rearrange("p (k e) -> p k e", k=KJ)))
                    for k in range(KJ):
                        step(nc.vector.tensor_copy(vTs[hf, k, 2 * k + j:2 * k + j + 1], pb[3][hf, k:k + 1]))
                dve.sem_inc(sem("tabsb"), 1)
                step(nc.vector.tensor_copy(xf[:, :, :], xi[:, :, :]))
                dve.sem_inc(sem("xf"), 1)
                dve.wait_ge(sem("xTp"), 1)
                step(nc.vector.tensor_copy(xT[:, :], pb[0][:, 0:P]))
                dve.sem_inc(sem("xT"), 1)
                dve.wait_ge(sem("iota"), 3)
                for g in range(NG):
                    dve.wait_ge(sem("xb"), g + 1)
                    nc.vector.tensor_scalar(OH[:, :, g * P:(g + 1) * P],
                                            pb[4 + g % 4][:, :].rearrange("p (k n) -> p k n", k=KJ),
                                            vp[:, 0:1], None, ALU.is_equal).then_inc(sem("oh"), 1)
                for b in range(4):
                    dve.wait_ge(sem("summ"), b + 1)
                    nc.vector.tensor_scalar(hm[:, b * 512:(b + 1) * 512], pb[b][:, :], 1.0 / C,
                                            vc("L0_tok_pool_b"), ALU.mult, ALU.add).then_inc(sem("hm"), 1)

            @block.scalar
            def _(act):
                for c in range(2):
                    act.wait_ge(sem("g1p"), c + 1)
                    nc.scalar.activation(g1[:, c, :], pb[6 + c][:, :], ACT.Gelu, bias=vc("L0_tok_lb1", c)) \
                        .then_inc(sem("g1"), 1)

            @block.tensor
            def _(pe):
                pe.wait_ge(sem("loaded"), NLOAD)
                nc.tensor.transpose(pb[0][:, 0:NR], vrow[:, :], ident[0:NR, 0:NR]).then_inc(sem("vcolp"), 1)
                pe.wait_ge(sem("exn"), 1)
                for k in range(KJ):
                    nc.tensor.transpose(pb[2][:, k * P:(k + 1) * P], epost[:, k, :], ident[:, :])
                    last = nc.tensor.transpose(pb[1][:, k * P:(k + 1) * P], exc[:, k, :], ident[:, :])
                last.then_inc(sem("exTp"), 1)
                pe.sem_inc(sem("eTp"), 1)
                pe.wait_ge(sem("exT"), 1)
                for c in range(2):
                    nc.tensor.matmul(pb[6 + c][:, :], lw1[:, c * D:(c + 1) * D], exT[:, :],
                                     start=True, stop=True).then_inc(sem("g1p"), 1)
                pe.wait_ge(sem("gh"), 1)
                nc.tensor.matmul(pb[3][:, 0:V], onesD[:, :], gh[:, :], start=True, stop=True)
                nc.tensor.matmul(pb[3][:, V:2 * V], bcast(vc("L0_tok_fln_b"), [P, P]), head[:, :],
                                 start=True, stop=True)
                nc.tensor.transpose(pb[4][:, 0:D], mw2[:, :], ident[:, :]).then_inc(sem("ghm"), 1)
                for c in range(2):
                    pe.wait_ge(sem("g1"), c + 1)
                    last = nc.tensor.matmul(pb[5][:, :], lw2[:, c, :], g1[:, c, :], start=c == 0, stop=c == 1)
                last.then_inc(sem("tlp"), 1)
                pe.wait_ge(sem("mw2T"), 1)
                nc.tensor.matmul(pb[7][:, 0:D], mw2T[:, :], uw1[:, 1, :], start=True, stop=True)
                nc.tensor.matmul(pb[7][:, D:D + 1], uw1[:, 1, :], vc("L0_tok_msg_b2"),
                                 start=True, stop=True).then_inc(sem("w21p"), 1)
                pe.wait_ge(sem("TT"), 1)
                nc.tensor.matmul(pb[6][:, :], onesD[:, :], TT[:, :], start=True, stop=True).then_inc(sem("TTm"), 1)
                pe.wait_ge(sem("TTq"), 1)
                for k in range(KJ):
                    sl = TT[:, k * P:(k + 1) * P]
                    nc.tensor.matmul(pb[1][:, k * D:(k + 1) * D], sl, poolw[:, :], start=True, stop=True)
                    nc.tensor.matmul(pb[2][:, k * V:(k + 1) * V], sl, wl[:, :], start=True, stop=True)
                    last = nc.tensor.matmul(pb[3][:, k:k + 1], g1[:, 0, k * P:(k + 1) * P], onesD[:, 0:1],
                                            start=True, stop=True)
                last.then_inc(sem("tabs"), 1)
                pe.wait_ge(sem("xf"), 1)
                nc.tensor.transpose(pb[0][:, 0:P], xf[:, :, :].rearrange("p g c -> p (g c)"), ident[:, :]) \
                    .then_inc(sem("xTp"), 1)
                pe.wait_ge(sem("xT"), 1)
                for g in range(NG):
                    if g >= 4:
                        pe.wait_ge(sem("oh"), g - 3)
                    for k in range(KJ):
                        for j in range(2):
                            r = g * C + 2 * k + j
                            last = nc.tensor.matmul(pb[4 + g % 4][j * V:(j + 1) * V, k * P:(k + 1) * P],
                                                    ident[:, r:r + 1].broadcast_to([P, V]), xT[:, :],
                                                    start=True, stop=True)
                    last.then_inc(sem("xb"), 1)
                pe.wait_ge(sem("oh"), NG)
                pe.wait_ge(sem("tabsb"), 1)
                for b in range(4):
                    for k in range(KJ):
                        last = nc.tensor.matmul(pb[b][:, :], Tp[:, k, :], OH[:, k, b * 512:(b + 1) * 512],
                                                start=k == 0, stop=k == KJ - 1)
                    last.then_inc(sem("summ"), 1)
        tower_rounds(nc, sem, pb, K, icnt, vc, mw1, w21, uw1, uw2, bu1, hm, sb)
        tower_logits(nc, sem, pb, K, vc, bcw, TTc, wl, OH, Tl, vTs, frow, hm, xf, viota, h_out, sb)


def tower_rounds(nc, sem, pb, K, icnt, vc, mw1, w21, uw1, uw2, bu1, hm, sb):
    NB, W = 4, NCH // 4
    SB = W // CPS
    selfp = [sb(f"selfp{i}", [P, W]) for i in range(4)]
    gel = [sb(f"gel{i}", [P, WIN + 1, W]) for i in range(2)]
    agg = [sb(f"agg{i}", [P, W]) for i in range(2)]
    ug = [sb(f"ug{i}", [P, W]) for i in range(4)]
    res = [sb(f"res{i}", [P, W]) for i in range(4)]
    sq = [sb(f"sqr{i}", [P, W]) for i in range(4)]
    rcol = [sb(f"rcol{i}", [P, W // P]) for i in range(4)]
    blk = [slice(b * W, (b + 1) * W) for b in range(NB)]

    def seqs(ap):
        return ap.rearrange("p (s c) -> p s c", c=CPS)

    with nc.Block() as block:
        @block.tensor
        def _(pe):
            with pe.Fori(0, 3) as r:
                at = lambda b: r * NB + b + 1
                for b in range(NB):
                    pe.wait_ge(sem("hm"), at(b))
                    nc.tensor.matmul(pb[2 * b][:, :], mw1[:, 0, :], hm[:, blk[b]], start=True, stop=True)
                    nc.tensor.matmul(pb[2 * b + 1][:, :], mw1[:, 1, :], hm[:, blk[b]], start=True, stop=True) \
                        .then_inc(sem("msgp"), 1)
                for b in range(NB):
                    pe.wait_ge(sem("added"), at(b))
                    nc.tensor.matmul(pb[2 * b][:, :], uw1[:, 0, :], hm[:, blk[b]], start=True, stop=False)
                    pe.wait_ge(sem("agg"), at(b))
                    nc.tensor.matmul(pb[2 * b][:, :], w21[:, :], agg[b % 2][:, :], start=False, stop=True) \
                        .then_inc(sem("updp"), 1)
                for b in range(NB):
                    pe.wait_ge(sem("ug"), at(b))
                    nc.tensor.matmul(pb[2 * b + 1][:, :], uw2[:, :], ug[b][:, :], start=True, stop=True) \
                        .then_inc(sem("upd2p"), 1)
                for b in range(NB):
                    pe.wait_ge(sem("res"), at(b))
                    nc.tensor.matmul(pb[2 * b][:, :], K.onesD[:, :], res[b][:, :], start=True, stop=True) \
                        .then_inc(sem("meanp"), 1)
                for b in range(NB):
                    pe.wait_ge(sem("sq"), at(b))
                    for k in range(W // P):
                        last = nc.tensor.matmul(pb[2 * b + 1][:, k:k + 1], sq[b][:, k * P:(k + 1) * P],
                                                K.onesD[:, 0:1], start=True, stop=True)
                    last.then_inc(sem("varp"), 1)
                for b in range(NB):
                    pe.wait_ge(sem("rs"), at(b))
                    for k in range(W // P):
                        last = nc.tensor.matmul(pb[2 * b + 1][:, k * P:(k + 1) * P],
                                                bcast(rcol[b][:, k:k + 1], [P, P]), K.ident[:, :],
                                                start=True, stop=True)
                    last.then_inc(sem("rsp"), 1)

        @block.scalar
        def _(act):
            with act.Fori(0, 3) as r:
                at = lambda b: r * NB + b + 1
                for b in range(NB):
                    act.wait_ge(sem("msgp"), at(b))
                    nc.scalar.activation(selfp[b][:, :], pb[2 * b][:, :], ACT.Identity,
                                         bias=vc("L0_tok_msg_b1")).then_inc(sem("selfp"), 1)
                for b in range(NB):
                    act.wait_ge(sem("added"), at(b))
                    nc.scalar.activation(gel[b % 2][:, :, :], gel[b % 2][:, :, :], ACT.Gelu) \
                        .then_inc(sem("gel"), 1)
                for b in range(NB):
                    act.wait_ge(sem("updp"), at(b))
                    nc.scalar.activation(ug[b][:, :], pb[2 * b][:, :], ACT.Gelu, bias=bu1[:, 0:1]) \
                        .then_inc(sem("ug"), 1)
                for b in range(NB):
                    act.wait_ge(sem("resc"), at(b))
                    nc.scalar.activation(sq[b][:, :], res[b][:, :], ACT.Square).then_inc(sem("sq"), 1)
                for b in range(NB):
                    act.wait_ge(sem("varp"), at(b))
                    nc.scalar.activation(rcol[b][:, :], pb[2 * b + 1][:, 0:W // P], ACT.Sqrt, bias=K.eps[:, 0:1]) \
                        .then_inc(sem("std"), 1)

        @block.gpsimd
        def _(pool):
            step = None
            with pool.Fori(0, 3) as r:
                at = lambda b: r * NB + b + 1
                step = Chain(pool, sem("poolc"), r * (NB * 2))
                for b in range(NB):
                    pool.wait_ge(sem("pairs"), at(b))
                    g = gel[b % 2]
                    for d in range(1, 3):
                        step(nc.gpsimd.tensor_tensor(seqs(g[:, 0, :])[:, :, d:], seqs(g[:, 0, :])[:, :, d:],
                                                     seqs(g[:, d, :])[:, :, d:], ALU.add))
                    pool.wait_ge(sem("updp0"), at(b))
                    nc.gpsimd.tensor_tensor(seqs(agg[b % 2][:, :]), seqs(g[:, 0, :]),
                                            icnt[:, :].unsqueeze(1).broadcast_to([P, SB, CPS]), ALU.mult) \
                        .then_inc(sem("agg"), 1)

        @block.vector
        def _(dve):
            for g in gel:
                nc.vector.memset(g[:, :, :], 0.0).then_inc(sem("gel0"), 1)
            dve.wait_ge(sem("gel0"), 2)
            with dve.Fori(0, 3) as r:
                at = lambda b: r * NB + b + 1

                def pairs(b):
                    g = gel[b % 2]
                    dve.wait_ge(sem("gel"), at(b))
                    nc.vector.tensor_tensor(g[:, 1:3, :], g[:, 1:3, :], g[:, 3:5, :], ALU.add) \
                        .then_inc(sem("pairs"), 1)

                for b in range(NB):
                    if b >= 2:
                        pairs(b - 2)
                    dve.wait_ge(sem("selfp"), at(b))
                    if b >= 2:
                        dve.wait_ge(sem("agg"), at(b - 2))
                    g = gel[b % 2]
                    for d in range(WIN + 1):
                        last = nc.vector.tensor_tensor(seqs(g[:, d, :])[:, :, d:], seqs(selfp[b][:, :])[:, :, d:],
                                                       seqs(pb[2 * b + 1][:, :])[:, :, 0:CPS - d], ALU.add)
                    last.then_inc(sem("added"), 1)
                for b in range(NB - 2, NB):
                    pairs(b)
                for b in range(NB):
                    dve.wait_ge(sem("upd2p"), at(b))
                    nc.vector.scalar_tensor_tensor(res[b][:, :], pb[2 * b + 1][:, :], vc("L0_tok_upd_b2"),
                                                   hm[:, blk[b]], ALU.add, ALU.add).then_inc(sem("res"), 1)
                for b in range(NB):
                    dve.wait_ge(sem("meanp"), at(b))
                    nc.vector.tensor_tensor(res[b][:, :], res[b][:, :], pb[2 * b][:, :], ALU.subtract) \
                        .then_inc(sem("resc"), 1)
                for b in range(NB):
                    dve.wait_ge(sem("std"), at(b))
                    nc.vector.reciprocal(rcol[b][:, :], rcol[b][:, :]).then_inc(sem("rs"), 1)
                for b in range(NB):
                    dve.wait_ge(sem("rsp"), at(b))
                    nc.vector.tensor_tensor(res[b][:, :], res[b][:, :], pb[2 * b + 1][:, :], ALU.mult) \
                        .then_inc(sem("rn"), 1)
                    dve.wait_ge(sem("rn"), at(b))
                    nc.vector.tensor_scalar(hm[:, blk[b]], res[b][:, :], vc("L0_tok_mln_g"), vc("L0_tok_mln_b"),
                                            ALU.mult, ALU.add).then_inc(sem("hm"), 1)

        @block.sync
        def _(sp):
            sp.sem_inc(sem("updp0"), 2)
            for k in range(3 * NB - 2):
                sp.wait_ge(sem("updp"), k + 1)
                sp.sem_inc(sem("updp0"), 1)


def tower_logits(nc, sem, pb, K, vc, bcw, TTc, wl, OH, Tl, vTs, frow, hm, xf, viota, h_out, sb):
    NB, W = 4, NCH // 4
    bct = sb("bct", [P, NCH])
    bcq = sb("bcq", [P, NCH])
    oh = [sb(f"ohn{i}", [P, C, V]) for i in range(2)]
    cov = [sb(f"cov{i}", [P, C, V]) for i in range(2)]
    st = [sb(f"lst{i}", [P, 3, C]) for i in range(2)]
    lg = [sb(f"lg{i}", [P, C, V]) for i in range(2)]
    h_v = h_out.rearrange("(g n c) e -> g n (c e)", n=P, c=C)
    with nc.Block() as block:
        @block.tensor
        def _(pe):
            for b in range(NB):
                nc.tensor.matmul(pb[b][:, :], bcw[:, :], hm[:, b * W:(b + 1) * W],
                                 start=True, stop=True).then_inc(sem("bcp"), 1)
            for b in range(NB):
                pe.wait_ge(sem("bct"), b + 1)
                nc.tensor.matmul(pb[4 + b][:, :], K.onesD[:, :], bct[:, b * W:(b + 1) * W],
                                 start=True, stop=True).then_inc(sem("bcm"), 1)
            pe.wait_ge(sem("bcq"), 4)
            for g in range(NG):
                n = slice(g * P, (g + 1) * P)
                pc, pl, pv = pb[g % 3], pb[3 + g % 3], pb[6 + g % 2]
                if g >= 2:
                    pe.wait_ge(sem("lvar"), g - 1)
                if g >= 3:
                    pe.wait_ge(sem("lg"), g - 2)
                nc.tensor.matmul(pv[:, 0:C], bcq[:, n], bcast(K.onesD[:, 0:1], [P, C]), start=True, stop=False)
                nc.tensor.matmul(pl[:, :].rearrange("p (c e) -> p c e", c=C), bct[:, n],
                                 wl[:, :].unsqueeze(1).broadcast_to([P, C, V]), start=True, stop=False)
                nc.tensor.matmul(pc[:, :], bct[:, n], TTc[:, :], start=True, stop=True)
                for k in range(KJ):
                    nc.tensor.matmul(pv[:, 0:C], OH[:, k, n], vTs[:, k, :], start=False, stop=k == KJ - 1)
                    last = nc.tensor.matmul(pl[:, k * P:(k + 1) * P], OH[:, k, n],
                                            Tl[:, k, :, :].rearrange("p j e -> p (j e)"),
                                            start=False, stop=k == KJ - 1)
                last.then_inc(sem("lgp"), 1)

        @block.scalar
        def _(act):
            for b in range(NB):
                act.wait_ge(sem("bcp"), b + 1)
                nc.scalar.activation(bct[:, b * W:(b + 1) * W], pb[b][:, :], ACT.Identity,
                                     bias=vc("L0_tok_bc_b")).then_inc(sem("bct"), 1)
            for b in range(NB):
                act.wait_ge(sem("bcc"), b + 1)
                nc.scalar.activation(bcq[:, b * W:(b + 1) * W], bct[:, b * W:(b + 1) * W], ACT.Square) \
                    .then_inc(sem("bcq"), 1)

        @block.gpsimd
        def _(pool):
            for g in range(NG):
                st_ = st[g % 2]
                pool.wait_ge(sem("lvar"), g + 1)
                nc.gpsimd.tensor_tensor(st_[:, 2, :], st_[:, 1, :], K.mhalf[:, 0:1].broadcast_to([P, C]), ALU.pow) \
                    .then_inc(sem("lrstd"), 1)

        @block.vector
        def _(dve):
            for b in range(NB):
                dve.wait_ge(sem("bcm"), b + 1)
                nc.vector.tensor_tensor(bct[:, b * W:(b + 1) * W], bct[:, b * W:(b + 1) * W], pb[4 + b][:, :],
                                        ALU.subtract).then_inc(sem("bcc"), 1)
            step = Chain(dve, sem("ldve"))

            def variance(g):
                u = g % 2
                step(nc.vector.tensor_tensor(oh[u][:, :, :], viota[:, :, :],
                                             xf[:, g, :].unsqueeze(2).broadcast_to([P, C, V]), ALU.is_equal))
                dve.wait_ge(sem("lgp"), g + 1)
                nc.vector.tensor_tensor(cov[u][:, :, :], oh[u][:, :, :],
                                        pb[g % 3][:, :].rearrange("p (c e) -> p c e", c=C), ALU.mult) \
                    .then_inc(sem("covm"), 1)
                dve.wait_ge(sem("covm"), g + 1)
                step(nc.vector.tensor_reduce(st[u][:, 0, :], cov[u][:, :, :], AX.X, ALU.add))
                step(nc.vector.scalar_tensor_tensor(st[u][:, 1, :], st[u][:, 0, :], 2.0 / D, pb[6 + u][:, 0:C],
                                                    ALU.mult, ALU.add))
                nc.vector.tensor_scalar(st[u][:, 1, :], st[u][:, 1, :], EPS, None, ALU.add).then_inc(sem("lvar"), 1)

            def logits(g):
                u = g % 2
                dve.wait_ge(sem("lrstd"), g + 1)
                if g >= 2:
                    dve.wait_ge(sem(f"lstored{u}"), 16 * (g // 2))
                step(nc.vector.tensor_tensor(lg[u][:, :, :], pb[3 + g % 3][:, :].rearrange("p (c e) -> p c e", c=C),
                                             st[u][:, 2, :].unsqueeze(2).broadcast_to([P, C, V]), ALU.mult))
                nc.vector.tensor_tensor(lg[u][:, :, :], lg[u][:, :, :],
                                        frow[:, :].unsqueeze(1).broadcast_to([P, C, V]), ALU.add) \
                    .then_inc(sem("lg"), 1)

            variance(0)
            for g in range(NG):
                if g + 1 < NG:
                    variance(g + 1)
                logits(g)

        @block.sync
        def _(sp):
            for g in range(NG):
                sp.wait_ge(sem("lg"), g + 1)
                sp.dma_start(h_v[g], lg[g % 2][:, :, :].rearrange("p c e -> p (c e)")) \
                    .then_inc(sem(f"lstored{g % 2}"), 16)
            for u in range(2):
                sp.wait_ge(sem(f"lstored{u}"), 16 * (NG // 2))


HEADS, HD = 8, 8
NJ = 4
NGRP = HEADS // NJ
Q_SCALE = HD ** -0.5
NPP = HEADS // 2
SLOTS = ((0, 0), (0, 1), (1, 0), (1, 1), (0, 2), (2, 0))
OFF = 8


UNITS = 4
AHEAD = UNITS + 1
ORDER_WIDE = (
    ("load", 4), ("maxima 1", 2), ("queries 0", 3), ("weights 1", 1), ("stack queries 0", 3), ("divide", 0),
    ("scores 2", 2), ("turn out", 0), ("exp 1", 1), ("norm", 4), ("keys 0", 3), ("copy out", 0),
    ("maxima 2", 2), ("weights 2", 1), ("stack keys 0", 3), ("product", 0), ("add bias 2", 1), ("rsqrt", 4),
    ("scores 3", 2), ("maxima 3", 2), ("exp 2", 1), ("weights 3", 1), ("finish", 0), ("turn max", 2),
    ("store", 0), ("scale", 4), ("scores 0", 3), ("copy max", 2), ("add bias 3", 1), ("turn", 4),
    ("copy turned", 4), ("exp 3", 1), ("project", 4), ("maxima 0", 3), ("insert max", 2), ("keep", 4),
    ("values", 1), ("round", 4), ("scores 1", 3), ("split", 4), ("copy values", 1), ("weights 0", 2),
    ("turn values", 1), ("exp 0", 2))
ORDER_NARROW = (
    ("load", 4), ("queries 1", 3), ("divide", 0), ("scores 1", 2), ("norm", 4), ("stack queries 1", 3),
    ("turn out", 0), ("maxima 1", 2), ("copy out", 0), ("rsqrt", 4), ("product", 0), ("keys 0", 3),
    ("weights 1", 1), ("stack keys 0", 3), ("finish", 0), ("scale", 4), ("keep", 4), ("turn", 4),
    ("turn max", 2), ("add bias 1", 1), ("copy turned", 4), ("store", 0), ("copy max", 2), ("project", 4),
    ("tally norm", 0), ("insert max", 2), ("keys 1", 3), ("round", 4), ("tally rsqrt", 0), ("exp 1", 1),
    ("weights 0", 2), ("split", 4), ("stack keys 1", 3), ("scores 0", 3), ("add bias 0", 2), ("queries 0", 4),
    ("tally", 0), ("values", 1), ("stack queries 0", 4), ("maxima 0", 3), ("exp 0", 2))


def in_flight(eng, nit, order, stages):
    def step(i, u, units):
        for name, ahead in order:
            if name in stages and ahead in units:
                stages[name](i + (u + ahead) // UNITS, (u + ahead) % UNITS)

    for u in range(1 - AHEAD, 0):
        step(0, u, range(-u, AHEAD))
    with eng.Fori(0, nit - 1) as i:
        for u in range(UNITS):
            step(i, u, range(AHEAD))
    for u in range(UNITS):
        step(nit - 1, u, range(UNITS - u))


def attention(nc, name, K, A, h_in, h_out, wide, feat):
    T = 2 if wide else 4
    NT = T * P
    NIT = NTOK // NT // UNITS
    W = 64
    VW = 32 if wide else 16
    NS = 4 if wide else 2
    NPQ = 1 if wide else 2
    ORDER = ORDER_WIDE if wide else ORDER_NARROW
    with ExitStack() as ctx:
        def sb(n, shape, dt=F32):
            return [ctx.enter_context(nc.sbuf_tensor(f"{name}_{n}{u}", shape, dt)) for u in range(UNITS)]

        sem = Signals(nc, name + "_")
        ctx.callback(sem.close)

        hin = sb("hin", [P, T, V])
        stat = sb("stat", [P, T, 6])
        mv = sb("mv", [P, T, 2])
        rstd = sb("rstd", [P, 2, T])
        xn = sb("xn", [P, T, V])
        xT = sb("xT", [P, T // 2, P])
        parts = sb("parts", [P, 3, NT], BF16)
        rest = sb("rest", [P, NT])
        qst = sb("qst", [P, NPP, NT], BF16)
        kst = sb("kst", [P, HEADS if wide else NPP, NT], BF16)
        va = sb("va", [P, T, HEADS, VW])
        mx = sb("mx", [P, T, HEADS])
        mrest = sb("mrest", [P, T, HEADS])
        m3 = sb("m3", [P, T, 2, 3, NPP], BF16)
        mT = sb("mT", [3 * HEADS, NT], BF16)
        if wide:
            pr = sb("pr", [P, NS, NPP, NT])
        else:
            pr = sb("pr", [P, NS, HEADS, 2, W])
        oT = sb("oT", [P, NGRP, NT if wide else 1])
        rs = sb("rs", [P, T, HEADS])
        on = sb("on", [P, T, V])
        onT = sb("onT", [P, T // 2, P])
        hres = sb("hres", [P, T, V])
        hout = sb("hout", [P, T, V])
        if not wide:
            tstat, tmv, trs = sb("tstat", [P, T, 6]), sb("tmv", [P, T, 2]), sb("trs", [P, 2, T])
            tn = sb("tn", [P, T, V])
        bank = [ctx.enter_context(nc.psum_tensor(f"{name}_banks{u}", [P, 2, 512], F32)) for u in range(UNITS)]
        flat = [q[:, :, :].rearrange("p b n -> p (b n)") for q in bank]
        hi_v = h_in.rearrange("(i u t p) e -> i u p t e", p=P, t=T, u=UNITS)
        ho_v = h_out.rearrange("(i u t p) e -> i u p t e", p=P, t=T, u=UNITS)
        halves = [slice(64 * q, 64 * q + 64) for q in range(2)]

        def up(i, u):
            return UNITS * i + u + 1

        with nc.Block() as block:
            @block.sync
            def _(sp):
                def insert_max(i, u):
                    sp.wait_ge(sem("mT"), up(i, u))
                    for q in range(2):
                        sp.dma_start(qst[u][64 * q:64 * q + 3, :, :], mT[u][q * 3 * NPP:(q + 1) * 3 * NPP, :]) \
                            .then_inc(sem(f"max{u}"), 16)

                def store(i, u):
                    sp.wait_ge(sem("hout"), up(i, u))
                    sp.dma_start(ho_v[i, u], hout[u][:, :, :]).then_inc(sem(f"stored{u}"), 16)

                in_flight(sp, NIT, ORDER, {"insert max": insert_max, "store": store})
                for u in range(UNITS):
                    sp.wait_ge(sem(f"stored{u}"), 16 * (NIT + 1))

            @block.gpsimd
            def _(pool):
                def load(i, u):
                    pool.wait_ge(sem("hin_seen"), up(i, u))
                    pool.wait_ge(sem("hin_kept"), up(i, u))
                    pool.dma_start(hin[u][:, :, :], hi_v[i, u]).then_inc(sem(f"hin{u}"), 16)

                def rsqrt(i, u):
                    pool.wait_ge(sem("var"), up(i, u))
                    nc.gpsimd.tensor_tensor(rstd[u][:, 1, :], rstd[u][:, 0, :],
                                            K.mhalf[:, 0:1].broadcast_to([P, T]), ALU.pow).then_inc(sem("rstd"), 1)

                def keep(i, u):
                    pool.wait_ge(sem("hres_free"), up(i, u))
                    nc.gpsimd.tensor_tensor(hres[u][:, :, :], hin[u][:, :, :],
                                            A.brow[:, :].unsqueeze(1).broadcast_to([P, T, V]), ALU.add) \
                        .then_inc(sem("hin_kept"), 1)

                def tally_rsqrt(i, u):
                    pool.wait_ge(sem("tvar"), up(i, u))
                    nc.gpsimd.tensor_tensor(trs[u][:, 1, :], trs[u][:, 0, :],
                                            K.mhalf[:, 0:1].broadcast_to([P, T]), ALU.pow).then_inc(sem("trs"), 1)

                if wide:
                    for u in range(UNITS):
                        nc.gpsimd.memset(kst[u][:, :, :], 0.0).then_inc(sem("kst0"), 1)
                pool.sem_inc(sem("hin_kept"), UNITS)
                in_flight(pool, NIT, ORDER, {"load": load, "rsqrt": rsqrt, "keep": keep, "tally rsqrt": tally_rsqrt})

            @block.vector
            def _(dve):
                per = 2 * T + 2

                def norm(i, u):
                    step = Chain(dve, sem("ln"), (UNITS * i + u) * per)
                    dve.wait_ge(sem(f"hin{u}"), 16 * i + 16)
                    for t in range(T):
                        nc.vector.bn_stats(stat[u][:, t, :], hin[u][:, t, :]).then_inc(sem("ln"), 1)
                        step.n += 1
                    wait_alone(dve, sem("ln"), step.start + step.n, sem("dve_passed"))
                    for t in range(T):
                        nc.vector.bn_aggr(mv[u][:, t, :], stat[u][:, t, :]).then_inc(sem("ln"), 1)
                        step.n += 1
                    dve.wait_ge(sem("ln"), step.start + step.n)
                    nc.vector.tensor_scalar(rstd[u][:, 0, :], mv[u][:, :, 1], EPS, None, ALU.add) \
                        .then_inc(sem("var"), 1)
                    nc.vector.tensor_tensor(xn[u][:, :, :], hin[u][:, :, :],
                                            mv[u][:, :, 0:1].broadcast_to([P, T, V]), ALU.subtract) \
                        .then_inc(sem("ln"), 1)
                    step.n += 1

                def scale(i, u):
                    step = Chain(dve, sem("ln"), (UNITS * i + u) * per + per - 1)
                    dve.wait_ge(sem("ln"), step.start)
                    dve.wait_ge(sem("rstd"), up(i, u))
                    step(nc.vector.tensor_tensor(xn[u][:, :, :], xn[u][:, :, :],
                                                 rstd[u][:, 1, :].unsqueeze(2).broadcast_to([P, T, V]),
                                                 ALU.mult))
                    dve.sem_inc(sem("hin_seen"), 1)
                    dve.sem_inc(sem("xn"), 1)

                def split(i, u):
                    dve.wait_ge(sem("part0"), up(i, u))
                    link = Chain(dve, sem("split"), 2 * (UNITS * i + u))
                    link(nc.vector.scalar_tensor_tensor(rest[u][:, :], flat[u][:, 0:NT], A.qkb[:, 0:1],
                                                        parts[u][:, 0, :], ALU.add, ALU.subtract))
                    link(nc.vector.tensor_copy(parts[u][:, 1, :], rest[u][:, :]))
                    nc.vector.tensor_tensor(parts[u][:, 2, :], rest[u][:, :], parts[u][:, 1, :],
                                            ALU.subtract).then_inc(sem("parts"), 1)
                    dve.wait_ge(sem("v_ps"), up(i, u))
                    nc.vector.tensor_copy(va[u][:, :, :, 1:HD + 1],
                                          flat[u][:, 512:512 + T * V].rearrange(
                                              "p (t h d) -> p t h d", t=T, h=HEADS)).then_inc(sem("va"), 1)

                def maxima(s):
                    def stage(i, u):
                        dve.wait_ge(sem(f"s{s}_ps"), up(i, u))
                        if wide:
                            t, c = divmod(s, 2)
                            f = flat[u].rearrange("p (h m) -> p h m", m=NT)
                            if t == 0:
                                blk = f[:, :, P:]
                                nc.vector.tensor_tensor(blk, blk, A.biasS[:, c * NPP:(c + 1) * NPP, :], ALU.add) \
                                    .then_inc(sem(f"s_bias{s}"), 1)
                                dve.wait_ge(sem(f"s_bias{s}"), up(i, u))
                            nc.vector.tensor_reduce(mx[u][:, t, c * NPP:(c + 1) * NPP], f, AX.X, ALU.max) \
                                .then_inc(sem(f"m{s}"), 1)
                        else:
                            blk = flat[u].rearrange("p (h m) -> p h m", m=W)
                            nc.vector.tensor_tensor(blk, blk,
                                                    A.biasS[:, :].unsqueeze(1).broadcast_to([P, 1024 // W, W]),
                                                    ALU.add).then_inc(sem(f"s_bias{s}"), 1)
                            dve.wait_ge(sem(f"s_bias{s}"), up(i, u))
                            nc.vector.tensor_reduce(mx[u][:, 2 * s:2 * s + 2, :].rearrange("p t h -> p h t"),
                                                    flat[u].rearrange("p (h t m) -> p h t m", h=HEADS, t=2),
                                                    AX.X, ALU.max).then_inc(sem(f"m{s}"), 1)
                        if s == NS - 1:
                            split_max(i, u)
                    return stage

                def split_max(i, u):
                    dve.wait_ge(sem(f"m{NS - 1}"), up(i, u))
                    link = Chain(dve, sem("msplit"), 3 * (UNITS * i + u))

                    def part(r):
                        return m3[u][:, :, :, r, :].rearrange("p t q h -> p (t q) h")

                    def heads(tile):
                        return tile[u][:, :, :].rearrange("p t (q h) -> p (t q) h", q=2)
                    link(nc.vector.tensor_scalar(part(0), heads(mx), -1.0, None, ALU.mult))
                    link(nc.vector.scalar_tensor_tensor(heads(mrest), heads(mx), -1.0, part(0),
                                                        ALU.mult, ALU.subtract))
                    link(nc.vector.tensor_copy(part(1), heads(mrest)))
                    nc.vector.tensor_tensor(part(2), heads(mrest), part(1), ALU.subtract).then_inc(sem("max_parts"), 1)

                def add_bias(s):
                    def stage(i, u):
                        dve.wait_ge(sem(f"t{s}_ps"), up(i, u))
                        if wide:
                            blk = flat[u].rearrange("p (h m) -> p h m", m=NT)[:, :, 0:P]
                            bias = A.biasT[:, s % 2 * NPP:(s % 2 + 1) * NPP, :]
                        else:
                            blk = flat[u].rearrange("p (h m) -> p h m", m=W)
                            bias = A.biasT[:, :].unsqueeze(1).broadcast_to([P, 1024 // W, W])
                        nc.vector.tensor_tensor(blk, blk, bias, ALU.add).then_inc(sem(f"t_bias{s}"), 1)
                    return stage

                def divide(i, u):
                    dve.wait_ge(sem("o_ps"), up(i, u))
                    if wide:
                        o = flat[u][:, 512:].rearrange("p (t h s) -> p t h s", t=T, s=VW)
                        todo = [(slice(0, P), o)]
                    else:
                        todo = [(halves[q], bank[u][halves[q], q, :].rearrange("p (t h s) -> p t h s", t=T, s=VW))
                                for q in range(2)]
                    for r, o in todo:
                        nc.vector.reciprocal(rs[u][r, :, :], o[:, :, :, 0]).then_inc(sem("rs"), 1)
                    dve.wait_ge(sem("rs"), len(todo) * up(i, u))
                    for r, o in todo:
                        nc.vector.tensor_tensor(
                            on[u][r, :, :].rearrange("p t (h d) -> p t h d", d=HD), o[:, :, :, 1:HD + 1],
                            rs[u][r, :, :].unsqueeze(3).broadcast_to([r.stop - r.start, T, HEADS, HD]),
                            ALU.mult).then_inc(sem("on"), 1)

                def finish(i, u):
                    dve.wait_ge(sem("y_ps"), up(i, u))
                    dve.wait_ge(sem("hin_kept"), up(i, u) + UNITS)
                    dve.wait_ge(sem(f"stored{u}"), 16 * i + 16)
                    nc.vector.tensor_tensor(hout[u][:, :, :].rearrange("p t e -> p (t e)"),
                                            flat[u][:, 512:512 + T * V],
                                            hres[u][:, :, :].rearrange("p t e -> p (t e)"), ALU.add) \
                        .then_inc(sem("hout"), 1)
                    dve.wait_ge(sem("hout"), up(i, u))
                    dve.sem_inc(sem("hres_free"), 1)
                    dve.sem_inc(sem("quad_free"), 1)

                def tally_norm(i, u):
                    link = Chain(dve, sem("tally"), (UNITS * i + u) * TPER)
                    for t in range(T):
                        nc.vector.bn_stats(tstat[u][:, t, :], hout[u][:, t, :]).then_inc(sem("tally"), 1)
                    wait_alone(dve, sem("tally"), link.start + T, sem("dve_passed"))
                    for t in range(T):
                        nc.vector.bn_aggr(tmv[u][:, t, :], tstat[u][:, t, :]).then_inc(sem("tally"), 1)
                    dve.wait_ge(sem("tally"), link.start + 2 * T)
                    nc.vector.tensor_scalar(trs[u][:, 0, :], tmv[u][:, :, 1], EPS, None, ALU.add) \
                        .then_inc(sem("tvar"), 1)
                    nc.vector.tensor_tensor(tn[u][:, :, :], hout[u][:, :, :],
                                            tmv[u][:, :, 0:1].broadcast_to([P, T, V]), ALU.subtract) \
                        .then_inc(sem("tally"), 1)

                def tally(i, u):
                    link = Chain(dve, sem("tally"), (UNITS * i + u) * TPER + 2 * T + 1)
                    dve.wait_ge(sem("tally"), link.start)
                    dve.wait_ge(sem("trs"), up(i, u))
                    link(nc.vector.tensor_tensor(tn[u][:, :, :], tn[u][:, :, :],
                                                 trs[u][:, 1, :].unsqueeze(2).broadcast_to([P, T, V]), ALU.mult))
                    for r in range(2):
                        link(nc.vector.tensor_tensor(feat[:, :, :], feat[:, :, :], tn[u][:, 2 * r:2 * r + 2, :],
                                                     ALU.add))

                TPER = 2 * T + 4
                if not wide:
                    nc.vector.memset(feat[:, :, :], 0.0).then_inc(sem("feat0"), 1)
                    dve.wait_ge(sem("feat0"), 1)
                for u in range(UNITS):
                    nc.vector.memset(va[u][:, :, :, :], 0.0).then_inc(sem("pad"), 1)
                dve.wait_ge(sem("pad"), UNITS)
                for u in range(UNITS):
                    nc.vector.memset(va[u][:, :, :, 0:1], 1.0).then_inc(sem("pad"), 1)
                dve.wait_ge(sem("pad"), 2 * UNITS)
                dve.sem_inc(sem("hin_seen"), UNITS)
                dve.sem_inc(sem("hres_free"), UNITS)
                dve.sem_inc(sem("quad_free"), UNITS)
                for u in range(UNITS):
                    dve.sem_inc(sem(f"stored{u}"), 16)
                stages = {"norm": norm, "scale": scale, "split": split, "divide": divide, "finish": finish,
                          "tally norm": tally_norm, "tally": tally}
                for s in range(NS):
                    stages[f"maxima {s}"] = maxima(s)
                    if not wide or s >= 2:
                        stages[f"add bias {s}"] = add_bias(s)
                in_flight(dve, NIT, ORDER, stages)

            @block.scalar
            def _(act):
                def copy_turned(i, u):
                    act.wait_ge(sem("xT_ps"), up(i, u))
                    nc.scalar.copy(xT[u][:, :, :].rearrange("p s n -> p (s n)"), flat[u][:, 0:NT // 2]) \
                        .then_inc(sem("xT"), 1)

                def round_qk(i, u):
                    act.wait_ge(sem("qk_ps"), up(i, u))
                    nc.scalar.activation(parts[u][:, 0, :], flat[u][:, 0:NT], ACT.Identity,
                                         bias=A.qkb[:, 0:1]).then_inc(sem("part0"), 1)

                def stack_queries(c):
                    def stage(i, u):
                        act.wait_ge(sem(f"q{c}_ps"), up(i, u))
                        n = NPP // NPQ
                        nc.scalar.copy(qst[u][:, c * n:(c + 1) * n, :].rearrange("p a n -> p (a n)"), flat[u]) \
                            .then_inc(sem(f"qst{c}"), 1)
                    return stage

                def stack_keys(c):
                    def stage(i, u):
                        act.wait_ge(sem(f"k{c}_ps"), up(i, u))
                        if wide:
                            for q in range(2):
                                nc.scalar.activation(
                                    kst[u][halves[q], q * NPP:(q + 1) * NPP, :].rearrange("p a n -> p (a n)"),
                                    flat[u][halves[q], :], ACT.Identity, bias=K.ones_rows[halves[q], 0:1]) \
                                    .then_inc(sem(f"kst_{c}"), 1)
                        else:
                            nc.scalar.activation(kst[u][:, 2 * c:2 * c + 2, :].rearrange("p a n -> p (a n)"),
                                                 flat[u], ACT.Identity,
                                                 bias=K.ones_rows[:, 0:1]).then_inc(sem(f"kst_{c}"), 1)
                    return stage

                def copy_max(i, u):
                    act.wait_ge(sem("mT_ps"), up(i, u))
                    nc.scalar.copy(mT[u][:, :], flat[u][0:3 * HEADS, 0:NT]).then_inc(sem("mT"), 1)

                def exps(s):
                    def stage(i, u):
                        act.wait_ge(sem(f"t_bias{s}" if not wide or s >= 2 else f"t{s}_ps"), up(i, u))
                        dst = pr[u][:, s, :, :].rearrange("p h n -> p (h n)") if wide \
                            else pr[u][:, s, :, :, :].rearrange("p h t n -> p (h t n)")
                        nc.scalar.activation(dst, flat[u], ACT.Exp).then_inc(sem(f"p{s}"), 1)
                    return stage

                def copy_values(i, u):
                    act.wait_ge(sem("pv_ps"), up(i, u))
                    nc.scalar.copy(oT[u][:, :, :].rearrange("p g n -> p (g n)"), flat[u][:, 0:512]) \
                        .then_inc(sem("oT"), 1)

                def copy_out(i, u):
                    act.wait_ge(sem("onT_ps"), up(i, u))
                    nc.scalar.copy(onT[u][:, :, :].rearrange("p s n -> p (s n)"), flat[u][:, 0:NT // 2]) \
                        .then_inc(sem("onT"), 1)

                if wide:
                    act.wait_ge(sem("kst0"), UNITS)
                stages = {"copy turned": copy_turned, "round": round_qk, "copy max": copy_max, "copy out": copy_out}
                for c in range(NPQ):
                    stages[f"stack queries {c}"], stages[f"stack keys {c}"] = stack_queries(c), stack_keys(c)
                for s in range(NS):
                    stages[f"exp {s}"] = exps(s)
                if wide:
                    stages["copy values"] = copy_values
                in_flight(act, NIT, ORDER, stages)

            @block.tensor
            def _(pe):
                def turned(u, src):
                    for s in range(T // 2):
                        last = nc.tensor.transpose(flat[u][:, s * P:(s + 1) * P],
                                                   src[u][:, 2 * s:2 * s + 2, :].rearrange("p q e -> p (q e)"),
                                                   K.ident[:, :])
                    return last

                def product(u, srcT, w):
                    for s in range(T // 2):
                        last = nc.tensor.matmul(flat[u][:, 512 + s * P:512 + (s + 1) * P], srcT[u][:, s, :],
                                                w[:, :, :].rearrange("p q e -> p (q e)"), start=True, stop=True)
                    return last

                def select(u, qk, c):
                    for a in range(NPP // NPQ):
                        for r in range(3):
                            last = nc.tensor.matmul(flat[u][:, a * NT:(a + 1) * NT],
                                                    K.sel[:, qk, r, c * NPP // NPQ + a, :], parts[u][:, r, :],
                                                    start=r == 0, stop=r == 2)
                    return last

                def score_mms(u, s, stat_, mov):
                    if wide:
                        t, c = divmod(s, 2)
                        for a in range(NPP):
                            h = c * NPP + a
                            last = nc.tensor.matmul(flat[u][:, a * NT:(a + 1) * NT],
                                                    stat_[u][:, h if stat_ is kst else a, t * P:(t + 1) * P],
                                                    mov[u][:, h if mov is kst else a, :], start=True, stop=True)
                        return last
                    for pp in range(NPP):
                        for t in range(2):
                            for par in range(2):
                                k = (2 * s + t) * P + par * W
                                for q in range(2):
                                    c = q * 512 + (pp * 2 + t) * W
                                    last = nc.tensor.matmul(flat[u][par * W:(par + 1) * W, c:c + W],
                                                            stat_[u][halves[q], pp, k:k + W],
                                                            mov[u][halves[q], pp, k:k + W],
                                                            start=True, stop=True, tile_position=(64 * q, par * W))
                    return last

                def turn(i, u):
                    pe.wait_ge(sem("xn"), up(i, u))
                    wait_alone(pe, sem("quad_free"), up(i, u), sem("pe_passed"))
                    turned(u, xn).then_inc(sem("xT_ps"), 1)

                def project(i, u):
                    pe.wait_ge(sem("xT"), up(i, u))
                    for par in range(2):
                        last = nc.tensor.matmul(
                            flat[u][:, 0:NT].rearrange("p (s q n) -> p q s n", q=2, n=P)[:, par],
                            A.wqk[:, par, :], xT[u][:, :, :], start=True, stop=True)
                    last.then_inc(sem("qk_ps"), 1)
                    product(u, xT, A.wv).then_inc(sem("v_ps"), 1)

                def queries(c):
                    def stage(i, u):
                        if c == 0:
                            pe.wait_ge(sem("parts"), up(i, u))
                            pe.wait_ge(sem("va"), up(i, u))
                        else:
                            pe.wait_ge(sem(f"qst{c - 1}"), up(i, u))
                        select(u, 0, c).then_inc(sem(f"q{c}_ps"), 1)
                    return stage

                def keys(c):
                    def stage(i, u):
                        if c == 0:
                            pe.wait_ge(sem(f"qst{NPQ - 1}"), up(i, u))
                        else:
                            pe.wait_ge(sem(f"kst_{c - 1}"), up(i, u))
                        select(u, 1, c).then_inc(sem(f"k{c}_ps"), 1)
                    return stage

                def scores(s):
                    def stage(i, u):
                        if s == 0:
                            wait_alone(pe, sem(f"kst_{NPQ - 1}"), (2 if wide else 1) * up(i, u), sem("pe_passed"))
                        else:
                            wait_alone(pe, sem(f"m{s - 1}"), up(i, u), sem("pe_passed"))
                        score_mms(u, s, qst, kst).then_inc(sem(f"s{s}_ps"), 1)
                    return stage

                def turn_max(i, u):
                    pe.wait_ge(sem("max_parts"), up(i, u))
                    for t in range(T):
                        last = nc.tensor.matmul(flat[u][0:3 * HEADS, t * P:(t + 1) * P],
                                                m3[u][:, t, :, :, :].rearrange("p q r h -> p (q r h)"),
                                                K.identb[:, :], start=True, stop=True)
                    last.then_inc(sem("mT_ps"), 1)

                def weights(s):
                    def stage(i, u):
                        if s == 0:
                            wait_alone(pe, sem(f"max{u}"), 32 * i + 32, sem("pe_passed"))
                        else:
                            wait_alone(pe, sem(f"p{s - 1}"), up(i, u), sem("pe_passed"))
                        score_mms(u, s, kst, qst).then_inc(sem(f"t{s}_ps"), 1)
                    return stage

                def values(i, u):
                    wait_alone(pe, sem(f"p{NS - 1}"), up(i, u), sem("pe_passed"))
                    if wide:
                        for g in range(NGRP):
                            for t in range(T):
                                for j in range(NJ):
                                    last = nc.tensor.matmul(flat[u][32 * j:32 * j + 32, g * NT:(g + 1) * NT],
                                                            va[u][:, t, g * NJ + j, :], pr[u][:, 2 * t + g, j, :],
                                                            start=t == 0, stop=t == T - 1,
                                                            tile_position=(0, 32 * j))
                        last.then_inc(sem("pv_ps"), 1)
                    else:
                        for t in range(T):
                            for h in range(HEADS):
                                for q in range(2):
                                    c = (t * HEADS + h) * VW
                                    last = nc.tensor.matmul(bank[u][halves[q], q, c:c + VW],
                                                            pr[u][halves[q], t // 2, h, t % 2, :],
                                                            va[u][halves[q], t, h, :], start=True, stop=True,
                                                            tile_position=(64 * q, 64 * q))
                        last.then_inc(sem("o_ps"), 1)

                def turn_values(i, u):
                    pe.wait_ge(sem("oT"), up(i, u))
                    for t in range(T):
                        for g in range(NGRP):
                            c = 512 + (t * NGRP + g) * P
                            last = nc.tensor.transpose(flat[u][:, c:c + P], oT[u][:, g, t * P:(t + 1) * P],
                                                       K.ident[:, :])
                    last.then_inc(sem("o_ps"), 1)

                def turn_out(i, u):
                    wait_alone(pe, sem("on"), (1 if wide else 2) * up(i, u), sem("pe_passed"))
                    turned(u, on).then_inc(sem("onT_ps"), 1)

                def output(i, u):
                    pe.wait_ge(sem("onT"), up(i, u))
                    product(u, onT, A.wo).then_inc(sem("y_ps"), 1)

                stages = {"turn": turn, "project": project, "turn max": turn_max, "values": values,
                          "turn out": turn_out, "product": output}
                if wide:
                    stages["turn values"] = turn_values
                for c in range(NPQ):
                    stages[f"queries {c}"], stages[f"keys {c}"] = queries(c), keys(c)
                for s in range(NS):
                    stages[f"scores {s}"], stages[f"weights {s}"] = scores(s), weights(s)
                in_flight(pe, NIT, ORDER, stages)


def attention_weights(nc, a, K, dram_ext, ctx):
    A0, A1 = Consts(), Consts()

    def sb(name, shape, dt=F32):
        return ctx.enter_context(nc.sbuf_tensor(name, shape, dt))

    for A, n in ((A0, "a0"), (A1, "a1")):
        A.wqk = sb(n + "_wqk", [P, 2, P])
        A.wv, A.wo = sb(n + "_wv", [P, 2, V]), sb(n + "_wo", [P, 2, V])
        A.qkb = sb(n + "_qkb", [P, 1])
        A.brow = sb(n + "_brow", [P, V])
    A0.biasS, A0.biasT = sb("a0_biasS", [P, 64]), sb("a0_biasT", [P, 64])
    A1.biasS, A1.biasT = sb("a1_biasS", [P, HEADS, P]), sb("a1_biasT", [P, HEADS, P])
    K.sel = sb("sel", [P, 2, 3, NPP, P], BF16)
    K.identb = sb("identb", [P, P], BF16)
    K.ones_rows = sb("ones_rows", [P, 1])
    EXT = 2 * P - 1
    NTAB = a["L1_attn_rpb_table"].shape[0]
    with ExitStack() as tmp:
        def ts(name, shape):
            return tmp.enter_context(nc.sbuf_tensor(name, shape, F32))

        sem = Signals(nc, "aw_")
        tmp.callback(sem.close)

        w0 = ts("aw_w0", [V, 3, 2, V])
        o0 = ts("aw_o0", [V, 2, V])
        w1 = ts("aw_w1", [P, 3 * V])
        o1 = ts("aw_o1", [P, V])
        tab = ts("aw_tab", [NTAB, HEADS])
        ext = ts("aw_ext", [HEADS, EXT])
        hank0 = ts("aw_hank0", [P, 64])
        hank1 = ts("aw_hank1", [P, HEADS, P])
        brd = ts("aw_brd", [P, V])
        bv = ts("aw_bv", [V, 1])
        bqk = ts("aw_bqk", [P, 1])
        onesh = ts("aw_onesh", [P, 2])
        rel2 = ts("aw_rel2", [64, 2, 64])
        ps = [tmp.enter_context(nc.psum_tensor(f"aw_ps{b}", [P, 512], F32)) for b in range(8)]
        hf = [slice(64 * q, 64 * q + 64) for q in range(2)]

        with nc.Block() as block:
            @block.sync
            def _(sp):
                wq0 = a["L0_attn_w_qkv"].rearrange("(q o) c -> o q c", q=3)
                loads = [(w0[:, :, r, :], wq0) for r in range(2)]
                loads += [(o0[:, r, :], a["L0_attn_w_proj"]) for r in range(2)]
                loads += [(w1[hf[r], :], a["L1_attn_qkv_w"]) for r in range(2)]
                loads += [(o1[hf[r], :], a["L1_attn_proj_w"]) for r in range(2)]
                loads += [(tab[:, :], a["L1_attn_rpb_table"]),
                          (A0.brow[:, :], a["L0_attn_b_proj"].partition_broadcast(P)),
                          (brd[:, :], a["L1_attn_proj_b"].partition_broadcast(P)),
                          (bv[:, :], a["L1_attn_qkv_b"][2 * V:3 * V].unsqueeze(1)),
                          (bqk[:, :], a["L1_attn_qkv_b"][0:2 * V].unsqueeze(1))]
                rb = a["L0_attn_rel_bias"]
                for q in range(2):
                    loads.append((hank0[hf[q], :], bass.AP(rb.tensor, 0, [[1, 64], [1, 64]])))
                for dst, src in loads:
                    sp.dma_start(dst, src).then_inc(sem("loaded"), 16)
                K.n_aw = 16 * len(loads)
                sp.wait_ge(sem("ext"), 1)
                sp.dma_start(dram_ext, ext[:, :]).then_inc(sem("extd"), 16)
                sp.wait_ge(sem("extd"), 16)
                for h in range(HEADS):
                    sp.dma_start(hank1[:, h, :], bass.AP(dram_ext.tensor, h * EXT, [[1, P], [1, P]])) \
                        .then_inc(sem("bT"), 16)

            @block.gpsimd
            def _(pool):
                nc.gpsimd.memset(K.sel[:, :, :, :, :], 0.0).then_inc(sem("sel0"), 1)

            @block.vector
            def _(dve):
                step = Chain(dve, sem("dve"))
                for A in (A0, A1):
                    nc.vector.memset(A.wqk[:, :, :], 0.0)
                    nc.vector.memset(A.wv[:, :, :], 0.0)
                    step(nc.vector.memset(A.wo[:, :, :], 0.0))
                nc.vector.memset(A0.qkb[:, :], 0.0)
                step(nc.vector.tensor_reduce(onesh[:, :], K.ident[:, :].rearrange("p (q n) -> p q n", q=2)[:, :, 0:3],
                                             AX.X, ALU.add))
                step(nc.vector.tensor_reduce(K.ones_rows[:, :], onesh[:, :], AX.X, ALU.add))
                step(nc.vector.tensor_copy(K.identb[:, :], K.ident[:, :]))
                dve.wait_ge(sem("sel0"), 1)
                for n, pair in enumerate(SLOTS):
                    for qk in range(2):
                        c = OFF + n * HD
                        dst = K.sel[:, qk, pair[qk], :, :].rearrange("p a (q n) -> p a q n", q=2)[:, :, :, c:c + HD]
                        src = K.ident[:, qk * V:(qk + 1) * V].rearrange("p (q a d) -> p a q d", q=2, a=NPP)
                        step(nc.vector.tensor_copy(dst, src))
                dve.wait_ge(sem("loaded"), K.n_aw)
                for r in range(2):
                    nc.vector.tensor_scalar(A1.wqk[hf[r], r, 0:V], w1[hf[r], 0:V], Q_SCALE, None, ALU.mult)
                    nc.vector.tensor_copy(A1.wqk[hf[r], r, V:], w1[hf[r], V:2 * V])
                    nc.vector.tensor_copy(A1.wv[hf[r], r, :], w1[hf[r], 2 * V:])
                    step(nc.vector.tensor_copy(A1.wo[hf[r], r, :], o1[hf[r], :]))
                nc.vector.tensor_scalar(A1.qkb[hf[0], :], bqk[hf[0], :], Q_SCALE, None, ALU.mult)
                step(nc.vector.tensor_copy(A1.qkb[hf[1], :], bqk[hf[1], :]))
                step(nc.vector.tensor_copy(A0.biasT[:, :], hank0[:, ::-1]))
                for q in range(2):
                    step(nc.vector.tensor_copy(rel2[:, q, :], hank0[0:64, ::-1]))
                dve.sem_inc(sem("rel2"), 1)
                dve.wait_ge(sem("wT"), 1)
                for r in range(2):
                    nc.vector.tensor_scalar(A0.wqk[hf[r], r, 0:V], ps[0][hf[r], 0:V], Q_SCALE, None, ALU.mult)
                    nc.vector.tensor_copy(A0.wqk[hf[r], r, V:], ps[1][hf[r], 0:V])
                    nc.vector.tensor_copy(A0.wv[hf[r], r, :], ps[2][hf[r], 0:V])
                    step(nc.vector.tensor_copy(A0.wo[hf[r], r, :], ps[3][hf[r], 0:V]))
                step(nc.vector.tensor_copy(A0.biasS[:, :], ps[4][:, 0:64]))
                step(nc.vector.tensor_tensor(A1.brow[:, :], ps[7][:, 0:V], brd[:, :], ALU.add))
                step(nc.vector.memset(ext[:, :], 0.0))
                step(nc.vector.tensor_scalar(ext[:, 0:NTAB], ps[6][0:HEADS, 0:NTAB],
                                             ps[6][0:HEADS, NTAB - 1:NTAB], None, ALU.subtract))
                dve.sem_inc(sem("ext"), 1)
                dve.wait_ge(sem("bT"), 16 * HEADS)
                step(nc.vector.tensor_copy(A1.biasS[:, :, :], hank1[:, :, ::-1]))
                dve.sem_inc(sem("biasS"), 1)
                for c in range(2):
                    dve.wait_ge(sem("bS"), c + 1)
                    step(nc.vector.tensor_copy(A1.biasT[:, 4 * c:4 * c + 4, :].rearrange("p h m -> p (h m)"),
                                               ps[c][:, :]))

            @block.tensor
            def _(pe):
                pe.wait_ge(sem("loaded"), K.n_aw)
                idv = K.ident[0:V, 0:V]
                for q in range(3):
                    nc.tensor.transpose(ps[q][:, 0:V], w0[:, q, :, :].rearrange("p r c -> p (r c)"), idv)
                nc.tensor.transpose(ps[3][:, 0:V], o0[:, :, :].rearrange("p r c -> p (r c)"), idv)
                pe.wait_ge(sem("rel2"), 1)
                nc.tensor.transpose(ps[4][:, 0:64], rel2[:, :, :].rearrange("p q m -> p (q m)"), idv)
                nc.tensor.transpose(ps[6][0:HEADS, 0:NTAB], tab[:, :], K.ident[0:NTAB, 0:NTAB])
                nc.tensor.matmul(ps[7][:, 0:V], bv[:, 0:1].broadcast_to([V, P]), o1[0:V, :], start=True, stop=True) \
                    .then_inc(sem("wT"), 1)
                pe.wait_ge(sem("biasS"), 1)
                for h in range(HEADS):
                    last = nc.tensor.transpose(ps[h // 4][:, (h % 4) * P:(h % 4 + 1) * P], A1.biasS[:, h, :],
                                               K.ident[:, :])
                    if h % 4 == 3:
                        last.then_inc(sem("bS"), 1)
    return A0, A1


class Consts:
    pass


NE = 8
NPAIR = NE // 2
TB = 8
BN_EPS = 1e-3
NBLK = NTOK // (TB * P)


def norm_stats(nc, dve, sem, count, hin, stat, mv, tiles):
    n = count
    for t in range(tiles):
        nc.vector.bn_stats(stat[:, t, :], hin[:, t, :]).then_inc(sem, 1)
    wait = n + tiles
    dve.wait_ge(sem, wait)
    dve.sem_inc(sem, 1)
    for t in range(tiles):
        nc.vector.bn_aggr(mv[:, t, :], stat[:, t, :]).then_inc(sem, 1)
    dve.wait_ge(sem, wait + 1 + tiles)
    return 2 * tiles + 1


def ffn0_gate(nc, a, K, F):
    with ExitStack() as ctx:
        def sb(n, shape):
            return ctx.enter_context(nc.sbuf_tensor("fg_" + n, shape, F32))

        sem = Signals(nc, "fg_")
        ctx.callback(sem.close)

        names = ["b1", "g1", "be1", "m1", "v1", "b2", "g2", "be2", "m2", "v2"]
        NV = len(names)
        rows = sb("rows", [NV * NPAIR, P])
        col = sb("col", [P, NV, NPAIR])
        sc = sb("sc", [P, 2, NPAIR])
        dg = sb("dg", [P, P])
        b2m = sb("b2m", [P, NPAIR, NE])
        cb = sb("cb", [NE, V])
        bo = sb("bo", [NE, V])
        wr = sb("wr", [V, NE])
        br = sb("br", [P, NE])
        feat = F.feat
        featT = sb("featT", [V, 2, P])
        lg = sb("lg", [P, 2, NE])
        st = sb("st", [P, 2, 2])
        gw = sb("gw", [P, 2, NE])
        gwT = sb("gwT", [NE, 2, P])
        ps = [ctx.enter_context(nc.psum_tensor(f"fg_ps{b}", [P, 512], F32)) for b in range(8)]
        with nc.Block() as block:
            @block.sync
            def _(sp):
                sp.wait_ge(sem("zero"), 1)
                n = 0

                def load(dst, src):
                    nonlocal n
                    sp.dma_start(dst, src).then_inc(sem("loaded"), 16)
                    n += 1
                for i, nm in enumerate(names):
                    load(rows[i * NPAIR:(i + 1) * NPAIR, :], a["L0_ffn_" + nm].rearrange("(q s) h -> q (s h)", s=2))
                for half in range(2):
                    load(F.w1[half * V:(half + 1) * V, half, :, :], a["L0_ffn_W1"].rearrange("e d h -> d e h"))
                    for p in range(NPAIR):
                        load(F.w2[half * V:(half + 1) * V, p, half * V:(half + 1) * V], a["L0_ffn_W2"][2 * p + half])
                load(F.wo[:, :, :], a["L0_ffn_Wo"].rearrange("(q s) h d -> (s h) q d", s=2))
                load(bo[:, :], a["L0_ffn_bo"])
                load(wr[:, :], a["L0_ffn_Wr"])
                load(br[:, :], a["L0_ffn_br"].partition_broadcast(P))
                F.n_loads = 16 * n

            @block.gpsimd
            def _(pool):
                pool.wait_ge(sem("bnv"), 1)
                nc.gpsimd.tensor_tensor(sc[:, :, :], sc[:, :, :],
                                        K.mhalf[:, 0:1].unsqueeze(2).broadcast_to([P, 2, NPAIR]), ALU.pow) \
                    .then_inc(sem("bnr"), 1)

            @block.vector
            def _(dve):
                step = Chain(dve, sem("dve"))
                nc.vector.memset(b2m[:, :, :], 0.0).then_inc(sem("z"), 1)
                nc.vector.memset(F.w1[:, :, :, :], 0.0).then_inc(sem("z"), 1)
                dve.wait_ge(sem("z"), 2)
                step(nc.vector.memset(F.w2[:, :, :], 0.0))
                dve.sem_inc(sem("zero"), 1)
                dve.wait_ge(sem("colp"), 1)
                step(nc.vector.tensor_copy(col[:, :, :].rearrange("p v q -> p (v q)"), ps[0][:, 0:NV * NPAIR]))
                for k in range(2):
                    step(nc.vector.tensor_scalar(sc[:, k, :], col[:, 5 * k + 4, :], BN_EPS, None, ALU.add))
                dve.sem_inc(sem("bnv"), 1)
                dve.wait_ge(sem("bnr"), 1)
                for k, t in ((0, F.t1), (1, F.t2)):
                    b, g, be, m = (col[:, 5 * k + r, :] for r in range(4))
                    step(nc.vector.tensor_tensor(F.s[:, k, :], sc[:, k, :], g, ALU.mult))
                    step(nc.vector.tensor_tensor(t[:, :], b, m, ALU.subtract))
                    step(nc.vector.tensor_tensor(t[:, :], t[:, :], F.s[:, k, :], ALU.mult))
                    step(nc.vector.tensor_tensor(t[:, :], t[:, :], be, ALU.add))
                step(nc.vector.tensor_scalar(F.nt2[:, :], F.t2[:, :], -1.0, None, ALU.mult))
                for p in range(NPAIR):
                    step(nc.vector.tensor_scalar(dg[:, :], K.ident[:, :], F.s[:, 1, p:p + 1], float(D), ALU.mult, ALU.mult))
                    dve.sem_inc(sem("dg"), 1)
                    dve.wait_ge(sem("s2row"), p + 1)
                    step(nc.vector.tensor_tensor(F.w2[:, p, :], F.w2[:, p, :], ps[1][:, 0:P], ALU.mult))
                    for s in range(2):
                        hf = slice(s * V, (s + 1) * V)
                        step(nc.vector.tensor_copy(b2m[hf, p, 2 * p + s:2 * p + s + 1], F.t2[hf, p:p + 1]))
                dve.sem_inc(sem("b2m"), 1)
                dve.wait_ge(sem("cbp"), 1)
                step(nc.vector.tensor_tensor(cb[:, :], ps[2][0:NE, 0:V], bo[:, :], ALU.add))
                dve.wait_ge(sem("featp"), 1)
                step(nc.vector.tensor_scalar(featT[:, :, :].rearrange("p q n -> p (q n)"), ps[3][0:V, 0:2 * P],
                                             1.0 / SEQ, None, ALU.mult))
                dve.sem_inc(sem("featT"), 1)
                dve.wait_ge(sem("lgp"), 1)
                step(nc.vector.tensor_tensor(lg[:, :, :], ps[4][:, 0:2 * NE].rearrange("p (q e) -> p q e", q=2),
                                             br[:, :].unsqueeze(1).broadcast_to([P, 2, NE]), ALU.add))
                step(nc.vector.tensor_reduce(st[:, 0, :], lg[:, :, :], AX.X, ALU.max))
                step(nc.vector.tensor_tensor(lg[:, :, :], lg[:, :, :],
                                             st[:, 0, :].unsqueeze(2).broadcast_to([P, 2, NE]), ALU.subtract))
                dve.sem_inc(sem("lg"), 1)
                dve.wait_ge(sem("lge"), 1)
                step(nc.vector.tensor_reduce(st[:, 0, :], lg[:, :, :], AX.X, ALU.add))
                step(nc.vector.reciprocal(st[:, 1, :], st[:, 0, :]))
                step(nc.vector.tensor_tensor(gw[:, :, :], lg[:, :, :],
                                             st[:, 1, :].unsqueeze(2).broadcast_to([P, 2, NE]), ALU.mult))
                dve.sem_inc(sem("gw"), 1)
                dve.wait_ge(sem("gwp"), 1)
                for p in range(NPAIR):
                    step(nc.vector.tensor_copy(F.gate[:, p, :, :].rearrange("p q n -> p (q n)"),
                                               ps[5 + p // 2][:, (p % 2) * 256:(p % 2) * 256 + 256]))
                step(nc.vector.tensor_copy(gwT[:, :, :].rearrange("p q n -> p (q n)"), ps[7][0:NE, 0:2 * P]))
                dve.sem_inc(sem("gwT"), 1)
                dve.wait_ge(sem("corrp"), 1)
                step(nc.vector.tensor_copy(F.corr[:, :, :].rearrange("p q n -> p (q n)"), ps[0][:, 0:2 * V]))

            @block.scalar
            def _(act):
                act.wait_ge(sem("lg"), 1)
                nc.scalar.activation(lg[:, :, :], lg[:, :, :], ACT.Exp).then_inc(sem("lge"), 1)

            @block.tensor
            def _(pe):
                pe.wait_ge(sem("loaded"), F.n_loads)
                nc.tensor.transpose(ps[0][:, 0:NV * NPAIR], rows[:, :], K.ident[0:NV * NPAIR, 0:NV * NPAIR]) \
                    .then_inc(sem("colp"), 1)
                for p in range(NPAIR):
                    pe.wait_ge(sem("dg"), p + 1)
                    nc.tensor.matmul(ps[1][:, 0:P], K.onesD[:, :], dg[:, :], start=True, stop=True) \
                        .then_inc(sem("s2row"), 1)
                pe.wait_ge(sem("b2m"), 1)
                for p in range(NPAIR):
                    last = nc.tensor.matmul(ps[2][0:NE, 0:V], b2m[:, p, :], F.wo[:, p, :],
                                            start=p == 0, stop=p == NPAIR - 1)
                last.then_inc(sem("cbp"), 1)
                for q in range(2):
                    last = nc.tensor.transpose(ps[3][0:V, q * P:(q + 1) * P], feat[:, q, :], K.ident[:, :])
                last.then_inc(sem("featp"), 1)
                pe.wait_ge(sem("featT"), 1)
                for q in range(2):
                    last = nc.tensor.matmul(ps[4][:, q * NE:(q + 1) * NE], featT[:, q, :], wr[:, :],
                                            start=True, stop=True)
                last.then_inc(sem("lgp"), 1)
                pe.wait_ge(sem("gw"), 1)
                for q in range(2):
                    for p in range(NPAIR):
                        for s in range(2):
                            c = (p % 2) * 256 + q * P
                            nc.tensor.matmul(ps[5 + p // 2][s * V:(s + 1) * V, c:c + P],
                                             gw[:, q, 2 * p + s:2 * p + s + 1].broadcast_to([P, V]), K.ident[:, :],
                                             start=True, stop=True)
                    last = nc.tensor.transpose(ps[7][0:NE, q * P:(q + 1) * P], gw[:, q, :], K.ident[:, :])
                last.then_inc(sem("gwp"), 1)
                pe.wait_ge(sem("gwT"), 1)
                for q in range(2):
                    last = nc.tensor.matmul(ps[0][:, q * V:(q + 1) * V], gwT[:, q, :], cb[:, :], start=True, stop=True)
                last.then_inc(sem("corrp"), 1)


def ffn0(nc, K, F, h_in, h_out):
    with ExitStack() as ctx:
        def sb(n, shape):
            return [ctx.enter_context(nc.sbuf_tensor(f"f0_{n}{u}", shape, F32)) for u in range(2)]

        sem = Signals(nc, "f0_")
        ctx.callback(sem.close)

        hin, hout, hres = sb("hin", [P, TB, V]), sb("hout", [P, TB, V]), sb("hres", [P, TB, V])
        stat, mv, rstd = sb("stat", [P, TB, 6]), sb("mv", [P, TB, 2]), sb("rstd", [P, 2, TB])
        xn, xT = sb("xn", [P, TB, V]), sb("xT", [P, 512])
        h1, g2 = sb("h1", [P, 2, 512]), sb("g2", [P, 2, 512])
        ps = [ctx.enter_context(nc.psum_tensor(f"f0_ps{b}", [P, 512], F32)) for b in range(8)]
        py, pt = ps[6], ps[7]
        hi_v = h_in.rearrange("(i u t p) e -> i u p t e", p=P, t=TB, u=2)
        ho_v = h_out.rearrange("(i u t p) e -> i u p t e", p=P, t=TB, u=2)
        NIT = NBLK // 2

        def up(i, u):
            return 2 * i + u + 1

        def pair(i, u, p):
            return NPAIR * (2 * i + u) + p + 1

        with nc.Block() as block:
            @block.sync
            def _(sp):
                for u in range(2):
                    sp.dma_start(hin[u][:, :, :], hi_v[0, u]).then_inc(sem(f"hin{u}"), 16)
                with sp.Fori(0, NIT - 1) as i:
                    for u in range(2):
                        sp.wait_ge(sem("hout"), up(i, u))
                        sp.dma_start(ho_v[i, u], hout[u][:, :, :]).then_inc(sem(f"stored{u}"), 16)
                        sp.wait_ge(sem("hin_seen"), up(i, u))
                        sp.wait_ge(sem("hin_kept"), up(i, u))
                        sp.dma_start(hin[u][:, :, :], hi_v[i + 1, u]).then_inc(sem(f"hin{u}"), 16)
                for u in range(2):
                    sp.wait_ge(sem("hout"), up(NIT - 1, u))
                    sp.dma_start(ho_v[NIT - 1, u], hout[u][:, :, :]).then_inc(sem(f"stored{u}"), 16)
                for u in range(2):
                    sp.wait_ge(sem(f"stored{u}"), 16 * (NIT + 1))

            @block.gpsimd
            def _(pool):
                def norm(i, u):
                    pool.wait_ge(sem("var"), up(i, u))
                    nc.gpsimd.tensor_tensor(rstd[u][:, 1, :], rstd[u][:, 0, :],
                                            K.mhalf[:, 0:1].broadcast_to([P, TB]), ALU.pow) \
                        .then_inc(sem("rstd"), 1)

                def keep(i, u, following):
                    pool.wait_ge(sem("hres_free"), up(i, u))
                    nc.gpsimd.tensor_tensor(hres[u][:, :, :].rearrange("p (s q) e -> p s (q e)", q=2),
                                            hin[u][:, :, :].rearrange("p (s q) e -> p s (q e)", q=2),
                                            F.corr[:, :, :].rearrange("p q e -> p (q e)").unsqueeze(1)
                                            .broadcast_to([P, TB // 2, 2 * V]), ALU.add) \
                        .then_inc(sem("hin_kept"), 1)
                    if following:
                        norm(*following)

                norm(0, 0)
                in_turns(pool, NIT, keep)

            @block.vector
            def _(dve):
                per = 2 * TB + 1 + 2

                def norm(i, u):
                    k = (2 * i + u) * per
                    dve.wait_ge(sem(f"hin{u}"), 16 * i + 16)
                    n = norm_stats(nc, dve, sem("ln"), k, hin[u], stat[u], mv[u], TB)
                    nc.vector.tensor_scalar(rstd[u][:, 0, :], mv[u][:, :, 1], EPS, None, ALU.add) \
                        .then_inc(sem("var"), 1)
                    link = Chain(dve, sem("ln"), k + n)
                    link(nc.vector.tensor_tensor(xn[u][:, :, :], hin[u][:, :, :],
                                                 mv[u][:, :, 0:1].broadcast_to([P, TB, V]), ALU.subtract))
                    dve.sem_inc(sem("hin_seen"), 1)
                    dve.wait_ge(sem("rstd"), up(i, u))
                    link(nc.vector.tensor_tensor(xn[u][:, :, :], xn[u][:, :, :],
                                                 rstd[u][:, 1, :].unsqueeze(2).broadcast_to([P, TB, V]),
                                                 ALU.mult))
                    dve.sem_inc(sem("xn"), 1)

                def experts(i, u, following):
                    for p in range(NPAIR):
                        for q in range(2):
                            dve.wait_ge(sem("h2_ps"), 2 * (pair(i, u, p) - 1) + q + 1)
                            nc.vector.scalar_tensor_tensor(
                                g2[p % 2][:, q, :].rearrange("p (s n) -> p s n", n=P),
                                ps[4 + q][:, :].rearrange("p (s n) -> p s n", n=P), F.nt2[:, p:p + 1],
                                F.gate[:, p, q:q + 1, :].broadcast_to([P, TB // 2, P]), ALU.max, ALU.mult) \
                                .then_inc(sem("g2"), 1)
                        if p == 0 and following:
                            norm(*following)
                    dve.wait_ge(sem("y_ps"), up(i, u))
                    dve.wait_ge(sem("hin_kept"), up(i, u))
                    dve.wait_ge(sem(f"stored{u}"), 16 * i + 16)
                    nc.vector.tensor_tensor(hout[u][:, :, :].rearrange("p t e -> p (t e)"), py[:, :],
                                            hres[u][:, :, :].rearrange("p t e -> p (t e)"), ALU.add) \
                        .then_inc(sem("hout"), 1)
                    dve.wait_ge(sem("hout"), up(i, u))
                    dve.sem_inc(sem("hres_free"), 1)
                    dve.sem_inc(sem("py_free"), 1)

                dve.sem_inc(sem("hres_free"), 2)
                for u in range(2):
                    dve.sem_inc(sem(f"stored{u}"), 16)
                norm(0, 0)
                in_turns(dve, NIT, experts)

            @block.scalar
            def _(act):
                def turned(i, u):
                    act.wait_ge(sem("xT_ps"), up(i, u))
                    nc.scalar.copy(xT[u][:, :], pt[:, :]).then_inc(sem("xT"), 1)

                def experts(i, u, following):
                    for p in range(NPAIR):
                        act.wait_ge(sem("h1_ps"), pair(i, u, p))
                        for q in range(2):
                            nc.scalar.activation(h1[p % 2][:, q, :], ps[2 * (p % 2) + q][:, :], ACT.Relu,
                                                 bias=F.t1[:, p:p + 1], scale=F.s[:, 0, p:p + 1]) \
                                .then_inc(sem("h1"), 1)
                        if p == 2 and following:
                            turned(*following)

                turned(0, 0)
                in_turns(act, NIT, experts)

            @block.tensor
            def _(pe):
                def turn(i, u):
                    pe.wait_ge(sem("xn"), up(i, u))
                    for s in range(TB // 2):
                        last = nc.tensor.transpose(pt[:, s * P:(s + 1) * P],
                                                   xn[u][:, 2 * s:2 * s + 2, :].rearrange("p q e -> p (q e)"),
                                                   K.ident[:, :])
                    last.then_inc(sem("xT_ps"), 1)

                def first(i, u, p):
                    if p == 0:
                        pe.wait_ge(sem("xT"), up(i, u))
                    for q in range(2):
                        last = nc.tensor.matmul(ps[2 * (p % 2) + q][:, :],
                                                F.w1[:, q, 2 * p:2 * p + 2, :].rearrange("p e h -> p (e h)"),
                                                xT[u][:, :], start=True, stop=True)
                    last.then_inc(sem("h1_ps"), 1)

                def out(i, u, p):
                    pe.wait_ge(sem("g2"), 2 * pair(i, u, p))
                    if p == 0:
                        pe.wait_ge(sem("py_free"), up(i, u))
                    for t in range(TB):
                        s, q = t // 2, t % 2
                        last = nc.tensor.matmul(py[:, t * V:(t + 1) * V], g2[p % 2][:, q, s * P:(s + 1) * P],
                                                F.wo[:, p, :], start=p == 0 and t == 0, stop=p == NPAIR - 1,
                                                skip_group_check=True)
                    if p == NPAIR - 1:
                        last.then_inc(sem("y_ps"), 1)

                def experts(i, u, following):
                    for p in range(NPAIR):
                        if p + 1 < NPAIR:
                            first(i, u, p + 1)
                        elif following:
                            first(*following, 0)
                        if p >= 1:
                            out(i, u, p - 1)
                        for q in range(2):
                            pe.wait_ge(sem("h1"), 2 * (pair(i, u, p) - 1) + q + 1)
                            nc.tensor.matmul(ps[4 + q][:, :], F.w2[:, p, :], h1[p % 2][:, q, :],
                                             start=True, stop=True).then_inc(sem("h2_ps"), 1)
                        if p == 1 and following:
                            turn(*following)
                    out(i, u, NPAIR - 1)

                pe.sem_inc(sem("py_free"), 1)
                turn(0, 0)
                first(0, 0, 0)
                in_turns(pe, NIT, experts)


def ffn1(nc, a, K, h_in, h_out):
    with ExitStack() as ctx:
        def one(n, shape):
            return ctx.enter_context(nc.sbuf_tensor("f1_" + n, shape, F32))

        def sb(n, shape):
            return [one(f"{n}{u}", shape) for u in range(2)]

        sem = Signals(nc, "f1_")
        ctx.callback(sem.close)

        H = P
        w1, w2 = one("w1", [P, 2, NE, H]), one("w2", [H, NE, V])
        b1r, b1 = one("b1r", [NE, H]), one("b1", [H, NE])
        gam, bet = one("gam", [P, 1]), one("bet", [V, 1])
        wr, wrg = one("wr", [P, NE]), one("wrg", [P, 2, NE])
        br = one("br", [P, NE])
        b2bd = one("b2bd", [TB * NE, TB, V])
        lower = one("lower", [P, NE, NE])
        hin, hout = sb("hin", [P, TB, V]), sb("hout", [P, TB, V])
        stat, mv, rstd = sb("stat", [P, TB, 6]), sb("mv", [P, TB, 2]), sb("rstd", [P, 2, TB])
        xn, xT = sb("xn", [P, TB, V]), sb("xT", [P, 512])
        act1 = sb("act1", [H, 2, 512])
        lg = sb("lg", [P, TB, NE])
        gt, eq = one("gt", [P, TB, NE, NE]), one("eq", [P, TB, NE, NE])
        rank, sel = one("rank", [P, TB, NE]), one("sel", [P, 2, TB, NE])
        v12 = sb("v12", [P, 4, TB])
        gate = sb("gate", [P, TB, NE])
        gT = sb("gT", [TB * NE, P])
        term = sb("term", [P, TB, V])
        acc = sb("acc", [P, TB, V])
        ps = [ctx.enter_context(nc.psum_tensor(f"f1_ps{b}", [P, 512], F32)) for b in range(8)]
        pm, pt = ps[6], ps[7]
        hi_v = h_in.rearrange("(i u p t) e -> i u p t e", p=P, t=TB, u=2)
        ho_v = h_out.rearrange("(i u p t) e -> i u p t e", p=P, t=TB, u=2)
        NIT = NBLK // 2
        NL = [0]

        def up(i, u):
            return 2 * i + u + 1

        def ex(i, u, e):
            return NE * (2 * i + u) + e + 1

        with nc.Block() as block:
            @block.sync
            def _(sp):
                sp.wait_ge(sem("zero"), 1)

                def load(dst, src):
                    sp.dma_start(dst, src).then_inc(sem("loaded"), 16)
                    NL[0] += 16
                for q in range(2):
                    hf = slice(q * V, (q + 1) * V)
                    load(w1[hf, q, :, :], a["L1_ffn_W1"].rearrange("e d h -> d e h"))
                    load(wr[hf, :], a["L1_ffn_Wr"])
                    load(gam[hf, :], a["L1_ffn_gamma"].unsqueeze(1))
                load(bet[:, :], a["L1_ffn_beta"].unsqueeze(1))
                load(w2[:, :, :], a["L1_ffn_W2"].rearrange("e h d -> h e d"))
                load(b1r[:, :], a["L1_ffn_b1"])
                load(br[:, :], a["L1_ffn_br"].partition_broadcast(P))
                for t in range(TB):
                    load(b2bd[t * NE:(t + 1) * NE, t, :], a["L1_ffn_b2"])
                for u in range(2):
                    sp.dma_start(hin[u][:, :, :], hi_v[0, u]).then_inc(sem(f"hin{u}"), 16)
                with sp.Fori(0, NIT - 1) as i:
                    for u in range(2):
                        sp.wait_ge(sem("hout"), up(i, u))
                        sp.dma_start(ho_v[i, u], hout[u][:, :, :]).then_inc(sem(f"stored{u}"), 16)
                        sp.wait_ge(sem("hin_seen"), up(i, u))
                        sp.wait_ge(sem("hin_kept"), up(i, u))
                        sp.dma_start(hin[u][:, :, :], hi_v[i + 1, u]).then_inc(sem(f"hin{u}"), 16)
                for u in range(2):
                    sp.wait_ge(sem("hout"), up(NIT - 1, u))
                    sp.dma_start(ho_v[NIT - 1, u], hout[u][:, :, :]).then_inc(sem(f"stored{u}"), 16)
                for u in range(2):
                    sp.wait_ge(sem(f"stored{u}"), 16 * (NIT + 1))

            @block.gpsimd
            def _(pool):
                def norm(i, u):
                    pool.wait_ge(sem("var"), up(i, u))
                    nc.gpsimd.tensor_tensor(rstd[u][:, 1, :], rstd[u][:, 0, :],
                                            K.mhalf[:, 0:1].broadcast_to([P, TB]), ALU.pow) \
                        .then_inc(sem("rstd"), 1)

                def experts(i, u, following):
                    for e in range(NE):
                        pool.wait_ge(sem("term"), ex(i, u, e) + 2)
                        pool.wait_ge(sem("acc"), ex(i, u, e) + 1)
                        if e == 0:
                            pool.wait_ge(sem("acc_free"), up(i, u))
                        nc.gpsimd.tensor_tensor(acc[u][:, :, :], (hin if e == 0 else acc)[u][:, :, :],
                                                term[e % 2][:, :, :], ALU.add).then_inc(sem("acc"), 1)
                        if e == 0:
                            pool.wait_ge(sem("acc"), ex(i, u, e) + 2)
                            pool.sem_inc(sem("hin_kept"), 1)
                        if e == 1 and following:
                            norm(*following)

                pool.sem_inc(sem("acc"), 2)
                norm(0, 0)
                in_turns(pool, NIT, experts)

            @block.vector
            def _(dve):
                step = Chain(dve, sem("dve"))
                step(nc.vector.memset(b2bd[:, :, :], 0.0))
                step(nc.vector.memset(wrg[:, :, :], 0.0))
                for q in range(2):
                    nc.vector.memset(w1[(1 - q) * V:(2 - q) * V, q, :, :], 0.0).then_inc(sem("w1_0"), 1)
                dve.wait_ge(sem("w1_0"), 2)
                dve.sem_inc(sem("zero"), 1)
                step(nc.vector.memset(lower[:, :, :], 0.0))
                for e in range(1, NE):
                    step(nc.vector.memset(lower[:, e, 0:e], 1.0))
                dve.wait_ge(sem("setp"), 1)
                step(nc.vector.tensor_copy(b1[:, :], ps[0][:, 0:NE]))
                step(nc.vector.tensor_tensor(b1[:, :], b1[:, :], ps[1][:, 0:NE], ALU.add))
                step(nc.vector.tensor_tensor(br[:, :], br[:, :], ps[2][:, 0:NE], ALU.add))
                step(nc.vector.tensor_scalar(w1[:, :, :, :], w1[:, :, :, :], gam[:, 0:1], None, ALU.mult))
                for q in range(2):
                    hf = slice(q * V, (q + 1) * V)
                    step(nc.vector.tensor_scalar(wrg[hf, q, :], wr[hf, :], gam[hf, 0:1], None, ALU.mult))
                dve.sem_inc(sem("set"), 1)
                dve.sem_inc(sem("acc_free"), 2)
                dve.sem_inc(sem("term"), 2)
                for u in range(2):
                    dve.sem_inc(sem(f"stored{u}"), 16)
                per = 2 * TB + 1 + 2
                perg = 12

                def norm(i, u):
                    k = (2 * i + u) * per
                    dve.wait_ge(sem(f"hin{u}"), 16 * i + 16)
                    n = norm_stats(nc, dve, sem("ln"), k, hin[u], stat[u], mv[u], TB)
                    nc.vector.tensor_scalar(rstd[u][:, 0, :], mv[u][:, :, 1], EPS, None, ALU.add) \
                        .then_inc(sem("var"), 1)
                    link = Chain(dve, sem("ln"), k + n)
                    link(nc.vector.tensor_tensor(xn[u][:, :, :], hin[u][:, :, :],
                                                 mv[u][:, :, 0:1].broadcast_to([P, TB, V]), ALU.subtract))
                    dve.sem_inc(sem("hin_seen"), 1)
                    dve.wait_ge(sem("rstd"), up(i, u))
                    link(nc.vector.tensor_tensor(xn[u][:, :, :], xn[u][:, :, :],
                                                 rstd[u][:, 1, :].unsqueeze(2).broadcast_to([P, TB, V]),
                                                 ALU.mult))
                    dve.sem_inc(sem("xn"), 1)

                def ranks(i, u):
                    dve.wait_ge(sem("lg_ps"), up(i, u))
                    link = Chain(dve, sem("gate"), (2 * i + u) * perg)
                    l, r0, r1 = lg[u], sel[:, 0, :, :], sel[:, 1, :, :]
                    a4 = l[:, :, :].unsqueeze(2).broadcast_to([P, TB, NE, NE])
                    b4 = l[:, :, :].unsqueeze(3).broadcast_to([P, TB, NE, NE])
                    link(nc.vector.tensor_tensor(l[:, :, :], pt[:, 0:TB * NE].rearrange("p (t e) -> p t e", e=NE),
                                                 br[:, :].unsqueeze(1).broadcast_to([P, TB, NE]), ALU.add))
                    link(nc.vector.tensor_tensor(gt[:, :, :, :], a4, b4, ALU.is_gt))
                    link(nc.vector.tensor_tensor(eq[:, :, :, :], a4, b4, ALU.is_equal))
                    link(nc.vector.tensor_tensor(eq[:, :, :, :], eq[:, :, :, :],
                                                 lower[:, :, :].unsqueeze(1).broadcast_to([P, TB, NE, NE]),
                                                 ALU.mult))
                    link(nc.vector.tensor_tensor(gt[:, :, :, :], gt[:, :, :, :], eq[:, :, :, :], ALU.add))
                    link(nc.vector.tensor_reduce(rank[:, :, :], gt[:, :, :, :], AX.X, ALU.add))
                    for s in range(2):
                        nc.vector.tensor_scalar(sel[:, s, :, :], rank[:, :, :], float(s), None, ALU.is_equal) \
                            .then_inc(sem("gate"), 1)
                        link.n += 1
                    dve.wait_ge(sem("gate"), link.start + link.n)
                    link(nc.vector.tensor_tensor(gt[:, 0:2, :, :].rearrange("p s t e -> p s (t e)"),
                                                 sel[:, :, :, :].rearrange("p s t e -> p s (t e)"),
                                                 l[:, :, :].rearrange("p t e -> p (t e)").unsqueeze(1)
                                                 .broadcast_to([P, 2, TB * NE]), ALU.mult))
                    link(nc.vector.tensor_reduce(v12[u][:, 0:2, :], gt[:, 0:2, :, :], AX.X, ALU.add))
                    nc.vector.tensor_tensor(v12[u][:, 2, :], v12[u][:, 0, :], v12[u][:, 1, :], ALU.subtract) \
                        .then_inc(sem("dv"), 1)
                    return link, r0, r1

                def weights(i, u, link, r0, r1):
                    dve.wait_ge(sem("th"), up(i, u))
                    for s in range(2):
                        nc.vector.tensor_scalar(v12[u][:, s, :], v12[u][:, 3, :], 0.5 - s, 0.5, ALU.mult, ALU.add) \
                            .then_inc(sem("v12"), 1)
                    dve.wait_ge(sem("v12"), 2 * up(i, u))
                    link(nc.vector.tensor_tensor(sel[:, :, :, :].rearrange("p s t e -> p (s t) e"),
                                                 sel[:, :, :, :].rearrange("p s t e -> p (s t) e"),
                                                 v12[u][:, 0:2, :].rearrange("p s t -> p (s t)").unsqueeze(2)
                                                 .broadcast_to([P, 2 * TB, NE]), ALU.mult))
                    link(nc.vector.tensor_tensor(gate[u][:, :, :], r0, r1, ALU.add))
                    assert link.n == perg, link.n
                    dve.sem_inc(sem("gated"), 1)

                def experts(i, u, following):
                    for e in range(NE):
                        dve.wait_ge(sem("y_ps"), ex(i, u, e))
                        dve.wait_ge(sem("acc"), ex(i, u, e))
                        nc.vector.tensor_tensor(term[e % 2][:, :, :],
                                                ps[4 + e % 2][:, :].rearrange("p (t d) -> p t d", d=V),
                                                gate[u][:, :, e:e + 1].broadcast_to([P, TB, V]), ALU.mult) \
                            .then_inc(sem("term"), 1)
                        if e == 1 and following:
                            norm(*following)
                        if e == 5 and following:
                            ranked = ranks(*following)
                        if e == 6 and following:
                            weights(*following, *ranked)
                    dve.wait_ge(sem("b2_ps"), up(i, u))
                    dve.wait_ge(sem("acc"), NE * up(i, u) + 2)
                    dve.wait_ge(sem(f"stored{u}"), 16 * i + 16)
                    nc.vector.tensor_tensor(hout[u][:, :, :].rearrange("p t e -> p (t e)"), pm[:, :],
                                            acc[u][:, :, :].rearrange("p t e -> p (t e)"), ALU.add) \
                        .then_inc(sem("hout"), 1)
                    dve.wait_ge(sem("hout"), up(i, u))
                    dve.sem_inc(sem("acc_free"), 1)

                norm(0, 0)
                weights(0, 0, *ranks(0, 0))
                in_turns(dve, NIT, experts)

            @block.scalar
            def _(act):
                def turned(i, u):
                    act.wait_ge(sem("xT_ps"), up(i, u))
                    nc.scalar.copy(xT[u][:, :], pt[:, :]).then_inc(sem("xT"), 1)

                def tanh(i, u):
                    act.wait_ge(sem("dv"), up(i, u))
                    nc.scalar.activation(v12[u][:, 3, :], v12[u][:, 2, :], ACT.Tanh, scale=0.5) \
                        .then_inc(sem("th"), 1)

                def experts(i, u, following):
                    for e in range(NE):
                        act.wait_ge(sem("h_ps"), ex(i, u, e))
                        for q in range(2):
                            nc.scalar.activation(act1[e % 2][:, q, :], ps[2 * (e % 2) + q][:, :], ACT.Gelu,
                                                 bias=b1[:, e:e + 1]).then_inc(sem("act1"), 1)
                        if e == 3 and following:
                            turned(*following)
                        if e == 4:
                            act.wait_ge(sem("gT_ps"), up(i, u))
                            nc.scalar.copy(gT[u][:, :], pm[0:TB * NE, 0:P]).then_inc(sem("gT"), 1)
                        if e == 7 and following:
                            tanh(*following)

                turned(0, 0)
                tanh(0, 0)
                in_turns(act, NIT, experts)

            @block.tensor
            def _(pe):
                pe.wait_ge(sem("loaded"), NL[0])
                nc.tensor.transpose(ps[0][:, 0:NE], b1r[:, :], K.ident[0:NE, 0:NE])
                for e in range(NE):
                    nc.tensor.matmul(ps[1][:, e:e + 1], w1[0:V, 0, e, :], bet[:, 0:1], start=True, stop=True)
                nc.tensor.matmul(ps[2][:, 0:NE], bet[:, 0:1].broadcast_to([V, P]), wr[0:V, :],
                                 start=True, stop=True).then_inc(sem("setp"), 1)
                pe.wait_ge(sem("set"), 1)

                def first(i, u, e):
                    for q in range(2):
                        last = nc.tensor.matmul(ps[2 * (e % 2) + q][:, :], w1[:, q, e, :], xT[u][:, :],
                                                start=True, stop=True)
                    last.then_inc(sem("h_ps"), 1)

                def turn(i, u):
                    pe.wait_ge(sem("xn"), up(i, u))
                    for s in range(TB // 2):
                        last = nc.tensor.transpose(pt[:, s * P:(s + 1) * P],
                                                   xn[u][:, 2 * s:2 * s + 2, :].rearrange("p q e -> p (q e)"),
                                                   K.ident[:, :])
                    last.then_inc(sem("xT_ps"), 1)

                def logits(i, u):
                    pe.wait_ge(sem("xT"), up(i, u))
                    for s in range(TB // 2):
                        last = nc.tensor.matmul(pt[:, 2 * s * NE:2 * (s + 1) * NE], xT[u][:, s * P:(s + 1) * P],
                                                wrg[:, :, :].rearrange("p q e -> p (q e)"), start=True, stop=True)
                    last.then_inc(sem("lg_ps"), 1)

                def experts(i, u, following):
                    for e in range(NE):
                        if e + 1 < NE:
                            first(i, u, e + 1)
                        elif following:
                            first(*following, 0)
                        if e == 3:
                            pe.wait_ge(sem("gated"), up(i, u))
                            wait_alone(pe, sem("acc_free"), up(i, u) + 1, sem("pe_passed"))
                            nc.tensor.transpose(pm[0:TB * NE, 0:P], gate[u][:, :, :].rearrange("p t e -> p (t e)"),
                                                K.ident[:, :]).then_inc(sem("gT_ps"), 1)
                            if following:
                                turn(*following)
                        if e == 4 and following:
                            logits(*following)
                        if e == 7:
                            pe.wait_ge(sem("gT"), up(i, u))
                            nc.tensor.matmul(pm[:, :], gT[u][:, :], b2bd[:, :, :].rearrange("p t e -> p (t e)"),
                                             start=True, stop=True).then_inc(sem("b2_ps"), 1)
                        pe.wait_ge(sem("act1"), 2 * ex(i, u, e))
                        pe.wait_ge(sem("term"), ex(i, u, e))
                        for t in range(TB):
                            s, q = t // 2, t % 2
                            last = nc.tensor.matmul(ps[4 + e % 2][:, t * V:(t + 1) * V],
                                                    act1[e % 2][:, q, s * P:(s + 1) * P], w2[:, e, :],
                                                    start=True, stop=True)
                        last.then_inc(sem("y_ps"), 1)

                turn(0, 0)
                logits(0, 0)
                first(0, 0, 0)
                in_turns(pe, NIT, experts)


def build(nc, a, out):
    with ExitStack() as ctx:
        K = Consts()
        K.ident = ctx.enter_context(nc.sbuf_tensor("ident", [P, P], F32))
        K.onesD = ctx.enter_context(nc.sbuf_tensor("onesD", [P, P], F32))
        K.eps = ctx.enter_context(nc.sbuf_tensor("eps", [P, 1], F32))
        K.mhalf = ctx.enter_context(nc.sbuf_tensor("mhalf", [P, 1], F32))
        made = ctx.enter_context(nc.semaphore("consts"))
        with nc.Block() as block:
            @block.gpsimd
            def _(pool):
                nc.gpsimd.memset(K.ident[:, :], 0.0).then_inc(made, 1)
                pool.wait_ge(made, 1)
                nc.gpsimd.affine_select(out=K.ident[:, :], in_=K.ident[:, :], compare_op=ALU.not_equal, fill=1.0,
                                        base=0, pattern=[[-1, P]], channel_multiplier=1).then_inc(made, 1)

            @block.vector
            def _(dve):
                nc.vector.memset(K.onesD[:, :], 1.0 / D)
                nc.vector.memset(K.mhalf[:, :], -0.5)
                nc.vector.memset(K.eps[:, :], EPS)
        ext = nc.dram_tensor("ext_table", (HEADS, 2 * P - 1), F32, kind="Internal").ap()
        h0 = nc.dram_tensor("h_tower", (NTOK, V), F32, kind="Internal").ap()
        h1 = nc.dram_tensor("h_attn0", (NTOK, V), F32, kind="Internal").ap()
        h2 = nc.dram_tensor("h_ffn0", (NTOK, V), F32, kind="Internal").ap()
        h3 = nc.dram_tensor("h_attn1", (NTOK, V), F32, kind="Internal").ap()

        def sb(n, shape):
            return ctx.enter_context(nc.sbuf_tensor(n, shape, F32))
        F = Consts()
        F.w1, F.w2, F.wo = sb("f0_w1", [P, 2, NE, V]), sb("f0_w2", [P, NPAIR, P]), sb("f0_wo", [P, NPAIR, V])
        F.s, F.t1, F.t2, F.nt2 = sb("f0_s", [P, 2, NPAIR]), sb("f0_t1", [P, NPAIR]), sb("f0_t2", [P, NPAIR]), \
            sb("f0_nt2", [P, NPAIR])
        F.feat = sb("f0_feat", [P, 2, V])
        F.gate, F.corr = sb("f0_gate", [P, NPAIR, 2, P]), sb("f0_corr", [P, 2, V])
        A0, A1 = attention_weights(nc, a, K, ext, ctx)
        chunk_tower(nc, a, h0, K)
        attention(nc, "a0", K, A0, h0, h1, False, F.feat)
        ffn0_gate(nc, a, K, F)
        ffn0(nc, K, F, h1, h2)
        attention(nc, "a1", K, A1, h2, h3, True, None)
        ffn1(nc, a, K, h3, out.rearrange("s l e -> (s l) e"))


def kernel(**inputs):
    import numpy as np
    import concourse.bacc as bacc
    from concourse.bass_utils import run_bass_kernel_spmd as run

    nc = bacc.Bacc("TRN2", target_bir_lowering=False, num_devices=1)
    arrays, args = {}, {}
    for name, x in inputs.items():
        x = np.ascontiguousarray(x)
        arrays["in_" + name] = x
        args[name] = nc.dram_tensor("in_" + name, x.shape, mybir.dt.from_np(x.dtype), kind="ExternalInput").ap()
    out = nc.dram_tensor("h_out", (SEQ, L, V), F32, kind="ExternalOutput").ap()
    build(nc, args, out)
    r = run(nc, [arrays], core_ids=[0])
    return r.results[0]["h_out"]
```
